# Optimizing a Trainium2 kernel written in Bass

```python
import numpy as np
import jax
import jax.numpy as jnp

def _softmax(x, axis=-1):
    return jax.nn.softmax(x, axis=axis)

def _gelu(x):
    return jax.nn.gelu(x, approximate=True)

def _silu(x):
    return jax.nn.silu(x)

def _sigmoid(x):
    return jax.nn.sigmoid(x)

def _layernorm(x, axis=-1, eps=1e-05):
    m = jnp.mean(x, axis=axis, keepdims=True)
    v = jnp.var(x, axis=axis, keepdims=True)
    return (x - m) / jnp.sqrt(v + eps)

def _scatter_add(tgt, idx, src, axis=0):
    return tgt.at[idx].add(src)

def _segment_sum(src, seg, n):
    return jax.ops.segment_sum(src, seg, n)
kernel_name = 'mk_prb_d1_jaxref_r4_622d3a'

def setup_inputs(seed: int=0):
    np.random.seed(seed)
    _w = jnp.asarray

    def _L0_attn_setup():
        import jax, jax.numpy as jnp
        import numpy as np
        N_HEAD = 16
        N_KV = 4
        N_EMBD = 512
        HEAD_DIM = N_EMBD // N_HEAD
        GROUP = N_HEAD // N_KV
        key = jax.random.key(seed)
        ks = jax.random.split(key, 5)
        B, S = (2, 512)
        scale = 0.02
        return {'x': jax.random.normal(ks[0], (B, S, N_EMBD), dtype=jnp.float32), 'Wq': jax.random.normal(ks[1], (N_EMBD, N_EMBD), dtype=jnp.float32) * scale, 'Wk': jax.random.normal(ks[2], (N_EMBD, N_EMBD // GROUP), dtype=jnp.float32) * scale, 'Wv': jax.random.normal(ks[3], (N_EMBD, N_EMBD // GROUP), dtype=jnp.float32) * scale, 'Wo': jax.random.normal(ks[4], (N_EMBD, N_EMBD), dtype=jnp.float32) * scale}
    _L0_attn_in = _L0_attn_setup()

    def _L0_ffn_setup():
        import jax, jax.numpy as jnp
        import numpy as np
        B, S, H = (1, 256, 512)
        I = 352
        E = 32
        K = 6
        G = 8
        TG = 3
        NSH = 2
        SCALE = 16.0
        C = 96

        def _moe_forward(x3, gate_w, w_gate_up, w_down, ws_gate_up, ws_down):
            b, s, h = x3.shape
            x = x3.reshape(-1, h)
            T = x.shape[0]
            logits = x @ gate_w.T
            grouped = logits.reshape(T, G, E // G)
            group_scores = jnp.max(grouped, axis=-1)
            _, group_idx = jax.lax.top_k(group_scores, TG)
            group_keep = jnp.zeros((T, G), bool).at[jnp.arange(T)[:, None], group_idx].set(True)
            masked = jnp.where(group_keep[..., None], grouped, 0.0)
            scores = masked.reshape(T, E)
            probs = jax.nn.softmax(scores.astype(jnp.float32), axis=-1)
            topk_w, topk_idx = jax.lax.top_k(probs, K)
            topk_w = topk_w * SCALE
            flat_e = topk_idx.reshape(-1)
            tok_idx = jnp.repeat(jnp.arange(T), K)
            oh = jax.nn.one_hot(flat_e, E, dtype=jnp.int32)
            pos = jnp.take_along_axis(jnp.cumsum(oh, axis=0) - 1, flat_e[:, None], axis=1)[:, 0]
            valid = pos < C
            slot = jnp.where(valid, flat_e * C + pos, E * C)
            buf = jnp.zeros((E * C + 1, h), x.dtype).at[slot].set(x[tok_idx])
            xb = buf[:E * C].reshape(E, C, h)
            gu = jnp.einsum('ech,ehf->ecf', xb, w_gate_up)
            g, u = jnp.split(gu, 2, axis=-1)
            act = jax.nn.silu(g) * u
            yb = jnp.einsum('eci,eih->ech', act, w_down)
            yflat = jnp.concatenate([yb.reshape(E * C, h), jnp.zeros((1, h), yb.dtype)], axis=0)
            y_pairs = yflat[slot].reshape(T, K, h)
            out = jnp.einsum('tk,tkh->th', topk_w.astype(x.dtype), y_pairs)
            gu_s = x @ ws_gate_up
            gs, us = jnp.split(gu_s, 2, axis=-1)
            out = out + jax.nn.silu(gs) * us @ ws_down
            return out.reshape(b, s, h)
        key = jax.random.key(seed)
        ks = jax.random.split(key, 6)
        s = 0.02
        return {'hidden_states': jax.random.normal(ks[0], (B, S, H), jnp.float32), 'gate_w': jax.random.normal(ks[1], (E, H), jnp.float32) * s, 'w_gate_up': jax.random.normal(ks[2], (E, H, 2 * I), jnp.float32) * s, 'w_down': jax.random.normal(ks[3], (E, I, H), jnp.float32) * s, 'ws_gate_up': jax.random.normal(ks[4], (H, 2 * I * NSH), jnp.float32) * s, 'ws_down': jax.random.normal(ks[5], (I * NSH, H), jnp.float32) * s}
    _L0_ffn_in = _L0_ffn_setup()
    _d = {'L0_attn_x': _L0_attn_in['x'], 'L0_attn_Wq': _L0_attn_in['Wq'], 'L0_attn_Wk': _L0_attn_in['Wk'], 'L0_attn_Wv': _L0_attn_in['Wv'], 'L0_attn_Wo': _L0_attn_in['Wo'], 'L0_ffn_gate_w': _L0_ffn_in['gate_w'], 'L0_ffn_w_gate_up': _L0_ffn_in['w_gate_up'], 'L0_ffn_w_down': _L0_ffn_in['w_down'], 'L0_ffn_ws_gate_up': _L0_ffn_in['ws_gate_up'], 'L0_ffn_ws_down': _L0_ffn_in['ws_down']}
    _x0 = _d['L0_attn_x']
    _d['L0_attn_x'] = jax.random.normal(jax.random.fold_in(jax.random.key(seed), 1), (4, 2048, 512), dtype=_x0.dtype)
    del _x0
    return _d

def reference(L0_attn_x, L0_attn_Wq, L0_attn_Wk, L0_attn_Wv, L0_attn_Wo, L0_ffn_gate_w, L0_ffn_w_gate_up, L0_ffn_w_down, L0_ffn_ws_gate_up, L0_ffn_ws_down):

    def _L0_attn_ref(x, Wq, Wk, Wv, Wo):
        import jax, jax.numpy as jnp
        import numpy as np
        N_HEAD = 16
        N_KV = 4
        N_EMBD = 512
        HEAD_DIM = N_EMBD // N_HEAD
        GROUP = N_HEAD // N_KV
        B, S, _ = x.shape
        scale = HEAD_DIM ** (-0.5)
        q = (x @ Wq).reshape(B, S, N_KV, GROUP, HEAD_DIM)
        k = (x @ Wk).reshape(B, S, N_KV, HEAD_DIM)
        v = (x @ Wv).reshape(B, S, N_KV, HEAD_DIM)
        scores = jnp.einsum('bqkgd,bskd->bkgqs', q, k) * scale
        causal = jnp.triu(jnp.ones((S, S), dtype=bool), k=1)
        scores = jnp.where(causal, jnp.finfo(scores.dtype).min, scores)
        attn = jax.nn.softmax(scores, axis=-1)
        out = jnp.einsum('bkgqs,bskd->bqkgd', attn, v)
        out = out.reshape(B, S, N_EMBD)
        return out @ Wo

    def _L0_ffn_ref(hidden_states, gate_w, w_gate_up, w_down, ws_gate_up, ws_down):
        import jax, jax.numpy as jnp
        import numpy as np
        B, S, H = (1, 256, 512)
        I = 352
        E = 32
        K = 6
        G = 8
        TG = 3
        NSH = 2
        SCALE = 16.0
        C = 96

        def _moe_forward(x3, gate_w, w_gate_up, w_down, ws_gate_up, ws_down):
            b, s, h = x3.shape
            x = x3.reshape(-1, h)
            T = x.shape[0]
            logits = x @ gate_w.T
            grouped = logits.reshape(T, G, E // G)
            group_scores = jnp.max(grouped, axis=-1)
            _, group_idx = jax.lax.top_k(group_scores, TG)
            group_keep = jnp.zeros((T, G), bool).at[jnp.arange(T)[:, None], group_idx].set(True)
            masked = jnp.where(group_keep[..., None], grouped, 0.0)
            scores = masked.reshape(T, E)
            probs = jax.nn.softmax(scores.astype(jnp.float32), axis=-1)
            topk_w, topk_idx = jax.lax.top_k(probs, K)
            topk_w = topk_w * SCALE
            flat_e = topk_idx.reshape(-1)
            tok_idx = jnp.repeat(jnp.arange(T), K)
            oh = jax.nn.one_hot(flat_e, E, dtype=jnp.int32)
            pos = jnp.take_along_axis(jnp.cumsum(oh, axis=0) - 1, flat_e[:, None], axis=1)[:, 0]
            valid = pos < C
            slot = jnp.where(valid, flat_e * C + pos, E * C)
            buf = jnp.zeros((E * C + 1, h), x.dtype).at[slot].set(x[tok_idx])
            xb = buf[:E * C].reshape(E, C, h)
            gu = jnp.einsum('ech,ehf->ecf', xb, w_gate_up)
            g, u = jnp.split(gu, 2, axis=-1)
            act = jax.nn.silu(g) * u
            yb = jnp.einsum('eci,eih->ech', act, w_down)
            yflat = jnp.concatenate([yb.reshape(E * C, h), jnp.zeros((1, h), yb.dtype)], axis=0)
            y_pairs = yflat[slot].reshape(T, K, h)
            out = jnp.einsum('tk,tkh->th', topk_w.astype(x.dtype), y_pairs)
            gu_s = x @ ws_gate_up
            gs, us = jnp.split(gu_s, 2, axis=-1)
            out = out + jax.nn.silu(gs) * us @ ws_down
            return out.reshape(b, s, h)
        return _moe_forward(hidden_states, gate_w, w_gate_up, w_down, ws_gate_up, ws_down)
    x = L0_attn_x
    xn = _layernorm(x, axis=-1)
    x = x + _L0_attn_ref(xn, L0_attn_Wq, L0_attn_Wk, L0_attn_Wv, L0_attn_Wo) + _L0_ffn_ref(xn, L0_ffn_gate_w, L0_ffn_w_gate_up, L0_ffn_w_down, L0_ffn_ws_gate_up, L0_ffn_ws_down)
    return x

_drawn_inputs = setup_inputs


def setup_inputs(seed=0):
    import zlib

    import numpy as np

    out = dict(_drawn_inputs(seed))
    spreads = {}
    factors = {'L0_attn_Wq': 8.0,
     'L0_attn_Wk': 8.0,
     'L0_attn_Wv': 4.237,
     'L0_attn_Wo': 4.354,
     'L0_ffn_gate_w': 5.536,
     'L0_ffn_w_gate_up': 4.155,
     'L0_ffn_w_down': 4.193,
     'L0_ffn_ws_gate_up': 3.367,
     'L0_ffn_ws_down': 3.372}
    for name, (base, spread) in spreads.items():
        noise = np.random.default_rng([zlib.crc32(name.encode()), seed]).standard_normal(out[name].shape)
        drawn = base * np.exp(spread * noise) if base else spread * noise
        out[name] = jnp.asarray(drawn.astype(out[name].dtype))
    for name, factor in factors.items():
        out[name] = (out[name] * factor).astype(out[name].dtype)
    return out
```

```python
from contextlib import ExitStack

import concourse.bass as bass
from concourse import mybir

ALU = mybir.AluOpType
ACT = mybir.ActivationFunctionType
AX = mybir.AxisListType
F32 = mybir.dt.float32
F32R = mybir.dt.float32r
BF16 = mybir.dt.bfloat16
U32 = mybir.dt.uint32
ds = bass.ds

P = 128
B, S, D = 4, 2048, 512
T = B * S
NH, NKV, HD = 16, 4, 32
GROUP = NH // NKV
KC = D // P
CH = 512
NT = CH // P
NC = T // CH
JC = S // CH
SCALE = HD ** -0.5
EPS = 1e-5

E, TOPK, NG, TG, CAP, I = 32, 6, 8, 3, 96, 352
GE = E // NG
ROUTE_SCALE = 16.0
ISH = 2 * I
FM = (ISH + P - 1) // P
FT = ISH - (FM - 1) * P
NOSLOT = 100000.0
IC = (I + P - 1) // P
IT = I - (IC - 1) * P
NKT = S // P
BG = B * NKV
NEG = -1.0e30

C_Q, C_K, C_V, C_G = 0, D, D + P, D + 2 * P
C_GU = C_G + E
WCOL = C_GU + 2 * ISH


def stage_a(nc, t, dbg=None):
    ctx = ExitStack()
    with ctx:
        def sb(name, shape, dt=F32):
            return ctx.enter_context(nc.sbuf_tensor(name, shape, dt))

        def ps(name, shape):
            return ctx.enter_context(nc.psum_tensor(name, shape, F32))

        def sem(name):
            return ctx.enter_context(nc.semaphore(name))

        w_hi = sb("w_hi", [P, KC, WCOL], F32R)
        w_lo = sb("w_lo", [P, KC, WCOL], F32R)
        d_hi = sb("d_hi", [P, FM, D], F32R)
        d_lo = sb("d_lo", [P, FM, D], F32R)
        ident = sb("ident", [P, P])
        uppf = sb("uppf", [P, P])
        before = sb("before", [P, P], BF16)
        ones = sb("ones", [P, P], BF16)
        cst = sb("cst", [P, 2 * E + NG * NG + NT])
        x_sb = sb("x_sb", [P, NT, D])
        xn = sb("xn", [P, NT, D])
        x_hi = sb("x_hi", [P, KC, CH], F32R)
        x_lo = sb("x_lo", [P, KC, CH], F32R)
        qk_hi = sb("qk_hi", [P, NKV + 1, CH], F32R)
        qk_lo = sb("qk_lo", [P, NKV + 1, CH], F32R)
        v_f = sb("v_f", [P, CH])
        v_t = sb("v_t", [P, NT, P])
        l_f = sb("l_f", [E, CH])
        sil = sb("sil", [P, CH])
        h_sb = sb("h_sb", [P, CH])
        up_t = sb("up_t", [FT, CH])
        h_hi = sb("h_hi", [P, FM, CH], F32R)
        h_lo = sb("h_lo", [P, FM, CH], F32R)
        y_sb = sb("y_sb", [P, NT, D])
        stats = sb("stats", [P, NT, 6])
        mv = sb("mv", [P, NT, 2])
        rstd = sb("rstd", [P, NT])
        var = sb("var", [P, NT])
        dev = sb("dev", [P, NT])
        nwt = sb("nwt", [P, NT])
        lg = sb("lg", [P, NT, E])
        gm = sb("gm", [P, NT, NG])
        gt = sb("gt", [P, NT, NG, NG])
        eq = sb("eq", [P, NT, NG, NG])
        rank = sb("rank", [P, NT, NG])
        keep = sb("keep", [P, NT, NG])
        sc = sb("sc", [P, NT, E])
        rmax = sb("rmax", [P, NT])
        shf = sb("shf", [P, NT, E])
        pe_ = sb("pexp", [P, NT, E])
        rs = sb("rs", [P, NT])
        rr = sb("rr", [P, NT])
        prob = sb("prob", [P, NT, E])
        v8 = sb("v8", [P, NT, 8])
        i8 = sb("i8", [P, NT, 8], U32)
        i8f = sb("i8f", [P, NT, 8])
        oh = sb("oh", [P, NT, TOPK, E])
        mask = sb("mask", [P, NT, E], BF16)
        cnt = sb("cnt", [P, E])
        pos = sb("pos", [P, NT, E])
        ovf = sb("ovf", [P, NT, E])
        slt = sb("slt", [P, NT, E])
        ohs = sb("ohs", [P, NT, TOPK, E])
        slk = sb("slk", [P, NT, TOPK])
        slot = sb("slot", [P, NT, TOPK], U32)
        tokf = sb("tokf", [P, NT])
        pay = sb("pay", [P, NT, TOPK, 2], U32)
        empty = sb("empty", [CAP, E, 2], U32)

        ACCB = 3
        acc = ps("acc", [P, ACCB, CH])
        xtp = ps("xtp", [P, 2, CH])
        yp = ps("yp", [P, 2, D])
        smp = ps("smp", [P, CH])

        cst_in = sem("cst_in")
        w_in = [sem("w_in0"), sem("w_in1")]
        w_hi_done = sem("w_hi_done")
        w_lo_done = sem("w_lo_done")
        init_v = sem("init_v")
        x_in = sem("x_in")
        xr_in = sem("xr_in")
        xn_out = sem("xn_out")
        qkv_out = sem("qkv_out")
        y_out = sem("y_out")
        tab_init = sem("tab_init")
        tab_out = sem("tab_out")
        acc_done = sem("acc_done")
        xt_done = sem("xt_done")
        vt_psum = sem("vt_psum")
        lt_psum = sem("lt_psum")
        pos_psum = sem("pos_psum")
        y_done = sem("y_done")
        qhi_done = sem("qhi_done")
        qlo_done = sem("qlo_done")
        v_done = sem("v_done")
        l_done = sem("l_done")
        vt_done = sem("vt_done")
        lt_read = sem("lt_read")
        pos_read = sem("pos_read")
        shf_done = sem("shf_done")
        pexp_done = sem("pexp_done")
        mask_done = sem("mask_done")
        slots_done = sem("slots_done")
        ln_done = sem("ln_done")
        x_free = sem("x_free")
        sil_done = sem("sil_done")
        glu_done = sem("glu_done")
        hhi_done = sem("hhi_done")
        hlo_done = sem("hlo_done")
        xhi_done = sem("xhi_done")
        xlo_done = sem("xlo_done")
        ysb_done = sem("ysb_done")
        upt_done = sem("upt_done")
        var_done = sem("var_done")
        dev_done = sem("dev_done")
        rstd_done = sem("rstd_done")
        dve_pass, pe_pass, sp_pass, pool_pass = (sem(f"{e}_pass_a") for e in ("dve", "pe", "sp", "pool"))
        chain = sem("chain")

        NACC = NKV + 3 + 2 * FM - 1
        FIRST_F = NKV + 3

        pieces = []
        for k in range(KC):
            for a, n in ((0, C_GU // 2), (C_GU // 2, C_GU // 2), (C_GU, ISH), (C_GU + ISH, ISH)):
                pieces.append((t["w_a"][k * P:(k + 1) * P, a:a + n], w_hi[:, k, a:a + n], w_lo[:, k, a:a + n], n))
        for m in range(0, FM, 2):
            pieces.append((t["w_d"].rearrange("(m p) n -> p m n", p=P)[:, m:m + 2, :],
                           d_hi[:, m:m + 2, :], d_lo[:, m:m + 2, :], 2 * D))
        NPC = len(pieces)
        stg = [y_sb[:, 0:2, :].rearrange("p a b -> p (a b)"), y_sb[:, 2:4, :].rearrange("p a b -> p (a b)")]

        def staged(n):
            src, hi, lo, cols = pieces[n]
            v = stg[n % 2][:, 0:cols]
            return v if len(hi.shape) == 2 else v.rearrange("p (a b) -> p a b", b=D)

        iota_e = cst[:, 0:E]
        slot_e = cst[:, E:2 * E]
        tri = cst[:, 2 * E:2 * E + NG * NG].rearrange("p (a b) -> p a b", b=NG)
        tok0 = cst[:, 2 * E + NG * NG:]

        x_d = t["x"].rearrange("(c t p) d -> c p t d", p=P, t=NT)
        xn_d = t["xn"][0:T, :].rearrange("(c t p) d -> c p t d", p=P, t=NT)
        base_d = t["base"][0:T, :].rearrange("(c t p) d -> c p t d", p=P, t=NT)
        v_d = t["v"].rearrange("(c t p) d -> c p t d", p=P, t=NT)

        def chunk(ap, c):
            return ap[c] if isinstance(c, int) else ap[ds(c, 1)].rearrange("o p t d -> (o p) t d")

        def columns(ap4, c):
            if isinstance(c, int):
                return ap4[c // JC, :, :, (c % JC) * CH:(c % JC + 1) * CH].rearrange("g p s -> p g s")
            return ap4[ds(c // JC, 1), :, :, ds((c % JC) * CH, CH)].rearrange("o g p s -> (o p) g s")

        block = ctx.enter_context(nc.Block())

        @block.sync
        def _(sp):
            sp.dma_start(ident[:], t["ident"]).then_inc(cst_in, 16)
            sp.dma_start(uppf[:], t["upper"]).then_inc(cst_in, 16)
            sp.dma_start(cst[:], t["cst"]).then_inc(cst_in, 16)
            sp.dma_start(x_sb[:], chunk(x_d, 0)).then_inc(x_in, 16)
            sp.wait_ge(init_v, 9)
            sp.dma_start(t["xn"][T:T + CAP, :], xn[0:CAP, 0, :]).then_inc(tab_init, 16)
            sp.dma_start(t["base"][T:T + CAP, :], xn[0:CAP, 0, :]).then_inc(tab_init, 16)
            for n, (src, hi, lo, cols) in enumerate(pieces):
                if n >= 2:
                    sp.wait_ge(w_lo_done, n - 1)
                sp.dma_start(staged(n), src).then_inc(w_in[n % 2], 16)
            sp.dma_start(t["tab"].rearrange("(e s) w -> s e w", s=CAP), empty[:]).then_inc(tab_init, 16)
            sp.wait_ge(ln_done, NT)
            sp.dma_start(chunk(xn_d, 0), xn[:]).then_inc(xn_out, 16)
            sp.dma_start(x_sb[:], chunk(x_d, 1)).then_inc(x_in, 16)

            def body(c, nxt, nxt2):
                sp.wait_ge(ysb_done, c * NT + 2)
                sp.sem_inc(sp_pass, 1)
                sp.dma_start(y_sb[:], chunk(x_d, c)).then_inc(xr_in, 16)
                sp.wait_ge(qlo_done, c * (NKV + 1) + NKV + 1)
                sp.sem_inc(sp_pass, 1)
                sp.wait_ge(qhi_done, c * (NKV + 1) + NKV + 1)
                sp.sem_inc(sp_pass, 1)
                sp.dma_start(columns(t["q_hi"], c), qk_hi[:, 0:NKV, :].bitcast(F32)).then_inc(qkv_out, 16)
                sp.dma_start(columns(t["q_lo"], c), qk_lo[:, 0:NKV, :].bitcast(F32)).then_inc(qkv_out, 16)
                sp.dma_start(columns(t["k_hi"], c), qk_hi[:, NKV:NKV + 1, :].bitcast(F32)).then_inc(qkv_out, 16)
                sp.dma_start(columns(t["k_lo"], c), qk_lo[:, NKV:NKV + 1, :].bitcast(F32)).then_inc(qkv_out, 16)
                sp.wait_ge(vt_done, c + 1)
                sp.sem_inc(sp_pass, 1)
                sp.dma_start(chunk(v_d, c), v_t[:]).then_inc(qkv_out, 16)
                if nxt:
                    sp.wait_ge(ln_done, c * NT + 2 * NT)
                    sp.sem_inc(sp_pass, 1)
                    sp.dma_start(chunk(xn_d, c + 1), xn[:]).then_inc(xn_out, 16)
                if nxt2:
                    sp.dma_start(x_sb[:], chunk(x_d, c + 2)).then_inc(x_in, 16)
                sp.wait_ge(ysb_done, c * NT + NT + 2)
                sp.sem_inc(sp_pass, 1)
                sp.dma_start(chunk(base_d, c), y_sb[:]).then_inc(y_out, 16)
                sp.wait_ge(y_out, c * 16 + 16)
                sp.sem_inc(sp_pass, 1)

            sp.wait_ge(w_lo_done, NPC)
            with sp.Fori(0, NC - 2) as c:
                body(c, True, True)
            body(NC - 2, True, False)
            body(NC - 1, False, False)
            sp.wait_ge(tab_init, 48)
            sp.wait_ge(xn_out, 16 * NC)
            sp.wait_ge(qkv_out, 80 * NC)
            sp.wait_ge(y_out, 16 * NC)

        @block.gpsimd
        def _(pool):
            pool.wait_ge(tab_init, 48)

            with pool.Fori(0, NC) as c:
                pool.wait_ge(slots_done, c + 1)
                pool.sem_inc(pool_pass, 1)
                for i in range(NT):
                    for k in range(TOPK):
                        nc.gpsimd.indirect_dma_start(
                            t["tab"], bass.IndirectOffsetOnAxis(ap=slot[:, i, k:k + 1], axis=0),
                            pay[:, i, k, :], None, bounds_check=E * CAP - 1, oob_is_err=False,
                        ).then_inc(tab_out, 16)
                pool.wait_ge(tab_out, c * (16 * NT * TOPK) + 16 * NT * TOPK)
                pool.sem_inc(pool_pass, 1)

            pool.wait_ge(tab_out, NC * (16 * NT * TOPK))

        @block.scalar
        def _(act):
            def deviation(c):
                act.wait_ge(var_done, 2 * c + 2)
                nc.scalar.activation(dev[:], var[:], ACT.Sqrt).then_inc(dev_done, 1)

            deviation(0)

            for n in range(NPC):
                act.wait_ge(w_in[n % 2], 16 * (n // 2 + 1))
                nc.scalar.activation(pieces[n][1], staged(n), ACT.Copy).then_inc(w_hi_done, 1)

            def xhi(c):
                for k in range(KC):
                    act.wait_ge(xt_done, c * KC + k + 1)
                    nc.scalar.activation(x_hi[:, k, :], xtp[:, k % 2, :], ACT.Copy).then_inc(xhi_done, 1)

            def body(c, nxt):
                act.wait_ge(qkv_out, c * 80)
                for i in range(NKV + 1):
                    act.wait_ge(acc_done, c * NACC + i + 1)
                    nc.scalar.activation(qk_hi[:, i, :], acc[:, i % ACCB, :], ACT.Copy).then_inc(qhi_done, 1)
                act.wait_ge(acc_done, c * NACC + NKV + 2)
                nc.scalar.activation(v_f[:], acc[:, (NKV + 1) % ACCB, :], ACT.Copy).then_inc(v_done, 1)
                act.wait_ge(acc_done, c * NACC + NKV + 3)
                nc.scalar.activation(l_f[:], acc[0:E, (NKV + 2) % ACCB, :], ACT.Copy).then_inc(l_done, 1)
                act.wait_ge(vt_psum, c + 1)
                nc.scalar.activation(v_t[:].rearrange("p t d -> p (t d)"), smp[:], ACT.Copy).then_inc(vt_done, 1)
                act.wait_ge(shf_done, c + 1)
                nc.scalar.activation(pe_[:], shf[:], ACT.Exp).then_inc(pexp_done, 1)
                if nxt:
                    deviation(c + 1)
                for m in range(FM):
                    last = m == FM - 1
                    rows = FT if last else P
                    i = FIRST_F + 2 * m
                    act.wait_ge(acc_done, c * NACC + i + 1)
                    act.wait_ge(glu_done, c * FM + m + FM)
                    nc.scalar.activation(sil[0:rows, :], acc[0:rows, i % ACCB, :], ACT.Silu).then_inc(sil_done, 1)
                    act.wait_ge(glu_done, c * FM + m + 1 + FM)
                    nc.scalar.activation(h_hi[0:rows, m, :], h_sb[0:rows, :], ACT.Copy).then_inc(hhi_done, 1)
                if nxt:
                    act.wait_ge(acc_done, c * NACC + NACC)
                    xhi(c + 1)

            act.wait_ge(init_v, 1)
            xhi(0)
            with act.Fori(0, NC - 1) as c:
                body(c, True)
            body(NC - 1, False)

        @block.vector
        def _(dve):
            N_CHAIN = 20
            count = [0]

            def link(ins, c):
                count[0] += 1
                ins.then_inc(chain, 1)
                dve.wait_ge(chain, c * N_CHAIN + count[0])

            V = nc.vector
            V.memset(h_hi[:, FM - 1, :].bitcast(F32), 0.0).then_inc(init_v, 1)
            V.memset(h_lo[:, FM - 1, :].bitcast(F32), 0.0).then_inc(init_v, 1)
            V.memset(ones[:], 1.0).then_inc(init_v, 1)
            V.memset(cnt[:], 0.0).then_inc(init_v, 1)
            V.memset(empty[:], 0).then_inc(init_v, 1)
            V.memset(xn[:, 0, :], 0.0).then_inc(init_v, 1)
            dve.sem_inc(glu_done, FM)
            dve.sem_inc(ysb_done, 2)
            dve.wait_ge(cst_in, 48)
            V.tensor_copy(before[:], uppf[:]).then_inc(init_v, 1)
            V.tensor_copy(tokf[:], tok0).then_inc(init_v, 1)
            dve.wait_ge(init_v, 6)
            V.tensor_scalar(empty[:, :, 0], tok0[0:CAP, 0:1].to_broadcast([CAP, E]), float(T), None,
                            ALU.add).then_inc(init_v, 1)
            dve.wait_ge(init_v, 9)

            def ln_stats(c):
                dve.wait_ge(x_in, c * 16 + 16)
                for i in range(NT):
                    V.bn_stats(out=stats[:, i, :], in_=x_sb[:, i, :]).then_inc(x_free, 1)

            def ln_variance(c):
                dve.wait_ge(x_free, c * NT + NT)
                dve.sem_inc(dve_pass, 1)
                for i in range(NT):
                    last = V.bn_aggr(out=mv[:, i, :], in_=stats[:, i, :])
                last.then_inc(var_done, 1)
                dve.wait_ge(var_done, 2 * c + 1)
                V.tensor_scalar(var[:], mv[:, :, 1], EPS, None, ALU.add).then_inc(var_done, 1)

            def ln_inverse(c):
                dve.wait_ge(dev_done, c + 1)
                V.reciprocal(rstd[:], dev[:]).then_inc(rstd_done, 1)
                dve.wait_ge(rstd_done, c * 5 + 1)
                V.tensor_tensor(nwt[:], var[:], rstd[:], ALU.mult).then_inc(rstd_done, 1)
                dve.wait_ge(rstd_done, c * 5 + 2)
                V.tensor_tensor(nwt[:], nwt[:], rstd[:], ALU.mult).then_inc(rstd_done, 1)
                dve.wait_ge(rstd_done, c * 5 + 3)
                V.tensor_scalar(nwt[:], nwt[:], -0.5, 1.5, ALU.mult, ALU.add).then_inc(rstd_done, 1)
                dve.wait_ge(rstd_done, c * 5 + 4)
                V.tensor_tensor(rstd[:], rstd[:], nwt[:], ALU.mult).then_inc(rstd_done, 1)

            def ln_scale(c):
                dve.wait_ge(rstd_done, c * 5 + 5)
                dve.wait_ge(tab_init, 32)
                dve.wait_ge(xn_out, c * 16)
                dve.wait_ge(xt_done, c * KC)
                for i in range(NT):
                    V.tensor_scalar(xn[:, i, :], x_sb[:, i, :], mv[:, i, 0:1], rstd[:, i:i + 1],
                                    ALU.subtract, ALU.mult).then_inc(ln_done, 1)

            def xlo(c):
                for k in range(KC):
                    dve.wait_ge(xhi_done, c * KC + k + 1)
                    V.tensor_tensor(x_lo[:, k, :], xtp[:, k % 2, :], x_hi[:, k, :].bitcast(F32),
                                    ALU.subtract).then_inc(xlo_done, 1)

            ln_stats(0)
            ln_variance(0)
            ln_inverse(0)
            ln_scale(0)
            for n in range(NPC):
                dve.wait_ge(w_hi_done, n + 1)
                V.tensor_tensor(pieces[n][2], staged(n), pieces[n][1].bitcast(F32),
                                ALU.subtract).then_inc(w_lo_done, 1)
            xlo(0)

            def body(c, nxt):
                count[0] = 0
                dve.wait_ge(qkv_out, c * 80)
                for i in range(NKV + 1):
                    dve.wait_ge(qhi_done, c * (NKV + 1) + i + 1)
                    V.tensor_tensor(qk_lo[:, i, :], acc[:, i % ACCB, :], qk_hi[:, i, :].bitcast(F32),
                                    ALU.subtract).then_inc(qlo_done, 1)
                dve.wait_ge(lt_psum, c + 1)
                V.tensor_copy(lg[:].rearrange("p t e -> p (t e)"), smp[:, 0:NT * E]).then_inc(lt_read, 1)
                dve.wait_ge(lt_read, c + 1)
                link(V.tensor_reduce(gm[:].rearrange("p t g -> p (t g)"),
                                     lg[:].rearrange("p t (g e) -> p (t g) e", g=NG), AX.X, ALU.max), c)
                other = gm[:].unsqueeze(2).to_broadcast([P, NT, NG, NG])
                own = gm[:].unsqueeze(3).to_broadcast([P, NT, NG, NG])
                V.tensor_tensor(gt[:], other, own, ALU.is_gt)
                link(V.tensor_tensor(eq[:], other, own, ALU.is_equal), c)
                link(V.tensor_tensor(eq[:], eq[:], tri.unsqueeze(1).to_broadcast([P, NT, NG, NG]), ALU.mult), c)
                link(V.tensor_tensor(gt[:], gt[:], eq[:], ALU.add), c)
                link(V.tensor_reduce(rank[:].rearrange("p t g -> p (t g)"),
                                     gt[:].rearrange("p t a b -> p (t a) b"), AX.X, ALU.add), c)
                link(V.tensor_scalar(keep[:], rank[:], float(TG), None, ALU.is_lt), c)
                link(V.tensor_tensor(sc[:].rearrange("p t (g e) -> p t g e", g=NG),
                                     lg[:].rearrange("p t (g e) -> p t g e", g=NG),
                                     keep[:].unsqueeze(3).to_broadcast([P, NT, NG, GE]), ALU.mult), c)
                link(V.tensor_reduce(rmax[:], sc[:], AX.X, ALU.max), c)
                V.tensor_tensor(shf[:], sc[:], rmax[:].unsqueeze(2).to_broadcast([P, NT, E]),
                                ALU.subtract).then_inc(shf_done, 1)
                if nxt:
                    ln_stats(c + 1)
                    ln_variance(c + 1)
                dve.wait_ge(pexp_done, c + 1)
                link(V.tensor_reduce(rs[:], pe_[:], AX.X, ALU.add), c)
                link(V.reciprocal(rr[:], rs[:]), c)
                link(V.tensor_tensor(prob[:], pe_[:], rr[:].unsqueeze(2).to_broadcast([P, NT, E]), ALU.mult), c)
                dve.sem_inc(dve_pass, 1)
                for i in range(NT):
                    last = V.max(v8[:, i, :], prob[:, i, :])
                link(last, c)
                dve.sem_inc(dve_pass, 1)
                for i in range(NT):
                    last = V.max_index(i8[:, i, :], v8[:, i, :], prob[:, i, :])
                link(last, c)
                link(V.tensor_copy(i8f[:], i8[:]), c)
                link(V.tensor_tensor(oh[:], iota_e.unsqueeze(1).unsqueeze(1).to_broadcast([P, NT, TOPK, E]),
                                     i8f[:, :, 0:TOPK].unsqueeze(3).to_broadcast([P, NT, TOPK, E]),
                                     ALU.is_equal), c)
                with nc.allow_low_precision(reason="sums of zeros and at most one 1 are exact"):
                    V.tensor_reduce(mask[:], oh[:].rearrange("p t k e -> p t e k"), AX.X,
                                    ALU.add).then_inc(mask_done, 1)

                def glu(m):
                    last = m == FM - 1
                    rows = FT if last else P
                    i = FIRST_F + 2 * m
                    if last:
                        dve.wait_ge(acc_done, c * NACC + i + 1)
                        V.tensor_copy(up_t[:], acc[FT:2 * FT, i % ACCB, :]).then_inc(upt_done, 1)
                        dve.wait_ge(upt_done, c + 1)
                        up = up_t[:]
                    else:
                        dve.wait_ge(acc_done, c * NACC + i + 2)
                        up = acc[:, (i + 1) % ACCB, :]
                    dve.wait_ge(sil_done, c * FM + m + 1)
                    dve.wait_ge(hlo_done, c * FM + m)
                    V.tensor_tensor(h_sb[0:rows, :], sil[0:rows, :], up, ALU.mult).then_inc(glu_done, 1)
                    dve.wait_ge(hhi_done, c * FM + m + 1)
                    V.tensor_tensor(h_lo[0:rows, m, :], h_sb[0:rows, :], h_hi[0:rows, m, :].bitcast(F32),
                                    ALU.subtract).then_inc(hlo_done, 1)

                glu(0)
                glu(1)
                glu(2)
                if nxt:
                    ln_inverse(c + 1)
                    ln_scale(c + 1)
                dve.wait_ge(pos_psum, c + 1)
                V.tensor_tensor(pos[:], smp[:, 0:NT * E].rearrange("p (t e) -> p t e", e=E),
                                cnt[:].unsqueeze(1).to_broadcast([P, NT, E]), ALU.add).then_inc(pos_read, 1)
                dve.wait_ge(pos_read, 2 * c + 1)
                V.tensor_tensor(cnt[:], cnt[:], smp[:, NT * E:(NT + 1) * E], ALU.add).then_inc(pos_read, 1)
                V.tensor_scalar(ovf[:], pos[:], float(CAP), NOSLOT, ALU.is_ge, ALU.mult)
                link(V.tensor_tensor(slt[:], pos[:], slot_e.unsqueeze(1).to_broadcast([P, NT, E]), ALU.add), c)
                link(V.tensor_tensor(slt[:], slt[:], ovf[:], ALU.add), c)
                glu(3)
                link(V.tensor_tensor(ohs[:], oh[:], slt[:].unsqueeze(2).to_broadcast([P, NT, TOPK, E]),
                                     ALU.mult), c)
                link(V.tensor_reduce(slk[:], ohs[:], AX.X, ALU.add), c)
                dve.wait_ge(tab_out, c * (16 * NT * TOPK))
                V.tensor_copy(slot[:], slk[:])
                V.tensor_copy(pay[:, :, :, 0], tokf[:].unsqueeze(2).to_broadcast([P, NT, TOPK]))
                link(V.tensor_scalar(pay[:, :, :, 1].bitcast(F32), v8[:, :, 0:TOPK], ROUTE_SCALE, None,
                                     ALU.mult), c)
                V.tensor_scalar(tokf[:], tokf[:], float(CH), None, ALU.add).then_inc(slots_done, 1)
                glu(4)
                glu(5)
                if nxt:
                    xlo(c + 1)
                dve.wait_ge(xr_in, c * 16 + 16)
                for i in range(NT):
                    dve.wait_ge(y_done, c * NT + i + 1)
                    V.tensor_tensor(y_sb[:, i, :], yp[:, i % 2, :], y_sb[:, i, :], ALU.add).then_inc(ysb_done, 1)
                if nxt:
                    assert count[0] == N_CHAIN, count

            with dve.Fori(0, NC - 1) as c:
                body(c, True)
            body(NC - 1, False)

        @block.tensor
        def _(pe):
            M = nc.tensor.matmul

            def transposes(c):
                pe.wait_ge(ln_done, c * NT + NT)
                for k in range(KC):
                    if not isinstance(c, int) or c * KC + k >= 2:
                        pe.wait_ge(xlo_done, c * KC + k - 1)
                    for i in range(NT):
                        last = nc.tensor.transpose(xtp[:, k % 2, i * P:(i + 1) * P],
                                                   xn[:, i, k * P:(k + 1) * P], ident[:])
                    last.then_inc(xt_done, 1)

            def product(c, i, col, width):
                n = 0
                for k in range(KC):
                    for w, x in ((w_hi, x_hi), (w_hi, x_lo), (w_lo, x_hi)):
                        last = M(acc[0:width, i % ACCB, :], w[:, k, col:col + width], x[:, k, :],
                                 start=(n == 0), stop=(n == 3 * KC - 1))
                        n += 1
                last.then_inc(acc_done, 1)

            def released(c, i):
                j = i - ACCB
                if j < 0:
                    pe.wait_ge(glu_done, c * FM + (j + NACC - FIRST_F) // 2 + 1)
                elif j <= NKV:
                    pe.wait_ge(qlo_done, c * (NKV + 1) + j + 1)
                elif j == NKV + 1:
                    pe.wait_ge(v_done, c + 1)
                elif j == NKV + 2:
                    pe.wait_ge(l_done, c + 1)
                else:
                    pe.wait_ge(glu_done, c * FM + (j - FIRST_F) // 2 + 1 + FM)

            def body(c, nxt):
                pe.wait_ge(xlo_done, c * KC + KC)
                cols = [C_Q + g * P for g in range(NKV)] + [C_K, C_V]
                for i, col in enumerate(cols):
                    released(c, i)
                    product(c, i, col, P)
                released(c, NKV + 2)
                product(c, NKV + 2, C_G, E)
                pe.wait_ge(v_done, c + 1)
                pe.wait_ge(pos_read, 2 * c)
                for i in range(NT):
                    last = nc.tensor.transpose(smp[:, i * P:(i + 1) * P], v_f[:, i * P:(i + 1) * P], ident[:])
                last.then_inc(vt_psum, 1)
                pe.wait_ge(l_done, c + 1)
                pe.wait_ge(vt_done, c + 1)
                pe.sem_inc(pe_pass, 1)
                for i in range(NT):
                    last = nc.tensor.transpose(smp[:, i * E:(i + 1) * E], l_f[:, i * P:(i + 1) * P],
                                               ident[0:E, 0:E])
                last.then_inc(lt_psum, 1)
                for n in range(2 * FM - 1):
                    if n == 6:
                        pe.wait_ge(mask_done, c + 1)
                        pe.wait_ge(lt_read, c + 1)
                        for i in range(NT):
                            for j in range(i + 1):
                                M(smp[:, i * E:(i + 1) * E], before[:] if j == i else ones[:], mask[:, j, :],
                                  start=(j == 0), stop=(j == i))
                        for j in range(NT):
                            last = M(smp[:, NT * E:(NT + 1) * E], ones[:], mask[:, j, :],
                                     start=(j == 0), stop=(j == NT - 1))
                        last.then_inc(pos_psum, 1)
                    released(c, FIRST_F + n)
                    product(c, FIRST_F + n, C_GU + n * P, P)
                if nxt:
                    transposes(c + 1)
                pe.wait_ge(hlo_done, c * FM + FM)
                for i in range(NT):
                    pe.wait_ge(ysb_done, c * NT + i + 1)
                    n = 0
                    for m in range(FM):
                        for h, w in ((h_hi, d_hi), (h_lo, d_hi), (h_hi, d_lo)):
                            last = M(yp[:, i % 2, :], h[:, m, i * P:(i + 1) * P], w[:, m, :],
                                     start=(n == 0), stop=(n == 3 * FM - 1))
                            n += 1
                    last.then_inc(y_done, 1)

            pe.wait_ge(cst_in, 48)
            transposes(0)
            pe.wait_ge(w_lo_done, NPC)
            pe.wait_ge(init_v, 9)
            with pe.Fori(0, NC - 1) as c:
                body(c, True)
            body(NC - 1, False)


def stage_m(nc, t):
    ctx = ExitStack()
    with ctx:
        def sb(name, shape, dt=F32):
            return ctx.enter_context(nc.sbuf_tensor(name, shape, dt))

        def ps(name, shape):
            return ctx.enter_context(nc.psum_tensor(name, shape, F32))

        def sem(name):
            return ctx.enter_context(nc.semaphore(name))

        def two(name, shape, dt=F32):
            return [sb(f"{name}{p}", shape, dt) for p in range(2)]

        wgu = two("wgu", [P, KC, 2 * I])
        wdn = two("wdn", [P, IC, D])
        ids = two("ids", [CAP, 2], U32)
        xb = two("xb", [CAP, D])
        xbt = two("xbt", [P, KC, CAP])
        sil = two("silu", [CAP, I])
        hid = two("hid", [CAP, I])
        hidt = two("hidt", [P, IC, CAP])
        ysb = two("ysb", [CAP, D])
        ident = sb("ident_m", [P, P])
        gps = [ps(f"gps{p}", [P, 512]) for p in range(2)]
        ups = [ps(f"ups{p}", [P, 512]) for p in range(2)]
        yps = [ps(f"yps{p}", [P, 512]) for p in range(2)]
        xtps = ps("xtps", [P, 512])
        htps = ps("htps", [P, 512])

        id_in = sem("id_in")
        w_in = [sem("wgu_in0"), sem("wgu_in1")]
        tok_in = [sem("tok_in0"), sem("tok_in1")]
        x_in = sem("xb_in")
        y_out = sem("yadd_out")
        xt_done = sem("xbt_psum")
        xt_read = sem("xbt_done")
        gu_done = sem("gu_done")
        sil_done = sem("esil_done")
        hid_done = sem("hid_done")
        ht_done = sem("ht_psum")
        ht_read = sem("ht_done")
        dn_done = sem("dn_done")
        y_done = sem("ey_done")
        sp_pass, pool_pass = sem("sp_pass_m"), sem("pool_pass_m")

        block = ctx.enter_context(nc.Block())

        def expert(ap, e):
            return ap[e] if isinstance(e, int) else ap[ds(e, 1)].rearrange("o a b -> (o a) b")

        def load(sp, e, p):
            sp.dma_start(ids[p][:], expert(t["tab"].rearrange("(e s) w -> e s w", s=CAP), e)).then_inc(tok_in[p], 16)
            sp.dma_start(wgu[p][:], expert(t["e_gu"], e).rearrange("(k p) n -> p k n", p=P)).then_inc(w_in[p], 16)
            w = expert(t["e_d"], e)
            sp.dma_start(wdn[p][:, 0:IC - 1, :], w[0:(IC - 1) * P, :].rearrange("(k p) n -> p k n", p=P)).then_inc(w_in[p], 16)
            sp.dma_start(wdn[p][0:IT, IC - 1, :], w[(IC - 1) * P:I, :]).then_inc(w_in[p], 16)

        @block.sync
        def _(sp):
            sp.dma_start(ident[:], t["ident"]).then_inc(id_in, 16)
            load(sp, 0, 0)
            load(sp, 1, 1)
            with sp.Fori(0, E // 2 - 1) as i:
                for p in range(2):
                    sp.wait_ge(dn_done, 2 * i + p + 1)
                    sp.sem_inc(sp_pass, 1)
                    sp.wait_ge(y_out, 32 * i + 16 * p + 16)
                    sp.sem_inc(sp_pass, 1)
                    load(sp, 2 * i + p + 2, p)

        @block.gpsimd
        def _(pool):
            def gather(i, p):
                pool.wait_ge(tok_in[p], 16 * i + 16)
                pool.sem_inc(pool_pass, 1)
                pool.wait_ge(xt_done, 2 * i + p)
                pool.sem_inc(pool_pass, 1)
                nc.gpsimd.indirect_dma_start(xb[p][:], None, t["xn"],
                                             bass.IndirectOffsetOnAxis(ap=ids[p][:, 0:1], axis=0),
                                             bounds_check=T + CAP - 1, oob_is_err=True).then_inc(x_in, 16)

            def scatter(i, p):
                pool.wait_ge(y_done, 2 * i + p + 1)
                pool.sem_inc(pool_pass, 1)
                if not (isinstance(i, int) and i == 0 and p == 0):
                    pool.wait_ge(y_out, 32 * i + 16 * p)
                    pool.sem_inc(pool_pass, 1)
                nc.gpsimd.indirect_dma_start(t["base"], bass.IndirectOffsetOnAxis(ap=ids[p][:, 0:1], axis=0),
                                             ysb[p][:], None, bounds_check=T + CAP - 1, oob_is_err=True,
                                             compute_op=ALU.add).then_inc(y_out, 16)

            gather(0, 0)

            def body(i, nxt):
                gather(i, 1)
                scatter(i, 0)
                if nxt:
                    gather(i + 1, 0)
                scatter(i, 1)

            with pool.Fori(0, E // 2 - 1) as i:
                body(i, True)
            body(E // 2 - 1, False)
            pool.wait_ge(y_out, 16 * E)

        @block.scalar
        def _(act):
            def rows(n, p):
                act.wait_ge(xt_done, n + 1)
                nc.scalar.activation(xbt[p][:].rearrange("p k s -> p (k s)"), xtps[:, 0:KC * CAP],
                                     ACT.Copy).then_inc(xt_read, 1)

            rows(0, 0)

            def body(i, nxt):
                for p in range(2):
                    n = 2 * i + p
                    act.wait_ge(gu_done, n + 1)
                    nc.scalar.activation(sil[p][:], gps[p][0:CAP, 0:I], ACT.Silu).then_inc(sil_done, 1)
                    if p == 0 or nxt:
                        rows(n + 1, 1 - p)
                    act.wait_ge(ht_done, n + 1)
                    nc.scalar.activation(hidt[p][:, 0:IC - 1, :].rearrange("p k s -> p (k s)"),
                                         htps[:, 0:(IC - 1) * CAP], ACT.Copy)
                    nc.scalar.activation(hidt[p][0:IT, IC - 1, :], htps[0:IT, (IC - 1) * CAP:IC * CAP],
                                         ACT.Copy).then_inc(ht_read, 1)

            with act.Fori(0, E // 2 - 1) as i:
                body(i, True)
            body(E // 2 - 1, False)

        @block.vector
        def _(dve):
            with dve.Fori(0, E // 2) as i:
                for p in range(2):
                    n = 2 * i + p
                    dve.wait_ge(sil_done, n + 1)
                    nc.vector.tensor_tensor(hid[p][:], sil[p][:], ups[p][0:CAP, 0:I], ALU.mult).then_inc(hid_done, 1)
                    dve.wait_ge(dn_done, n + 1)
                    nc.vector.tensor_scalar(ysb[p][:], yps[p][0:CAP, :], ids[p][:, 1:2].bitcast(F32), None,
                                            ALU.mult).then_inc(y_done, 1)

        @block.tensor
        def _(pe):
            M, TR = nc.tensor.matmul, nc.tensor.transpose

            def rows(n, p):
                pe.wait_ge(x_in, 16 * n + 16)
                for k in range(KC):
                    last = TR(xtps[:, k * CAP:(k + 1) * CAP], xb[p][:, k * P:(k + 1) * P], ident[0:CAP, 0:CAP])
                last.then_inc(xt_done, 1)

            def body(i, nxt):
                for p in range(2):
                    n = 2 * i + p
                    pe.wait_ge(w_in[p], 48 * i + 48)
                    pe.wait_ge(xt_read, n + 1)
                    if not (isinstance(i, int) and i == 0):
                        pe.wait_ge(hid_done, 2 * i + p - 1 if p else 2 * i)
                    for a, bank in ((0, gps[p]), (I, ups[p])):
                        for k in range(KC):
                            last = M(bank[0:CAP, 0:I], xbt[p][:, k, :], wgu[p][:, k, a:a + I],
                                     start=(k == 0), stop=(k == KC - 1))
                    last.then_inc(gu_done, 1)
                    if p == 0 or nxt:
                        rows(n + 1, 1 - p)
                    pe.wait_ge(hid_done, n + 1)
                    for k in range(IC):
                        w = P if k < IC - 1 else IT
                        last = TR(htps[0:w, k * CAP:(k + 1) * CAP], hid[p][:, k * P:k * P + w],
                                  ident[0:CAP, 0:CAP])
                    last.then_inc(ht_done, 1)
                    pe.wait_ge(ht_read, n + 1)
                    for k in range(IC):
                        w = P if k < IC - 1 else IT
                        last = M(yps[p][0:CAP, :], hidt[p][0:w, k, :], wdn[p][0:w, k, :],
                                 start=(k == 0), stop=(k == IC - 1))
                    last.then_inc(dn_done, 1)

            pe.wait_ge(id_in, 16)
            rows(0, 0)
            with pe.Fori(0, E // 2 - 1) as i:
                body(i, True)
            body(E // 2 - 1, False)


def stage_b(nc, t):
    ctx = ExitStack()
    with ctx:
        def sb(name, shape, dt=F32):
            return ctx.enter_context(nc.sbuf_tensor(name, shape, dt))

        def ps(name, shape):
            return ctx.enter_context(nc.psum_tensor(name, shape, F32))

        def sem(name):
            return ctx.enter_context(nc.semaphore(name))

        def two(name, shape, dt=F32):
            return [sb(f"{name}{p}", shape, dt) for p in range(2)]

        RP = 16
        R3 = 3 * HD
        qst = two("qst", [P, GROUP, S], F32R)
        kst = two("kst", [P, S], F32R)
        vst = two("vst", [P, NKT, HD])
        prb = sb("prb", [P, RP, 2, CH])
        suma = [two(f"suma{g}", [P, 2, CH]) for g in range(2)]
        sumb = [two(f"sumb{g}", [P, 2, CH]) for g in range(2)]
        mx = sb("mx", [P, GROUP * NKT, JC])
        neg = sb("neg", [P, GROUP * NKT])
        negt = sb("negt", [GROUP * NKT, P], F32R)
        rden = sb("rden", [P, CH])
        att = two("att", [P, CH])
        ident = sb("ident_b", [P, P])
        lowf = sb("lowf", [P, P])
        identb = sb("identb", [P, P], BF16)
        cmask = sb("cmask", [P, P], BF16)
        ones = sb("ones_b", [P, HD])
        sps = ps("sps", [P, 2, 2, CH])
        mps = ps("mps", [P, 2, CH])
        ops = ps("ops", [P, CH])
        dps = ps("dps", [P, CH])

        cst_in = sem("cst_b")
        init_v = sem("init_b")
        qk_in = [sem("qk_in0"), sem("qk_in1")]
        v_in = [sem("v_in0"), sem("v_in1")]
        c_in = sem("c_in")
        att_out = sem("att_out")
        s_done = sem("s_done")
        exp_done = sem("exp_done")
        sel_done = sem("sel_done")
        pv_done = sem("pv_done")
        add_done = sem("add_done")
        sumb_done = sem("sumb_done")
        suma_done = sem("suma_done")
        ones_done = sem("ones_done")
        m_done = sem("m_done")
        mred_done = sem("mred_done")
        neg_done = sem("neg_done")
        c_done = sem("c_done")
        rden_done = sem("rden_done")
        att_done = sem("att_done")
        pe_pass, sp_pass, pool_pass = (sem(f"{e}_pass_b") for e in ("pe", "sp", "pool"))

        steps = [(j, kt, kt - JC * j) for j in range(JC) for kt in range(JC * (j + 1))]
        NK = len(steps)
        NU = 2 * NK
        steps = [(j, kt, r if r >= 0 else -1) for j, kt, r in steps]
        full = [n for n, (j, kt, r) in enumerate(steps) if r < 0 and kt % 4 == 0]
        NGR = len(full)
        diag = [n for n, (j, kt, r) in enumerate(steps) if r >= 0]
        lasts = [n for n, (j, kt, r) in enumerate(steps) if r == 3]

        pieces = []
        for h in range(GROUP):
            for qt in range(NKT):
                n = (qt + 1) * P
                for j in range((n + CH - 1) // CH):
                    k0, w = j * CH, min(CH, n - j * CH)
                    if w == P and j:
                        k0, w = k0 - P, 2 * P
                    d = n - P - k0
                    pieces.append((h, qt, j, k0, max(w, 2 * P), w, d if n - k0 == w else None))
        NM = len(pieces)
        MI = NM + 1
        M0, M1 = 4, 36

        def quota(k):
            if not M0 <= k < M1:
                return range(0)
            n = -(-NM // (M1 - M0))
            return range((k - M0) * n, min(NM, (k - M0 + 1) * n))

        MFIN = M1

        block = ctx.enter_context(nc.Block())

        @block.sync
        def _(sp):
            def load_qk(i, p):
                b = i // 2
                g = 2 * (i % 2) + p
                if isinstance(i, int):
                    qh, ql = t["q_hi"][b, g], t["q_lo"][b, g]
                    kh, kl = (t[n][b, 0, g * HD:(g + 1) * HD, :] for n in ("k_hi", "k_lo"))
                else:
                    qh, ql = (t[n][ds(b, 1), ds(g, 1)].rearrange("o u p s -> (o u p) s") for n in ("q_hi", "q_lo"))
                    kh, kl = (t[n][ds(b, 1), :, ds(g * HD, HD), :].rearrange("o u p s -> (o u p) s") for n in ("k_hi", "k_lo"))
                for r, src in enumerate((qh, qh, ql)):
                    sp.dma_start(qst[p][r * HD:(r + 1) * HD, :, :].bitcast(F32),
                                 src.rearrange("(h d) s -> d h s", d=HD)).then_inc(qk_in[p], 16)
                for r, src in enumerate((kh, kl, kh)):
                    sp.dma_start(kst[p][r * HD:(r + 1) * HD, :].bitcast(F32), src).then_inc(qk_in[p], 16)

            def load_v(i, p):
                b = i // 2
                g = 2 * (i % 2) + p
                v = t["v"].rearrange("(b k p) (g d) -> b g p k d", p=P, k=NKT, d=HD)
                v = v[b, g] if isinstance(i, int) else v[ds(b, 1), ds(g, 1)].rearrange("o u p k d -> (o u p) k d")
                sp.dma_start(vst[p][:], v).then_inc(v_in[p], 16)

            def store(i, p, j):
                b = i // 2
                g = 2 * (i % 2) + p
                a = t["att"]
                a = a[b, g] if isinstance(i, int) else a[ds(b, 1), ds(g, 1)].rearrange("o u p s -> (o u p) s")
                bg = 2 * i + p
                sp.wait_ge(att_done, bg * JC + j + 1)
                sp.sem_inc(sp_pass, 1)
                sp.dma_start(a[:, j * CH:(j + 1) * CH], att[j % 2][:]).then_inc(att_out, 16)
                sp.wait_ge(att_out, 16 * (bg * JC + j + 1))
                sp.sem_inc(sp_pass, 1)

            sp.dma_start(ident[:], t["ident"]).then_inc(cst_in, 16)
            sp.dma_start(lowf[:], t["cmask"]).then_inc(cst_in, 16)
            for p in range(2):
                load_qk(0, p)
                load_v(0, p)
            with sp.Fori(0, BG // 2 - 1) as i:
                for p in range(2):
                    for j in range(JC):
                        store(i, p, j)
                    sp.wait_ge(s_done, (2 * i + p) * NU + NU)
                    sp.sem_inc(sp_pass, 1)
                    load_qk(i + 1, p)
                    sp.wait_ge(pv_done, (2 * i + p) * NK + NK + 8)
                    sp.sem_inc(sp_pass, 1)
                    load_v(i + 1, p)
            for p in range(2):
                for j in range(JC):
                    store(BG // 2 - 1, p, j)

        @block.gpsimd
        def _(pool):
            def group(bg):
                nd = 0
                for k in range(NK + 1):
                    for gi, f in enumerate(full):
                        if k == f + 4:
                            for pr in range(2):
                                G = bg * NGR + gi
                                pool.wait_ge(exp_done, bg * NU + 2 * (f + 3) + pr + 3)
                                pool.sem_inc(pool_pass, 1)
                                pool.wait_ge(suma_done, 2 * G + pr + 1)
                                pool.sem_inc(pool_pass, 1)
                                nc.gpsimd.tensor_tensor(sumb[gi % 2][pr][:], prb[:, (2 * (f + 2) + pr) % RP],
                                                        prb[:, (2 * (f + 3) + pr) % RP], ALU.add).then_inc(sumb_done, 1)
                    if k < NK and steps[k][2] >= 0:
                        q0 = steps[k][2] * P
                        for pr in range(2):
                            pool.wait_ge(exp_done, bg * NU + 2 * k + pr + 3)
                            pool.sem_inc(pool_pass, 1)
                            blk = prb[:, (2 * k + pr) % RP, :, q0:q0 + P]
                            nc.gpsimd.affine_select(out=blk, in_=blk, compare_op=ALU.is_ge, fill=0.0, base=0,
                                                    pattern=[[0, 2], [1, P]], channel_multiplier=-1).then_inc(sel_done, 1)

            with pool.Fori(0, BG // 2) as i:
                for p in range(2):
                    group(2 * i + p)

        @block.scalar
        def _(act):
            act.sem_inc(exp_done, 2)

            def maxima(bg, p):
                act.wait_ge(m_done, bg * MI + MI)
                act.wait_ge(c_in, 16 * bg)
                nc.scalar.activation(negt[:], mps[0:GROUP * NKT, (MI * p + NM) % 2, 0:P], ACT.Copy).then_inc(c_done, 1)
                act.wait_ge(c_done, bg + 1)
                act.dma_start(qst[p][R3:R3 + 1, :, :].bitcast(F32), negt[:].bitcast(F32)).then_inc(c_in, 16)

            maxima(0, 0)

            def group(bg, p, nxt):
                for k, (j, kt, r) in enumerate(steps):
                    q0 = max(r, 0) * P
                    if nxt and k == MFIN + 1:
                        maxima(bg + 1, 1 - p)
                    act.wait_ge(pv_done, bg * NK + k + 1)
                    for pr in range(2):
                        act.wait_ge(s_done, bg * NU + 2 * k + pr + 1)
                        kk = k - RP // 2
                        gi = [n for n, f in enumerate(full) if f <= kk % NK < f + 4]
                        if gi:
                            G = bg * NGR + gi[0] - (NGR if kk < 0 else 0)
                            if pr == 0:
                                act.wait_ge(add_done, 2 * G + 2)
                                act.wait_ge(sumb_done, 2 * G + 2)
                        nc.scalar.activation(prb[:, (2 * k + pr) % RP, :, q0:CH], sps[:, pr, :, q0:CH],
                                             ACT.Exp, scale=SCALE).then_inc(exp_done, 1)

            with act.Fori(0, BG // 2 - 1) as i:
                group(2 * i, 0, True)
                group(2 * i + 1, 1, True)
            group(BG - 2, 0, True)
            group(BG - 1, 1, False)

        @block.vector
        def _(dve):
            V = nc.vector
            V.memset(mx[:], -3.0e38).then_inc(init_v, 1)
            V.memset(ones[:], 1.0).then_inc(init_v, 1)
            for p in range(2):
                V.memset(kst[p][R3:R3 + 1, :].bitcast(F32), 1.0).then_inc(init_v, 1)
            dve.wait_ge(cst_in, 32)
            V.tensor_copy(identb[:], ident[:]).then_inc(init_v, 1)
            V.tensor_copy(cmask[:], lowf[:]).then_inc(init_v, 1)
            dve.wait_ge(init_v, 6)
            dve.sem_inc(suma_done, 4)

            def reduce(bg, p, n):
                h, qt, j, k0, w, wr, d = pieces[n]
                dve.wait_ge(m_done, bg * MI + n + 1)
                V.tensor_reduce(mx[:, h * NKT + qt, j:j + 1], mps[:, (MI * p + n) % 2, 0:wr], AX.X,
                                ALU.max).then_inc(mred_done, 1)

            def negate(bg):
                dve.wait_ge(mred_done, bg * NM + NM)
                V.tensor_reduce(neg[:], mx[:], AX.X, ALU.max, negate=True).then_inc(neg_done, 1)

            for n in range(NM):
                reduce(0, 0, n)
            negate(0)

            def normalize(bg, j):
                dve.wait_ge(pv_done, bg * NK + lasts[j] + 1 + 8)
                if j:
                    dve.wait_ge(ones_done, 2 * (bg * NGR + j * (j + 1) // 2) + 4)
                V.reciprocal(rden[:], dps[:]).then_inc(rden_done, 1)
                dve.wait_ge(rden_done, bg * JC + j + 1)
                dve.wait_ge(att_out, 16 * (bg * JC + j - 1) if j else 16 * (bg * JC))
                V.tensor_tensor(att[j % 2][:], ops[:], rden[:], ALU.mult).then_inc(att_done, 1)

            def group(bg, p, nxt):
                for k in range(NK + 1):
                    if k - 1 in lasts:
                        normalize(bg, lasts.index(k - 1))
                    for gi, f in enumerate(full):
                        G = bg * NGR + gi
                        if k == f + 2:
                            for pr in range(2):
                                dve.wait_ge(exp_done, bg * NU + 2 * (f + 1) + pr + 3)
                                dve.wait_ge(ones_done, 2 * G + pr + 1)
                                V.tensor_tensor(suma[gi % 2][pr][:], prb[:, (2 * f + pr) % RP],
                                                prb[:, (2 * (f + 1) + pr) % RP], ALU.add).then_inc(add_done, 1)
                        if k == f + 6:
                            for pr in range(2):
                                dve.wait_ge(add_done, 2 * G + pr + 1)
                                dve.wait_ge(sumb_done, 2 * G + pr + 1)
                                V.tensor_tensor(suma[gi % 2][pr][:], suma[gi % 2][pr][:], sumb[gi % 2][pr][:],
                                                ALU.add).then_inc(suma_done, 1)
                    if nxt:
                        for n in quota(k):
                            reduce(bg + 1, 1 - p, n)
                        if k == MFIN:
                            negate(bg + 1)

            with dve.Fori(0, BG // 2 - 1) as i:
                group(2 * i, 0, True)
                group(2 * i + 1, 1, True)
            group(BG - 2, 0, True)
            group(BG - 1, 1, False)

        @block.tensor
        def _(pe):
            M, TR = nc.tensor.matmul, nc.tensor.transpose

            def piece(bg, p, n):
                h, qt, j, k0, w, wr, d = pieces[n]
                if n >= 2:
                    pe.wait_ge(mred_done, bg * NM + n - 1)
                elif n == 0:
                    pe.wait_ge(mred_done, bg * NM)
                else:
                    pe.wait_ge(c_done, bg)
                out = mps[:, (MI * p + n) % 2, :]
                last = M(out[:, 0:w], qst[p][0:R3, h, qt * P:(qt + 1) * P], kst[p][0:R3, k0:k0 + w],
                         start=True, stop=True)
                if d is not None:
                    last = M(out[:, d:d + P], identb[:], cmask[:], start=False, stop=True, skip_group_check=True)
                last.then_inc(m_done, 1)

            def turn(bg, p):
                pe.wait_ge(neg_done, bg + 1)
                pe.sem_inc(pe_pass, 1)
                TR(mps[0:GROUP * NKT, (MI * p + NM) % 2, 0:P], neg[:], ident[:]).then_inc(m_done, 1)

            pe.wait_ge(init_v, 6)
            pe.sem_inc(pv_done, 8)
            pe.sem_inc(ones_done, 4)
            pe.wait_ge(qk_in[0], 96)
            for n in range(NM):
                piece(0, 0, n)
            turn(0, 0)

            def scores(bg, p, k):
                j, kt, r = steps[k]
                q0 = min(max(r, 0) * P, CH - 2 * P)
                for pr in range(2):
                    pe.wait_ge(exp_done, bg * NU + 2 * k + pr + 1)
                    for hh in range(2):
                        last = M(sps[:, pr, hh, q0:CH], kst[p][0:R3 + 1, kt * P:(kt + 1) * P],
                                 qst[p][0:R3 + 1, 2 * pr + hh, j * CH + q0:(j + 1) * CH], start=True, stop=True)
                    last.then_inc(s_done, 1)

            def output(bg, p, k):
                j, kt, r = steps[k]
                q0 = max(r, 0) * P
                pe.wait_ge(exp_done, bg * NU + 2 * k + 4)
                if r >= 0:
                    pe.wait_ge(sel_done, bg * 2 * len(diag) + 2 * diag.index(k) + 2)
                if kt == 0:
                    pe.wait_ge(att_done, bg * JC + j)
                for h in range(GROUP):
                    last = M(ops[HD * h:HD * (h + 1), q0:CH], vst[p][:, kt, :],
                             prb[:, (2 * k + h // 2) % RP, h % 2, q0:CH], start=(kt == 0), stop=(r == 3),
                             skip_group_check=True)
                if r >= 0:
                    for h in range(GROUP):
                        last = M(dps[HD * h:HD * (h + 1), q0:CH], ones[:],
                                 prb[:, (2 * k + h // 2) % RP, h % 2, q0:CH], start=(j <= 1 and r == 0),
                                 stop=(r == 3), skip_group_check=True)
                last.then_inc(pv_done, 1)

            def group_sum(bg, gi):
                for pr in range(2):
                    G = bg * NGR + gi
                    pe.wait_ge(suma_done, 2 * G + pr + 5)
                    first = steps[full[gi]][1] == 0 and steps[full[gi]][0] > 1
                    if first and pr == 0:
                        pe.wait_ge(att_done, bg * JC + steps[full[gi]][0])
                    for hh in range(2):
                        h = 2 * pr + hh
                        last = M(dps[HD * h:HD * (h + 1), :], ones[:], suma[gi % 2][pr][:, hh, :],
                                 start=first, stop=False, skip_group_check=True)
                    last.then_inc(ones_done, 1)

            def group(bg, p, nxt):
                for k in range(NK + 1):
                    if k < NK:
                        scores(bg, p, k)
                    for gi, f in enumerate(full):
                        if k == f + 7:
                            group_sum(bg, gi)
                    if k:
                        output(bg, p, k - 1)
                    if nxt:
                        for n in quota(k):
                            piece(bg + 1, 1 - p, n)
                        if k == MFIN:
                            turn(bg + 1, 1 - p)

            with pe.Fori(0, BG // 2 - 1) as i:
                for p in range(2):
                    bg = 2 * i + p
                    pe.wait_ge(c_in, 16 * bg + 16)
                    pe.wait_ge(v_in[p], 16 * i + 16)
                    pe.wait_ge(qk_in[1 - p], 96 * i + 96 * p + 96)
                    group(bg, p, True)
            for p in range(2):
                i = BG // 2 - 1
                pe.wait_ge(c_in, 16 * (2 * i + p) + 16)
                pe.wait_ge(v_in[p], 16 * i + 16)
                if p == 0:
                    pe.wait_ge(qk_in[1], 96 * i + 96)
                group(2 * i + p, p, p == 0)


def stage_c(nc, t):
    ctx = ExitStack()
    with ctx:
        def sb(name, shape, dt=F32):
            return ctx.enter_context(nc.sbuf_tensor(name, shape, dt))

        def sem(name):
            return ctx.enter_context(nc.semaphore(name))

        def two(name, shape, dt=F32):
            return [sb(f"{name}{p}", shape, dt) for p in range(2)]

        wo = sb("wo", [P, KC, D])
        wo_hi = sb("wo_hi", [P, KC, D], F32R)
        wo_lo = sb("wo_lo", [P, KC, D], F32R)
        a_in = two("a_in", [P, KC, CH])
        a_hi = two("a_hi", [P, KC, CH], F32R)
        a_lo = two("a_lo", [P, KC, CH], F32R)
        y = two("y_c", [P, NT, D])
        ops = ctx.enter_context(nc.psum_tensor("cps", [P, 8, D], F32))
        w_in = sem("wo_in")
        w_hi = sem("wo_hi_done")
        w_lo = sem("wo_lo_done")
        a_ld = [sem("a_ld0"), sem("a_ld1")]
        y_ld = [sem("y_ld0"), sem("y_ld1")]
        hi_done = sem("a_hi_done")
        lo_done = sem("a_lo_done")
        o_done = sem("o_done")
        y_done = sem("yc_done")
        y_st = [sem("y_st0"), sem("y_st1")]
        sp_pass = sem("sp_pass_c")
        block = ctx.enter_context(nc.Block())

        def rows(ap, c):
            v = ap.rearrange("(c t p) d -> c p t d", p=P, t=NT)
            return v[c] if isinstance(c, int) else v[ds(c, 1)].rearrange("o p t d -> (o p) t d")

        def load(sp, c, p):
            a = t["att"]
            if isinstance(c, int):
                a = a[c // JC, :, :, (c % JC) * CH:(c % JC + 1) * CH].rearrange("g p s -> p g s")
            else:
                a = a[ds(c // JC, 1), :, :, ds((c % JC) * CH, CH)].rearrange("o g p s -> (o p) g s")
            sp.dma_start(a_in[p][:], a).then_inc(a_ld[p], 16)
            sp.dma_start(y[p][:], rows(t["base"][0:T, :], c)).then_inc(y_ld[p], 16)

        @block.sync
        def _(sp):
            sp.dma_start(wo[:], t["w_o"].rearrange("(k p) n -> p k n", p=P)).then_inc(w_in, 16)
            load(sp, 0, 0)
            load(sp, 1, 1)
            with sp.Fori(0, NC // 2 - 1) as i:
                for p in range(2):
                    sp.wait_ge(y_st[p], 16 * i + 16)
                    sp.sem_inc(sp_pass, 1)
                    load(sp, 2 * i + p + 2, p)

        @block.scalar
        def _(act):
            act.wait_ge(w_in, 16)
            nc.scalar.activation(wo_hi[:], wo[:], ACT.Copy).then_inc(w_hi, 1)
            with act.Fori(0, NC // 2) as i:
                for p in range(2):
                    c = 2 * i + p
                    act.wait_ge(a_ld[p], 16 * i + 16)
                    act.wait_ge(o_done, 2 * NT * i)
                    nc.scalar.activation(a_hi[p][:], a_in[p][:], ACT.Copy).then_inc(hi_done, 1)
                    act.wait_ge(y_done, c * NT + NT)
                    act.dma_start(rows(t["out"], c), y[p][:]).then_inc(y_st[p], 16)
            act.wait_ge(y_st[0], 16 * (NC // 2))
            act.wait_ge(y_st[1], 16 * (NC // 2))

        @block.vector
        def _(dve):
            V = nc.vector
            dve.wait_ge(w_hi, 1)
            V.tensor_tensor(wo_lo[:], wo[:], wo_hi[:].bitcast(F32), ALU.subtract).then_inc(w_lo, 1)
            with dve.Fori(0, NC // 2) as i:
                for p in range(2):
                    c = 2 * i + p
                    dve.wait_ge(hi_done, c + 1)
                    V.tensor_tensor(a_lo[p][:], a_in[p][:], a_hi[p][:].bitcast(F32), ALU.subtract).then_inc(lo_done, 1)
                    dve.wait_ge(y_ld[p], 16 * i + 16)
                    for n in range(NT):
                        dve.wait_ge(o_done, c * NT + n + 1)
                        V.tensor_tensor(y[p][:, n, :], ops[:, NT * p + n, :], y[p][:, n, :], ALU.add).then_inc(y_done, 1)

        @block.tensor
        def _(pe):
            pe.wait_ge(w_lo, 1)
            with pe.Fori(0, NC // 2) as i:
                for p in range(2):
                    c = 2 * i + p
                    pe.wait_ge(lo_done, c + 1)
                    for n in range(NT):
                        m = 0
                        for k in range(KC):
                            for a, w in ((a_hi, wo_hi), (a_lo, wo_hi), (a_hi, wo_lo)):
                                last = nc.tensor.matmul(ops[:, NT * p + n, :], a[p][:, k, n * P:(n + 1) * P],
                                                        w[:, k, :], start=(m == 0), stop=(m == 3 * KC - 1))
                                m += 1
                        last.then_inc(o_done, 1)


def host_constants(np):
    tri = np.tril(np.ones((NG, NG), np.float32), -1).reshape(-1)
    row = np.concatenate([np.arange(E), np.arange(E) * CAP, tri]).astype(np.float32)
    cst = np.concatenate([np.tile(row, (P, 1)), (np.arange(P)[:, None] + P * np.arange(NT)[None, :])], 1)
    cmask = np.triu(np.full((P, P), NEG, np.float32), 1)
    upper = np.triu(np.ones((P, P)), 1)
    return {"ident": np.eye(P, dtype=np.float32), "upper": upper.astype(np.float32), "cmask": cmask,
            "cst": np.ascontiguousarray(cst, dtype=np.float32)}


def host_layout(np, a):
    gu = a["L0_ffn_ws_gate_up"]
    cols = []
    for m in range(FM):
        w = min(P, ISH - m * P)
        cols += [gu[:, m * P:m * P + w], gu[:, ISH + m * P:ISH + m * P + w]]
    w_a = np.concatenate([a["L0_attn_Wq"], a["L0_attn_Wk"], a["L0_attn_Wv"], a["L0_ffn_gate_w"].T] + cols, 1)
    w_d = np.concatenate([a["L0_ffn_ws_down"], np.zeros((FM * P - ISH, D), np.float32)], 0)
    return {"x": np.ascontiguousarray(a["L0_attn_x"]).reshape(T, D), "w_a": np.ascontiguousarray(w_a),
            "w_d": np.ascontiguousarray(w_d), "w_o": np.ascontiguousarray(a["L0_attn_Wo"]),
            "e_gu": np.ascontiguousarray(a["L0_ffn_w_gate_up"]), "e_d": np.ascontiguousarray(a["L0_ffn_w_down"])}


def scratch(nc, out, dbg=()):
    def dram(name, shape, dt):
        return nc.dram_tensor(name, shape, dt, **({"kind": "ExternalOutput"} if name in dbg else {})).ap()
    return {"base": dram("base", [T + CAP, D], F32), "xn": dram("xn_s", [T + CAP, D], F32), "v": dram("v_s", [T, P], F32),
            "q_hi": dram("q_hi_s", [B, NKV, P, S], F32), "q_lo": dram("q_lo_s", [B, NKV, P, S], F32),
            "k_hi": dram("k_hi_s", [B, 1, P, S], F32), "k_lo": dram("k_lo_s", [B, 1, P, S], F32),
            "tab": dram("tab_s", [E * CAP, 2], U32), "att": dram("att_s", [B, NKV, P, S], F32)}


def kernel(**inputs):
    import numpy as _np
    import concourse.bacc as _bacc
    from concourse.bass_utils import run_bass_kernel_spmd as _run

    nc = _bacc.Bacc("TRN2", target_bir_lowering=False, num_devices=1)
    arrays, t = {}, {}
    for name, a in {**host_layout(_np, inputs), **host_constants(_np)}.items():
        arrays[f"in_{name}"] = a
        t[name] = nc.dram_tensor(f"in_{name}", a.shape, mybir.dt.from_np(a.dtype), kind="ExternalInput").ap()
    t["out"] = nc.dram_tensor("out", [T, D], F32, kind="ExternalOutput").ap()
    t.update(scratch(nc, None))
    stage_a(nc, t)
    stage_m(nc, t)
    stage_b(nc, t)
    stage_c(nc, t)
    r = _run(nc, [arrays], core_ids=[0])
    return r.results[0]["out"].reshape(B, S, D)
```

```python
from contextlib import ExitStack

import concourse.bass as bass
from concourse import mybir

ALU = mybir.AluOpType
ACT = mybir.ActivationFunctionType
AX = mybir.AxisListType
F32 = mybir.dt.float32
F32R = mybir.dt.float32r
BF16 = mybir.dt.bfloat16
U32 = mybir.dt.uint32
ds = bass.ds

P = 128
B, S, D = 4, 2048, 512
T = B * S
NH, NKV, HD = 16, 4, 32
GROUP = NH // NKV
KC = D // P
CH = 512
NT = CH // P
NC = T // CH
JC = S // CH
SCALE = HD ** -0.5
EPS = 1e-5

E, TOPK, NG, TG, CAP, I = 32, 6, 8, 3, 96, 352
GE = E // NG
ROUTE_SCALE = 16.0
ISH = 2 * I
FM = (ISH + P - 1) // P
FT = ISH - (FM - 1) * P
NOSLOT = 100000.0
IC = (I + P - 1) // P
IT = I - (IC - 1) * P
NKT = S // P
BG = B * NKV
NEG = -1.0e30

C_Q, C_K, C_V, C_G = 0, D, D + P, D + 2 * P
C_GU = C_G + E
WCOL = C_GU + 2 * ISH


def stage_a(nc, t, dbg=None):
    ctx = ExitStack()
    with ctx:
        def sb(name, shape, dt=F32):
            return ctx.enter_context(nc.sbuf_tensor(name, shape, dt))

        def ps(name, shape):
            return ctx.enter_context(nc.psum_tensor(name, shape, F32))

        def sem(name):
            return ctx.enter_context(nc.semaphore(name))

        w_hi = sb("w_hi", [P, KC, WCOL], F32R)
        w_lo = sb("w_lo", [P, KC, WCOL], F32R)
        d_hi = sb("d_hi", [P, FM, D], F32R)
        d_lo = sb("d_lo", [P, FM, D], F32R)
        ident = sb("ident", [P, P])
        uppf = sb("uppf", [P, P])
        before = sb("before", [P, P], BF16)
        ones = sb("ones", [P, P], BF16)
        cst = sb("cst", [P, 2 * E + NG * NG + NT])
        x_sb = sb("x_sb", [P, NT, D])
        xn = sb("xn", [P, NT, D])
        x_hi = sb("x_hi", [P, KC, CH], F32R)
        x_lo = sb("x_lo", [P, KC, CH], F32R)
        qk_hi = sb("qk_hi", [P, NKV + 1, CH], F32R)
        qk_lo = sb("qk_lo", [P, NKV + 1, CH], F32R)
        v_f = sb("v_f", [P, CH])
        v_t = sb("v_t", [P, NT, P])
        l_f = sb("l_f", [E, CH])
        sil = sb("sil", [P, CH])
        h_sb = sb("h_sb", [P, CH])
        up_t = sb("up_t", [FT, CH])
        h_hi = sb("h_hi", [P, FM, CH], F32R)
        h_lo = sb("h_lo", [P, FM, CH], F32R)
        y_sb = sb("y_sb", [P, NT, D])
        stats = sb("stats", [P, NT, 6])
        mv = sb("mv", [P, NT, 2])
        rstd = sb("rstd", [P, NT])
        var = sb("var", [P, NT])
        dev = sb("dev", [P, NT])
        nwt = sb("nwt", [P, NT])
        lg = sb("lg", [P, NT, E])
        gm = sb("gm", [P, NT, NG])
        gt = sb("gt", [P, NT, NG, NG])
        eq = sb("eq", [P, NT, NG, NG])
        rank = sb("rank", [P, NT, NG])
        keep = sb("keep", [P, NT, NG])
        sc = sb("sc", [P, NT, E])
        rmax = sb("rmax", [P, NT])
        shf = sb("shf", [P, NT, E])
        pe_ = sb("pexp", [P, NT, E])
        rs = sb("rs", [P, NT])
        rr = sb("rr", [P, NT])
        prob = sb("prob", [P, NT, E])
        v8 = sb("v8", [P, NT, 8])
        i8 = sb("i8", [P, NT, 8], U32)
        i8f = sb("i8f", [P, NT, 8])
        oh = sb("oh", [P, NT, TOPK, E])
        mask = sb("mask", [P, NT, E], BF16)
        cnt = sb("cnt", [P, E])
        pos = sb("pos", [P, NT, E])
        ovf = sb("ovf", [P, NT, E])
        slt = sb("slt", [P, NT, E])
        ohs = sb("ohs", [P, NT, TOPK, E])
        slk = sb("slk", [P, NT, TOPK])
        slot = sb("slot", [P, NT, TOPK], U32)
        tokf = sb("tokf", [P, NT])
        pay = sb("pay", [P, NT, TOPK, 2], U32)
        empty = sb("empty", [CAP, E, 2], U32)

        ACCB = 3
        acc = ps("acc", [P, ACCB, CH])
        xtp = ps("xtp", [P, 2, CH])
        yp = ps("yp", [P, 2, D])
        smp = ps("smp", [P, CH])

        cst_in = sem("cst_in")
        w_in = [sem("w_in0"), sem("w_in1")]
        w_hi_done = sem("w_hi_done")
        w_lo_done = sem("w_lo_done")
        init_v = sem("init_v")
        x_in = sem("x_in")
        xr_in = sem("xr_in")
        xn_out = sem("xn_out")
        qkv_out = sem("qkv_out")
        y_out = sem("y_out")
        tab_init = sem("tab_init")
        tab_out = sem("tab_out")
        acc_done = sem("acc_done")
        xt_done = sem("xt_done")
        vt_psum = sem("vt_psum")
        lt_psum = sem("lt_psum")
        pos_psum = sem("pos_psum")
        y_done = sem("y_done")
        qhi_done = sem("qhi_done")
        qlo_done = sem("qlo_done")
        v_done = sem("v_done")
        l_done = sem("l_done")
        vt_done = sem("vt_done")
        lt_read = sem("lt_read")
        pos_read = sem("pos_read")
        shf_done = sem("shf_done")
        pexp_done = sem("pexp_done")
        mask_done = sem("mask_done")
        slots_done = sem("slots_done")
        ln_done = sem("ln_done")
        x_free = sem("x_free")
        sil_done = sem("sil_done")
        glu_done = sem("glu_done")
        hhi_done = sem("hhi_done")
        hlo_done = sem("hlo_done")
        xhi_done = sem("xhi_done")
        xlo_done = sem("xlo_done")
        ysb_done = sem("ysb_done")
        upt_done = sem("upt_done")
        var_done = sem("var_done")
        dev_done = sem("dev_done")
        rstd_done = sem("rstd_done")
        dve_pass, pe_pass, sp_pass, pool_pass = (sem(f"{e}_pass_a") for e in ("dve", "pe", "sp", "pool"))
        chain = sem("chain")

        NACC = NKV + 3 + 2 * FM - 1
        FIRST_F = NKV + 3

        pieces = []
        for k in range(KC):
            for a, n in ((0, C_GU // 2), (C_GU // 2, C_GU // 2), (C_GU, ISH), (C_GU + ISH, ISH)):
                pieces.append((t["w_a"][k * P:(k + 1) * P, a:a + n], w_hi[:, k, a:a + n], w_lo[:, k, a:a + n], n))
        for m in range(0, FM, 2):
            pieces.append((t["w_d"].rearrange("(m p) n -> p m n", p=P)[:, m:m + 2, :],
                           d_hi[:, m:m + 2, :], d_lo[:, m:m + 2, :], 2 * D))
        NPC = len(pieces)
        stg = [y_sb[:, 0:2, :].rearrange("p a b -> p (a b)"), y_sb[:, 2:4, :].rearrange("p a b -> p (a b)")]

        def staged(n):
            src, hi, lo, cols = pieces[n]
            v = stg[n % 2][:, 0:cols]
            return v if len(hi.shape) == 2 else v.rearrange("p (a b) -> p a b", b=D)

        iota_e = cst[:, 0:E]
        slot_e = cst[:, E:2 * E]
        tri = cst[:, 2 * E:2 * E + NG * NG].rearrange("p (a b) -> p a b", b=NG)
        tok0 = cst[:, 2 * E + NG * NG:]

        x_d = t["x"].rearrange("(c t p) d -> c p t d", p=P, t=NT)
        xn_d = t["xn"][0:T, :].rearrange("(c t p) d -> c p t d", p=P, t=NT)
        base_d = t["base"][0:T, :].rearrange("(c t p) d -> c p t d", p=P, t=NT)
        v_d = t["v"].rearrange("(c t p) d -> c p t d", p=P, t=NT)

        def chunk(ap, c):
            return ap[c] if isinstance(c, int) else ap[ds(c, 1)].rearrange("o p t d -> (o p) t d")

        def columns(ap4, c):
            if isinstance(c, int):
                return ap4[c // JC, :, :, (c % JC) * CH:(c % JC + 1) * CH].rearrange("g p s -> p g s")
            return ap4[ds(c // JC, 1), :, :, ds((c % JC) * CH, CH)].rearrange("o g p s -> (o p) g s")

        block = ctx.enter_context(nc.Block())

        @block.sync
        def _(sp):
            sp.dma_start(ident[:], t["ident"]).then_inc(cst_in, 16)
            sp.dma_start(uppf[:], t["upper"]).then_inc(cst_in, 16)
            sp.dma_start(cst[:], t["cst"]).then_inc(cst_in, 16)
            sp.dma_start(x_sb[:], chunk(x_d, 0)).then_inc(x_in, 16)
            sp.wait_ge(init_v, 9)
            sp.dma_start(t["xn"][T:T + CAP, :], xn[0:CAP, 0, :]).then_inc(tab_init, 16)
            sp.dma_start(t["base"][T:T + CAP, :], xn[0:CAP, 0, :]).then_inc(tab_init, 16)
            for n, (src, hi, lo, cols) in enumerate(pieces):
                if n >= 2:
                    sp.wait_ge(w_lo_done, n - 1)
                sp.dma_start(staged(n), src).then_inc(w_in[n % 2], 16)
            sp.dma_start(t["tab"].rearrange("(e s) w -> s e w", s=CAP), empty[:]).then_inc(tab_init, 16)
            sp.wait_ge(ln_done, NT)
            sp.dma_start(chunk(xn_d, 0), xn[:]).then_inc(xn_out, 16)
            sp.dma_start(x_sb[:], chunk(x_d, 1)).then_inc(x_in, 16)

            def body(c, nxt, nxt2):
                sp.wait_ge(ysb_done, c * NT + 2)
                sp.sem_inc(sp_pass, 1)
                sp.dma_start(y_sb[:], chunk(x_d, c)).then_inc(xr_in, 16)
                sp.wait_ge(qlo_done, c * (NKV + 1) + NKV + 1)
                sp.sem_inc(sp_pass, 1)
                sp.wait_ge(qhi_done, c * (NKV + 1) + NKV + 1)
                sp.sem_inc(sp_pass, 1)
                sp.dma_start(columns(t["q_hi"], c), qk_hi[:, 0:NKV, :].bitcast(F32)).then_inc(qkv_out, 16)
                sp.dma_start(columns(t["q_lo"], c), qk_lo[:, 0:NKV, :].bitcast(F32)).then_inc(qkv_out, 16)
                sp.dma_start(columns(t["k_hi"], c), qk_hi[:, NKV:NKV + 1, :].bitcast(F32)).then_inc(qkv_out, 16)
                sp.dma_start(columns(t["k_lo"], c), qk_lo[:, NKV:NKV + 1, :].bitcast(F32)).then_inc(qkv_out, 16)
                sp.wait_ge(vt_done, c + 1)
                sp.sem_inc(sp_pass, 1)
                sp.dma_start(chunk(v_d, c), v_t[:]).then_inc(qkv_out, 16)
                if nxt:
                    sp.wait_ge(ln_done, c * NT + 2 * NT)
                    sp.sem_inc(sp_pass, 1)
                    sp.dma_start(chunk(xn_d, c + 1), xn[:]).then_inc(xn_out, 16)
                if nxt2:
                    sp.dma_start(x_sb[:], chunk(x_d, c + 2)).then_inc(x_in, 16)
                sp.wait_ge(ysb_done, c * NT + NT + 2)
                sp.sem_inc(sp_pass, 1)
                sp.dma_start(chunk(base_d, c), y_sb[:]).then_inc(y_out, 16)
                sp.wait_ge(y_out, c * 16 + 16)
                sp.sem_inc(sp_pass, 1)

            sp.wait_ge(w_lo_done, NPC)
            with sp.Fori(0, NC - 2) as c:
                body(c, True, True)
            body(NC - 2, True, False)
            body(NC - 1, False, False)
            sp.wait_ge(tab_init, 48)
            sp.wait_ge(xn_out, 16 * NC)
            sp.wait_ge(qkv_out, 80 * NC)
            sp.wait_ge(y_out, 16 * NC)

        @block.gpsimd
        def _(pool):
            pool.wait_ge(tab_init, 48)

            with pool.Fori(0, NC) as c:
                pool.wait_ge(slots_done, c + 1)
                pool.sem_inc(pool_pass, 1)
                for i in range(NT):
                    for k in range(TOPK):
                        nc.gpsimd.indirect_dma_start(
                            t["tab"], bass.IndirectOffsetOnAxis(ap=slot[:, i, k:k + 1], axis=0),
                            pay[:, i, k, :], None, bounds_check=E * CAP - 1, oob_is_err=False,
                        ).then_inc(tab_out, 16)
                pool.wait_ge(tab_out, c * (16 * NT * TOPK) + 16 * NT * TOPK)
                pool.sem_inc(pool_pass, 1)

            pool.wait_ge(tab_out, NC * (16 * NT * TOPK))

        @block.scalar
        def _(act):
            def deviation(c):
                act.wait_ge(var_done, 2 * c + 2)
                nc.scalar.activation(dev[:], var[:], ACT.Sqrt).then_inc(dev_done, 1)

            deviation(0)

            for n in range(NPC):
                act.wait_ge(w_in[n % 2], 16 * (n // 2 + 1))
                nc.scalar.activation(pieces[n][1], staged(n), ACT.Copy).then_inc(w_hi_done, 1)

            def xhi(c):
                for k in range(KC):
                    act.wait_ge(xt_done, c * KC + k + 1)
                    nc.scalar.activation(x_hi[:, k, :], xtp[:, k % 2, :], ACT.Copy).then_inc(xhi_done, 1)

            def body(c, nxt):
                act.wait_ge(qkv_out, c * 80)
                for i in range(NKV + 1):
                    act.wait_ge(acc_done, c * NACC + i + 1)
                    nc.scalar.activation(qk_hi[:, i, :], acc[:, i % ACCB, :], ACT.Copy).then_inc(qhi_done, 1)
                act.wait_ge(acc_done, c * NACC + NKV + 2)
                nc.scalar.activation(v_f[:], acc[:, (NKV + 1) % ACCB, :], ACT.Copy).then_inc(v_done, 1)
                act.wait_ge(acc_done, c * NACC + NKV + 3)
                nc.scalar.activation(l_f[:], acc[0:E, (NKV + 2) % ACCB, :], ACT.Copy).then_inc(l_done, 1)
                act.wait_ge(vt_psum, c + 1)
                nc.scalar.activation(v_t[:].rearrange("p t d -> p (t d)"), smp[:], ACT.Copy).then_inc(vt_done, 1)
                act.wait_ge(shf_done, c + 1)
                nc.scalar.activation(pe_[:], shf[:], ACT.Exp).then_inc(pexp_done, 1)
                if nxt:
                    deviation(c + 1)
                for m in range(FM):
                    last = m == FM - 1
                    rows = FT if last else P
                    i = FIRST_F + 2 * m
                    act.wait_ge(acc_done, c * NACC + i + 1)
                    act.wait_ge(glu_done, c * FM + m + FM)
                    nc.scalar.activation(sil[0:rows, :], acc[0:rows, i % ACCB, :], ACT.Silu).then_inc(sil_done, 1)
                    act.wait_ge(glu_done, c * FM + m + 1 + FM)
                    nc.scalar.activation(h_hi[0:rows, m, :], h_sb[0:rows, :], ACT.Copy).then_inc(hhi_done, 1)
                if nxt:
                    act.wait_ge(acc_done, c * NACC + NACC)
                    xhi(c + 1)

            act.wait_ge(init_v, 1)
            xhi(0)
            with act.Fori(0, NC - 1) as c:
                body(c, True)
            body(NC - 1, False)

        @block.vector
        def _(dve):
            N_CHAIN = 20
            count = [0]

            def link(ins, c):
                count[0] += 1
                ins.then_inc(chain, 1)
                dve.wait_ge(chain, c * N_CHAIN + count[0])

            V = nc.vector
            V.memset(h_hi[:, FM - 1, :].bitcast(F32), 0.0).then_inc(init_v, 1)
            V.memset(h_lo[:, FM - 1, :].bitcast(F32), 0.0).then_inc(init_v, 1)
            V.memset(ones[:], 1.0).then_inc(init_v, 1)
            V.memset(cnt[:], 0.0).then_inc(init_v, 1)
            V.memset(empty[:], 0).then_inc(init_v, 1)
            V.memset(xn[:, 0, :], 0.0).then_inc(init_v, 1)
            dve.sem_inc(glu_done, FM)
            dve.sem_inc(ysb_done, 2)
            dve.wait_ge(cst_in, 48)
            V.tensor_copy(before[:], uppf[:]).then_inc(init_v, 1)
            V.tensor_copy(tokf[:], tok0).then_inc(init_v, 1)
            dve.wait_ge(init_v, 6)
            V.tensor_scalar(empty[:, :, 0], tok0[0:CAP, 0:1].to_broadcast([CAP, E]), float(T), None,
                            ALU.add).then_inc(init_v, 1)
            dve.wait_ge(init_v, 9)

            def ln_stats(c):
                dve.wait_ge(x_in, c * 16 + 16)
                for i in range(NT):
                    V.bn_stats(out=stats[:, i, :], in_=x_sb[:, i, :]).then_inc(x_free, 1)

            def ln_variance(c):
                dve.wait_ge(x_free, c * NT + NT)
                dve.sem_inc(dve_pass, 1)
                for i in range(NT):
                    last = V.bn_aggr(out=mv[:, i, :], in_=stats[:, i, :])
                last.then_inc(var_done, 1)
                dve.wait_ge(var_done, 2 * c + 1)
                V.tensor_scalar(var[:], mv[:, :, 1], EPS, None, ALU.add).then_inc(var_done, 1)

            def ln_inverse(c):
                dve.wait_ge(dev_done, c + 1)
                V.reciprocal(rstd[:], dev[:]).then_inc(rstd_done, 1)
                dve.wait_ge(rstd_done, c * 5 + 1)
                V.tensor_tensor(nwt[:], var[:], rstd[:], ALU.mult).then_inc(rstd_done, 1)
                dve.wait_ge(rstd_done, c * 5 + 2)
                V.tensor_tensor(nwt[:], nwt[:], rstd[:], ALU.mult).then_inc(rstd_done, 1)
                dve.wait_ge(rstd_done, c * 5 + 3)
                V.tensor_scalar(nwt[:], nwt[:], -0.5, 1.5, ALU.mult, ALU.add).then_inc(rstd_done, 1)
                dve.wait_ge(rstd_done, c * 5 + 4)
                V.tensor_tensor(rstd[:], rstd[:], nwt[:], ALU.mult).then_inc(rstd_done, 1)

            def ln_scale(c):
                dve.wait_ge(rstd_done, c * 5 + 5)
                dve.wait_ge(tab_init, 32)
                dve.wait_ge(xn_out, c * 16)
                dve.wait_ge(xt_done, c * KC)
                for i in range(NT):
                    V.tensor_scalar(xn[:, i, :], x_sb[:, i, :], mv[:, i, 0:1], rstd[:, i:i + 1],
                                    ALU.subtract, ALU.mult).then_inc(ln_done, 1)

            def xlo(c):
                for k in range(KC):
                    dve.wait_ge(xhi_done, c * KC + k + 1)
                    V.tensor_tensor(x_lo[:, k, :], xtp[:, k % 2, :], x_hi[:, k, :].bitcast(F32),
                                    ALU.subtract).then_inc(xlo_done, 1)

            ln_stats(0)
            ln_variance(0)
            ln_inverse(0)
            ln_scale(0)
            for n in range(NPC):
                dve.wait_ge(w_hi_done, n + 1)
                V.tensor_tensor(pieces[n][2], staged(n), pieces[n][1].bitcast(F32),
                                ALU.subtract).then_inc(w_lo_done, 1)
            xlo(0)

            def body(c, nxt):
                count[0] = 0
                dve.wait_ge(qkv_out, c * 80)
                for i in range(NKV + 1):
                    dve.wait_ge(qhi_done, c * (NKV + 1) + i + 1)
                    V.tensor_tensor(qk_lo[:, i, :], acc[:, i % ACCB, :], qk_hi[:, i, :].bitcast(F32),
                                    ALU.subtract).then_inc(qlo_done, 1)
                dve.wait_ge(lt_psum, c + 1)
                V.tensor_copy(lg[:].rearrange("p t e -> p (t e)"), smp[:, 0:NT * E]).then_inc(lt_read, 1)
                dve.wait_ge(lt_read, c + 1)
                link(V.tensor_reduce(gm[:].rearrange("p t g -> p (t g)"),
                                     lg[:].rearrange("p t (g e) -> p (t g) e", g=NG), AX.X, ALU.max), c)
                other = gm[:].unsqueeze(2).to_broadcast([P, NT, NG, NG])
                own = gm[:].unsqueeze(3).to_broadcast([P, NT, NG, NG])
                V.tensor_tensor(gt[:], other, own, ALU.is_gt)
                link(V.tensor_tensor(eq[:], other, own, ALU.is_equal), c)
                link(V.tensor_tensor(eq[:], eq[:], tri.unsqueeze(1).to_broadcast([P, NT, NG, NG]), ALU.mult), c)
                link(V.tensor_tensor(gt[:], gt[:], eq[:], ALU.add), c)
                link(V.tensor_reduce(rank[:].rearrange("p t g -> p (t g)"),
                                     gt[:].rearrange("p t a b -> p (t a) b"), AX.X, ALU.add), c)
                link(V.tensor_scalar(keep[:], rank[:], float(TG), None, ALU.is_lt), c)
                link(V.tensor_tensor(sc[:].rearrange("p t (g e) -> p t g e", g=NG),
                                     lg[:].rearrange("p t (g e) -> p t g e", g=NG),
                                     keep[:].unsqueeze(3).to_broadcast([P, NT, NG, GE]), ALU.mult), c)
                link(V.tensor_reduce(rmax[:], sc[:], AX.X, ALU.max), c)
                V.tensor_tensor(shf[:], sc[:], rmax[:].unsqueeze(2).to_broadcast([P, NT, E]),
                                ALU.subtract).then_inc(shf_done, 1)
                if nxt:
                    ln_stats(c + 1)
                    ln_variance(c + 1)
                dve.wait_ge(pexp_done, c + 1)
                link(V.tensor_reduce(rs[:], pe_[:], AX.X, ALU.add), c)
                link(V.reciprocal(rr[:], rs[:]), c)
                link(V.tensor_tensor(prob[:], pe_[:], rr[:].unsqueeze(2).to_broadcast([P, NT, E]), ALU.mult), c)
                dve.sem_inc(dve_pass, 1)
                for i in range(NT):
                    last = V.max(v8[:, i, :], prob[:, i, :])
                link(last, c)
                dve.sem_inc(dve_pass, 1)
                for i in range(NT):
                    last = V.max_index(i8[:, i, :], v8[:, i, :], prob[:, i, :])
                link(last, c)
                link(V.tensor_copy(i8f[:], i8[:]), c)
                link(V.tensor_tensor(oh[:], iota_e.unsqueeze(1).unsqueeze(1).to_broadcast([P, NT, TOPK, E]),
                                     i8f[:, :, 0:TOPK].unsqueeze(3).to_broadcast([P, NT, TOPK, E]),
                                     ALU.is_equal), c)
                with nc.allow_low_precision(reason="sums of zeros and at most one 1 are exact"):
                    V.tensor_reduce(mask[:], oh[:].rearrange("p t k e -> p t e k"), AX.X,
                                    ALU.add).then_inc(mask_done, 1)

                def glu(m):
                    last = m == FM - 1
                    rows = FT if last else P
                    i = FIRST_F + 2 * m
                    if last:
                        dve.wait_ge(acc_done, c * NACC + i + 1)
                        V.tensor_copy(up_t[:], acc[FT:2 * FT, i % ACCB, :]).then_inc(upt_done, 1)
                        dve.wait_ge(upt_done, c + 1)
                        up = up_t[:]
                    else:
                        dve.wait_ge(acc_done, c * NACC + i + 2)
                        up = acc[:, (i + 1) % ACCB, :]
                    dve.wait_ge(sil_done, c * FM + m + 1)
                    dve.wait_ge(hlo_done, c * FM + m)
                    V.tensor_tensor(h_sb[0:rows, :], sil[0:rows, :], up, ALU.mult).then_inc(glu_done, 1)
                    dve.wait_ge(hhi_done, c * FM + m + 1)
                    V.tensor_tensor(h_lo[0:rows, m, :], h_sb[0:rows, :], h_hi[0:rows, m, :].bitcast(F32),
                                    ALU.subtract).then_inc(hlo_done, 1)

                glu(0)
                glu(1)
                glu(2)
                if nxt:
                    ln_inverse(c + 1)
                    ln_scale(c + 1)
                dve.wait_ge(pos_psum, c + 1)
                V.tensor_tensor(pos[:], smp[:, 0:NT * E].rearrange("p (t e) -> p t e", e=E),
                                cnt[:].unsqueeze(1).to_broadcast([P, NT, E]), ALU.add).then_inc(pos_read, 1)
                dve.wait_ge(pos_read, 2 * c + 1)
                V.tensor_tensor(cnt[:], cnt[:], smp[:, NT * E:(NT + 1) * E], ALU.add).then_inc(pos_read, 1)
                V.tensor_scalar(ovf[:], pos[:], float(CAP), NOSLOT, ALU.is_ge, ALU.mult)
                link(V.tensor_tensor(slt[:], pos[:], slot_e.unsqueeze(1).to_broadcast([P, NT, E]), ALU.add), c)
                link(V.tensor_tensor(slt[:], slt[:], ovf[:], ALU.add), c)
                glu(3)
                link(V.tensor_tensor(ohs[:], oh[:], slt[:].unsqueeze(2).to_broadcast([P, NT, TOPK, E]),
                                     ALU.mult), c)
                link(V.tensor_reduce(slk[:], ohs[:], AX.X, ALU.add), c)
                dve.wait_ge(tab_out, c * (16 * NT * TOPK))
                V.tensor_copy(slot[:], slk[:])
                V.tensor_copy(pay[:, :, :, 0], tokf[:].unsqueeze(2).to_broadcast([P, NT, TOPK]))
                link(V.tensor_scalar(pay[:, :, :, 1].bitcast(F32), v8[:, :, 0:TOPK], ROUTE_SCALE, None,
                                     ALU.mult), c)
                V.tensor_scalar(tokf[:], tokf[:], float(CH), None, ALU.add).then_inc(slots_done, 1)
                glu(4)
                glu(5)
                if nxt:
                    xlo(c + 1)
                dve.wait_ge(xr_in, c * 16 + 16)
                for i in range(NT):
                    dve.wait_ge(y_done, c * NT + i + 1)
                    V.tensor_tensor(y_sb[:, i, :], yp[:, i % 2, :], y_sb[:, i, :], ALU.add).then_inc(ysb_done, 1)
                if nxt:
                    assert count[0] == N_CHAIN, count

            with dve.Fori(0, NC - 1) as c:
                body(c, True)
            body(NC - 1, False)

        @block.tensor
        def _(pe):
            M = nc.tensor.matmul

            def transposes(c):
                pe.wait_ge(ln_done, c * NT + NT)
                for k in range(KC):
                    if not isinstance(c, int) or c * KC + k >= 2:
                        pe.wait_ge(xlo_done, c * KC + k - 1)
                    for i in range(NT):
                        last = nc.tensor.transpose(xtp[:, k % 2, i * P:(i + 1) * P],
                                                   xn[:, i, k * P:(k + 1) * P], ident[:])
                    last.then_inc(xt_done, 1)

            def product(c, i, col, width):
                n = 0
                for k in range(KC):
                    for w, x in ((w_hi, x_hi), (w_hi, x_lo), (w_lo, x_hi)):
                        last = M(acc[0:width, i % ACCB, :], w[:, k, col:col + width], x[:, k, :],
                                 start=(n == 0), stop=(n == 3 * KC - 1))
                        n += 1
                last.then_inc(acc_done, 1)

            def released(c, i):
                j = i - ACCB
                if j < 0:
                    pe.wait_ge(glu_done, c * FM + (j + NACC - FIRST_F) // 2 + 1)
                elif j <= NKV:
                    pe.wait_ge(qlo_done, c * (NKV + 1) + j + 1)
                elif j == NKV + 1:
                    pe.wait_ge(v_done, c + 1)
                elif j == NKV + 2:
                    pe.wait_ge(l_done, c + 1)
                else:
                    pe.wait_ge(glu_done, c * FM + (j - FIRST_F) // 2 + 1 + FM)

            def body(c, nxt):
                pe.wait_ge(xlo_done, c * KC + KC)
                cols = [C_Q + g * P for g in range(NKV)] + [C_K, C_V]
                for i, col in enumerate(cols):
                    released(c, i)
                    product(c, i, col, P)
                released(c, NKV + 2)
                product(c, NKV + 2, C_G, E)
                pe.wait_ge(v_done, c + 1)
                pe.wait_ge(pos_read, 2 * c)
                for i in range(NT):
                    last = nc.tensor.transpose(smp[:, i * P:(i + 1) * P], v_f[:, i * P:(i + 1) * P], ident[:])
                last.then_inc(vt_psum, 1)
                pe.wait_ge(l_done, c + 1)
                pe.wait_ge(vt_done, c + 1)
                pe.sem_inc(pe_pass, 1)
                for i in range(NT):
                    last = nc.tensor.transpose(smp[:, i * E:(i + 1) * E], l_f[:, i * P:(i + 1) * P],
                                               ident[0:E, 0:E])
                last.then_inc(lt_psum, 1)
                for n in range(2 * FM - 1):
                    if n == 6:
                        pe.wait_ge(mask_done, c + 1)
                        pe.wait_ge(lt_read, c + 1)
                        for i in range(NT):
                            for j in range(i + 1):
                                M(smp[:, i * E:(i + 1) * E], before[:] if j == i else ones[:], mask[:, j, :],
                                  start=(j == 0), stop=(j == i))
                        for j in range(NT):
                            last = M(smp[:, NT * E:(NT + 1) * E], ones[:], mask[:, j, :],
                                     start=(j == 0), stop=(j == NT - 1))
                        last.then_inc(pos_psum, 1)
                    released(c, FIRST_F + n)
                    product(c, FIRST_F + n, C_GU + n * P, P)
                if nxt:
                    transposes(c + 1)
                pe.wait_ge(hlo_done, c * FM + FM)
                for i in range(NT):
                    pe.wait_ge(ysb_done, c * NT + i + 1)
                    n = 0
                    for m in range(FM):
                        for h, w in ((h_hi, d_hi), (h_lo, d_hi), (h_hi, d_lo)):
                            last = M(yp[:, i % 2, :], h[:, m, i * P:(i + 1) * P], w[:, m, :],
                                     start=(n == 0), stop=(n == 3 * FM - 1))
                            n += 1
                    last.then_inc(y_done, 1)

            pe.wait_ge(cst_in, 48)
            transposes(0)
            pe.wait_ge(w_lo_done, NPC)
            pe.wait_ge(init_v, 9)
            with pe.Fori(0, NC - 1) as c:
                body(c, True)
            body(NC - 1, False)


def stage_m(nc, t):
    ctx = ExitStack()
    with ctx:
        def sb(name, shape, dt=F32):
            return ctx.enter_context(nc.sbuf_tensor(name, shape, dt))

        def ps(name, shape):
            return ctx.enter_context(nc.psum_tensor(name, shape, F32))

        def sem(name):
            return ctx.enter_context(nc.semaphore(name))

        def two(name, shape, dt=F32):
            return [sb(f"{name}{p}", shape, dt) for p in range(2)]

        wgu = two("wgu", [P, KC, 2 * I])
        wdn = two("wdn", [P, IC, D])
        ids = two("ids", [CAP, 2], U32)
        xb = two("xb", [CAP, D])
        xbt = two("xbt", [P, KC, CAP])
        sil = two("silu", [CAP, I])
        hid = two("hid", [CAP, I])
        hidt = two("hidt", [P, IC, CAP])
        ysb = two("ysb", [CAP, D])
        ident = sb("ident_m", [P, P])
        gps = [ps(f"gps{p}", [P, 512]) for p in range(2)]
        ups = [ps(f"ups{p}", [P, 512]) for p in range(2)]
        yps = [ps(f"yps{p}", [P, 512]) for p in range(2)]
        xtps = ps("xtps", [P, 512])
        htps = ps("htps", [P, 512])

        id_in = sem("id_in")
        w_in = [sem("wgu_in0"), sem("wgu_in1")]
        tok_in = [sem("tok_in0"), sem("tok_in1")]
        x_in = sem("xb_in")
        y_out = sem("yadd_out")
        xt_done = sem("xbt_psum")
        xt_read = sem("xbt_done")
        gu_done = sem("gu_done")
        sil_done = sem("esil_done")
        hid_done = sem("hid_done")
        ht_done = sem("ht_psum")
        ht_read = sem("ht_done")
        dn_done = sem("dn_done")
        y_done = sem("ey_done")
        sp_pass, pool_pass = sem("sp_pass_m"), sem("pool_pass_m")

        block = ctx.enter_context(nc.Block())

        def expert(ap, e):
            return ap[e] if isinstance(e, int) else ap[ds(e, 1)].rearrange("o a b -> (o a) b")

        def load(sp, e, p):
            sp.dma_start(ids[p][:], expert(t["tab"].rearrange("(e s) w -> e s w", s=CAP), e)).then_inc(tok_in[p], 16)
            sp.dma_start(wgu[p][:], expert(t["e_gu"], e).rearrange("(k p) n -> p k n", p=P)).then_inc(w_in[p], 16)
            w = expert(t["e_d"], e)
            sp.dma_start(wdn[p][:, 0:IC - 1, :], w[0:(IC - 1) * P, :].rearrange("(k p) n -> p k n", p=P)).then_inc(w_in[p], 16)
            sp.dma_start(wdn[p][0:IT, IC - 1, :], w[(IC - 1) * P:I, :]).then_inc(w_in[p], 16)

        @block.sync
        def _(sp):
            sp.dma_start(ident[:], t["ident"]).then_inc(id_in, 16)
            load(sp, 0, 0)
            load(sp, 1, 1)
            with sp.Fori(0, E // 2 - 1) as i:
                for p in range(2):
                    sp.wait_ge(dn_done, 2 * i + p + 1)
                    sp.sem_inc(sp_pass, 1)
                    sp.wait_ge(y_out, 32 * i + 16 * p + 16)
                    sp.sem_inc(sp_pass, 1)
                    load(sp, 2 * i + p + 2, p)

        @block.gpsimd
        def _(pool):
            def gather(i, p):
                pool.wait_ge(tok_in[p], 16 * i + 16)
                pool.sem_inc(pool_pass, 1)
                pool.wait_ge(xt_done, 2 * i + p)
                pool.sem_inc(pool_pass, 1)
                nc.gpsimd.indirect_dma_start(xb[p][:], None, t["xn"],
                                             bass.IndirectOffsetOnAxis(ap=ids[p][:, 0:1], axis=0),
                                             bounds_check=T + CAP - 1, oob_is_err=True).then_inc(x_in, 16)

            def scatter(i, p):
                pool.wait_ge(y_done, 2 * i + p + 1)
                pool.sem_inc(pool_pass, 1)
                if not (isinstance(i, int) and i == 0 and p == 0):
                    pool.wait_ge(y_out, 32 * i + 16 * p)
                    pool.sem_inc(pool_pass, 1)
                nc.gpsimd.indirect_dma_start(t["base"], bass.IndirectOffsetOnAxis(ap=ids[p][:, 0:1], axis=0),
                                             ysb[p][:], None, bounds_check=T + CAP - 1, oob_is_err=True,
                                             compute_op=ALU.add).then_inc(y_out, 16)

            gather(0, 0)

            def body(i, nxt):
                gather(i, 1)
                scatter(i, 0)
                if nxt:
                    gather(i + 1, 0)
                scatter(i, 1)

            with pool.Fori(0, E // 2 - 1) as i:
                body(i, True)
            body(E // 2 - 1, False)
            pool.wait_ge(y_out, 16 * E)

        @block.scalar
        def _(act):
            def rows(n, p):
                act.wait_ge(xt_done, n + 1)
                nc.scalar.activation(xbt[p][:].rearrange("p k s -> p (k s)"), xtps[:, 0:KC * CAP],
                                     ACT.Copy).then_inc(xt_read, 1)

            rows(0, 0)

            def body(i, nxt):
                for p in range(2):
                    n = 2 * i + p
                    act.wait_ge(gu_done, n + 1)
                    nc.scalar.activation(sil[p][:], gps[p][0:CAP, 0:I], ACT.Silu).then_inc(sil_done, 1)
                    if p == 0 or nxt:
                        rows(n + 1, 1 - p)
                    act.wait_ge(ht_done, n + 1)
                    nc.scalar.activation(hidt[p][:, 0:IC - 1, :].rearrange("p k s -> p (k s)"),
                                         htps[:, 0:(IC - 1) * CAP], ACT.Copy)
                    nc.scalar.activation(hidt[p][0:IT, IC - 1, :], htps[0:IT, (IC - 1) * CAP:IC * CAP],
                                         ACT.Copy).then_inc(ht_read, 1)

            with act.Fori(0, E // 2 - 1) as i:
                body(i, True)
            body(E // 2 - 1, False)

        @block.vector
        def _(dve):
            with dve.Fori(0, E // 2) as i:
                for p in range(2):
                    n = 2 * i + p
                    dve.wait_ge(sil_done, n + 1)
                    nc.vector.tensor_tensor(hid[p][:], sil[p][:], ups[p][0:CAP, 0:I], ALU.mult).then_inc(hid_done, 1)
                    dve.wait_ge(dn_done, n + 1)
                    nc.vector.tensor_scalar(ysb[p][:], yps[p][0:CAP, :], ids[p][:, 1:2].bitcast(F32), None,
                                            ALU.mult).then_inc(y_done, 1)

        @block.tensor
        def _(pe):
            M, TR = nc.tensor.matmul, nc.tensor.transpose

            def rows(n, p):
                pe.wait_ge(x_in, 16 * n + 16)
                for k in range(KC):
                    last = TR(xtps[:, k * CAP:(k + 1) * CAP], xb[p][:, k * P:(k + 1) * P], ident[0:CAP, 0:CAP])
                last.then_inc(xt_done, 1)

            def body(i, nxt):
                for p in range(2):
                    n = 2 * i + p
                    pe.wait_ge(w_in[p], 48 * i + 48)
                    pe.wait_ge(xt_read, n + 1)
                    if not (isinstance(i, int) and i == 0):
                        pe.wait_ge(hid_done, 2 * i + p - 1 if p else 2 * i)
                    for a, bank in ((0, gps[p]), (I, ups[p])):
                        for k in range(KC):
                            last = M(bank[0:CAP, 0:I], xbt[p][:, k, :], wgu[p][:, k, a:a + I],
                                     start=(k == 0), stop=(k == KC - 1))
                    last.then_inc(gu_done, 1)
                    if p == 0 or nxt:
                        rows(n + 1, 1 - p)
                    pe.wait_ge(hid_done, n + 1)
                    for k in range(IC):
                        w = P if k < IC - 1 else IT
                        last = TR(htps[0:w, k * CAP:(k + 1) * CAP], hid[p][:, k * P:k * P + w],
                                  ident[0:CAP, 0:CAP])
                    last.then_inc(ht_done, 1)
                    pe.wait_ge(ht_read, n + 1)
                    for k in range(IC):
                        w = P if k < IC - 1 else IT
                        last = M(yps[p][0:CAP, :], hidt[p][0:w, k, :], wdn[p][0:w, k, :],
                                 start=(k == 0), stop=(k == IC - 1))
                    last.then_inc(dn_done, 1)

            pe.wait_ge(id_in, 16)
            rows(0, 0)
            with pe.Fori(0, E // 2 - 1) as i:
                body(i, True)
            body(E // 2 - 1, False)


def stage_b(nc, t):
    ctx = ExitStack()
    with ctx:
        def sb(name, shape, dt=F32):
            return ctx.enter_context(nc.sbuf_tensor(name, shape, dt))

        def ps(name, shape):
            return ctx.enter_context(nc.psum_tensor(name, shape, F32))

        def sem(name):
            return ctx.enter_context(nc.semaphore(name))

        def two(name, shape, dt=F32):
            return [sb(f"{name}{p}", shape, dt) for p in range(2)]

        LAG = 2
        RP = 16
        R3 = 3 * HD
        qst = two("qst", [P, GROUP, S], F32R)
        kst = two("kst", [P, S], F32R)
        vst = two("vst", [P, NKT, HD])
        prb = sb("prb", [P, RP, 2, CH])
        psum2 = [two(f"psum2{g}", [P, 2, CH]) for g in range(2)]
        mx = sb("mx", [P, GROUP * NKT, JC])
        neg = sb("neg", [P, GROUP * NKT])
        negt = sb("negt", [GROUP * NKT, P], F32R)
        den = sb("den", [P, CH])
        num = sb("num", [P, CH])
        rden = sb("rden", [P, CH])
        att = two("att", [P, CH])
        ident = sb("ident_b", [P, P])
        lowf = sb("lowf", [P, P])
        identb = sb("identb", [P, P], BF16)
        cmask = sb("cmask", [P, P], BF16)
        ones = sb("ones_b", [P, HD])
        R = 3
        sps = ps("sps", [P, R, CH])
        mps = ps("mps", [P, R, CH])
        ops = ps("ops", [P, CH])
        dps = ps("dps", [P, CH])

        cst_in = sem("cst_b")
        init_v = sem("init_b")
        qk_in = [[sem(f"qk_in{p}{c}") for c in range(JC)] for p in range(2)]
        v_in = [sem("v_in0"), sem("v_in1")]
        c_in = sem("c_in")
        att_out = sem("att_out")
        s_done = sem("s_done")
        exp_done = sem("exp_done")
        sel_done = sem("sel_done")
        pv_done = sem("pv_done")
        add_done = sem("add_done")
        ones_done = sem("ones_done")
        m_done = sem("m_done")
        mred_done = sem("mred_done")
        c_done = sem("c_done")
        den_done = sem("den_done")
        rden_done = sem("rden_done")
        att_done = sem("att_done")
        pe_pass, sp_pass, pool_pass = (sem(f"{e}_pass_b") for e in ("pe", "sp", "pool"))

        steps = [(j, kt, kt - JC * j) for j in range(JC) for kt in range(JC * (j + 1))]
        NK = len(steps)
        NU = GROUP * NK
        steps = [(j, kt, r if r >= 0 else -1) for j, kt, r in steps]
        full = [n for n, (j, kt, r) in enumerate(steps) if r < 0 and kt % 2 == 0]
        NGR = len(full)
        diag = [n for n, (j, kt, r) in enumerate(steps) if r >= 0]
        lasts = [n for n, (j, kt, r) in enumerate(steps) if r == 3]

        pieces = []
        for qt in range(NKT):
            for h in range(GROUP):
                n = (qt + 1) * P
                for j in range((n + CH - 1) // CH):
                    k0, w = j * CH, min(CH, n - j * CH)
                    if w == P and j:
                        k0, w = k0 - P, 2 * P
                    d = n - P - k0
                    pieces.append((h, qt, j, k0, max(w, 2 * P), w, d if n - k0 == w else None))
        NM = len(pieces)
        MI = NM + 1
        M1 = 36

        def quota(k):
            return range(min(k, M1) * NM // M1, min(k + 1, M1) * NM // M1)

        MFIN = M1

        block = ctx.enter_context(nc.Block())

        @block.sync
        def _(sp):
            def load_qk(i, p, c):
                b = i // 2
                g = 2 * (i % 2) + p
                cols = slice(c * CH, (c + 1) * CH)
                if isinstance(i, int):
                    qh, ql = t["q_hi"][b, g], t["q_lo"][b, g]
                    kh, kl = (t[n][b, 0, g * HD:(g + 1) * HD, :] for n in ("k_hi", "k_lo"))
                else:
                    qh, ql = (t[n][ds(b, 1), ds(g, 1)].rearrange("o u p s -> (o u p) s") for n in ("q_hi", "q_lo"))
                    kh, kl = (t[n][ds(b, 1), :, ds(g * HD, HD), :].rearrange("o u p s -> (o u p) s") for n in ("k_hi", "k_lo"))
                for r, src in enumerate((qh, qh, ql)):
                    sp.dma_start(qst[p][r * HD:(r + 1) * HD, :, cols].bitcast(F32),
                                 src[:, cols].rearrange("(h d) s -> d h s", d=HD)).then_inc(qk_in[p][c], 16)
                for r, src in enumerate((kh, kl, kh)):
                    sp.dma_start(kst[p][r * HD:(r + 1) * HD, cols].bitcast(F32), src[:, cols]).then_inc(qk_in[p][c], 16)

            def load_v(i, p):
                b = i // 2
                g = 2 * (i % 2) + p
                v = t["v"].rearrange("(b k p) (g d) -> b g p k d", p=P, k=NKT, d=HD)
                v = v[b, g] if isinstance(i, int) else v[ds(b, 1), ds(g, 1)].rearrange("o u p k d -> (o u p) k d")
                sp.dma_start(vst[p][:], v).then_inc(v_in[p], 16)

            def store(i, p, j):
                b = i // 2
                g = 2 * (i % 2) + p
                a = t["att"]
                a = a[b, g] if isinstance(i, int) else a[ds(b, 1), ds(g, 1)].rearrange("o u p s -> (o u p) s")
                bg = 2 * i + p
                sp.wait_ge(att_done, bg * JC + j + 2)
                sp.sem_inc(sp_pass, 1)
                sp.dma_start(a[:, j * CH:(j + 1) * CH], att[j % 2][:]).then_inc(att_out, 16)
                sp.wait_ge(att_out, 16 * (bg * JC + j + 2))
                sp.sem_inc(sp_pass, 1)

            sp.sem_inc(att_out, 16)
            sp.dma_start(ident[:], t["ident"]).then_inc(cst_in, 16)
            sp.dma_start(lowf[:], t["cmask"]).then_inc(cst_in, 16)
            for p in range(2):
                for c in range(JC):
                    load_qk(0, p, c)
                load_v(0, p)
            with sp.Fori(0, BG // 2 - 1) as i:
                for p in range(2):
                    for j in range(JC - 1):
                        store(i, p, j)
                    for c in range(JC):
                        sp.wait_ge(s_done, (2 * i + p) * NU + GROUP * (lasts[-2] + 1 + NT * (c + 1)))
                        sp.sem_inc(sp_pass, 1)
                        load_qk(i + 1, p, c)
                    sp.wait_ge(pv_done, (2 * i + p) * NK + NK + 8)
                    sp.sem_inc(sp_pass, 1)
                    load_v(i + 1, p)
                    store(i, p, JC - 1)
            for p in range(2):
                for j in range(JC):
                    store(BG // 2 - 1, p, j)

        @block.gpsimd
        def _(pool):
            def normalize(bg, j):
                pool.wait_ge(rden_done, NT * (bg * JC + j + 1))
                pool.sem_inc(pool_pass, 1)
                pool.wait_ge(att_out, 16 * (bg * JC + j))
                pool.sem_inc(pool_pass, 1)
                nc.gpsimd.tensor_tensor(att[j % 2][:], num[:], rden[:], ALU.mult).then_inc(att_done, 1)

            def group(bg, prev):
                for k in range(NK):
                    if k - LAG - NT - 1 in lasts:
                        normalize(bg, lasts.index(k - LAG - NT - 1))
                    if prev and k == LAG + NT:
                        normalize(bg - 1, JC - 1)
                    if steps[k][2] >= 0:
                        q0 = steps[k][2] * P
                        for pr in range(2):
                            pool.wait_ge(exp_done, bg * NU + GROUP * k + 2 * pr + 2 + R)
                            pool.sem_inc(pool_pass, 1)
                            blk = prb[:, (2 * k + pr) % RP, :, q0:q0 + P]
                            nc.gpsimd.affine_select(out=blk, in_=blk, compare_op=ALU.is_ge, fill=0.0, base=0,
                                                    pattern=[[0, 2], [1, P]], channel_multiplier=-1).then_inc(sel_done, 1)
                    for gi, f in enumerate(full):
                        G = bg * NGR + gi
                        if k in (f + 2, f + 3):
                            pr = k - f - 2
                            pool.wait_ge(exp_done, bg * NU + GROUP * (f + 1) + 2 * pr + 2 + R)
                            pool.sem_inc(pool_pass, 1)
                            pool.wait_ge(ones_done, 2 * G + pr + 1)
                            pool.sem_inc(pool_pass, 1)
                            nc.gpsimd.tensor_tensor(psum2[gi % 2][pr][:], prb[:, (2 * f + pr) % RP],
                                                    prb[:, (2 * (f + 1) + pr) % RP], ALU.add).then_inc(add_done, 1)

            pool.sem_inc(att_done, 1)
            group(0, False)
            with pool.Fori(0, BG // 2 - 1) as i:
                group(2 * i + 1, True)
                group(2 * i + 2, True)
            group(BG - 1, True)
            normalize(BG - 1, JC - 1)

        @block.scalar
        def _(act):
            act.sem_inc(exp_done, R)
            act.sem_inc(den_done, 1)
            act.sem_inc(c_done, 1)
            act.sem_inc(c_in, 16)

            def maxima(bg, p):
                act.wait_ge(m_done, bg * MI + MI)
                act.wait_ge(c_in, 16 * bg + 16)
                nc.scalar.activation(negt[:], mps[0:GROUP * NKT, NM % R, 0:P], ACT.Copy).then_inc(c_done, 1)
                act.wait_ge(c_done, bg + 2)
                act.dma_start(qst[p][R3:R3 + 1, :, :].bitcast(F32), negt[:].bitcast(F32)).then_inc(c_in, 16)

            maxima(0, 0)

            def evacuate(bg, j):
                act.wait_ge(pv_done, bg * NK + lasts[j] + 1 + 8)
                act.wait_ge(att_done, bg * JC + j + 1)
                nc.scalar.activation(num[:], ops[:], ACT.Copy)
                nc.scalar.activation(den[:], dps[:], ACT.Copy).then_inc(den_done, 1)

            def group(bg, p, nxt, prev=True):
                for k, (j, kt, r) in enumerate(steps):
                    q0 = max(r, 0) * P
                    if nxt and k == MFIN + 2:
                        maxima(bg + 1, 1 - p)
                    if k - LAG - 1 in lasts:
                        evacuate(bg, lasts.index(k - LAG - 1))
                    if prev and k == LAG:
                        evacuate(bg - 1, JC - 1)
                    act.wait_ge(pv_done, bg * NK + k + 1)
                    kk = k - RP // 2
                    gi = [n for n, f in enumerate(full) if f <= kk % NK < f + 2]
                    if gi and (kk >= 0 or prev):
                        act.wait_ge(add_done, 2 * (bg * NGR + gi[0] - (NGR if kk < 0 else 0)) + 2)
                    for h in range(GROUP):
                        act.wait_ge(s_done, bg * NU + GROUP * k + h + 1)
                        nc.scalar.activation(prb[:, (2 * k + h // 2) % RP, h % 2, q0:CH],
                                             sps[:, (GROUP * k + h) % R, q0:CH], ACT.Exp, scale=SCALE).then_inc(exp_done, 1)
                if not nxt:
                    evacuate(bg, JC - 1)

            group(0, 0, True, prev=False)
            with act.Fori(0, BG // 2 - 1) as i:
                group(2 * i + 1, 1, True)
                group(2 * i + 2, 0, True)
            group(BG - 1, 1, False)

        @block.vector
        def _(dve):
            V = nc.vector
            V.memset(mx[:], -3.0e38).then_inc(init_v, 1)
            V.memset(ones[:], 1.0).then_inc(init_v, 1)
            for p in range(2):
                V.memset(kst[p][R3:R3 + 1, :].bitcast(F32), 1.0).then_inc(init_v, 1)
            dve.wait_ge(cst_in, 32)
            V.tensor_copy(identb[:], ident[:]).then_inc(init_v, 1)
            V.tensor_copy(cmask[:], lowf[:]).then_inc(init_v, 1)
            dve.wait_ge(init_v, 6)
            dve.sem_inc(mred_done, R)

            def reduce(bg, p, n):
                h, qt, j, k0, w, wr, d = pieces[n]
                dve.wait_ge(m_done, bg * MI + n + 1)
                V.tensor_reduce(mx[:, h * NKT + qt, j:j + 1], mps[:, n % R, 0:wr], AX.X,
                                ALU.max).then_inc(mred_done, 1)

            def negate(bg):
                dve.wait_ge(mred_done, bg * MI + NM + R)
                V.tensor_reduce(neg[:], mx[:], AX.X, ALU.max, negate=True).then_inc(mred_done, 1)

            for n in range(NM):
                reduce(0, 0, n)
            negate(0)

            def invert(bg, j, part):
                if part == 0:
                    dve.wait_ge(den_done, bg * JC + j + 2)
                    dve.wait_ge(att_done, bg * JC + j + 1)
                cols = slice(part * P, (part + 1) * P)
                V.reciprocal(rden[:, cols], den[:, cols]).then_inc(rden_done, 1)

            def group(bg, p, nxt, prev=True):
                for k in range(NK):
                    if nxt:
                        for n in quota(k):
                            reduce(bg + 1, 1 - p, n)
                        if k == MFIN:
                            negate(bg + 1)
                    for part in range(NT):
                        if k - LAG - 1 - part in lasts:
                            invert(bg, lasts.index(k - LAG - 1 - part), part)
                        if prev and k == LAG + part:
                            invert(bg - 1, JC - 1, part)
                if not nxt:
                    for part in range(NT):
                        invert(bg, JC - 1, part)

            group(0, 0, True, prev=False)
            with dve.Fori(0, BG // 2 - 1) as i:
                group(2 * i + 1, 1, True)
                group(2 * i + 2, 0, True)
            group(BG - 1, 1, False)

        @block.tensor
        def _(pe):
            M, TR = nc.tensor.matmul, nc.tensor.transpose

            def piece(bg, p, n):
                h, qt, j, k0, w, wr, d = pieces[n]
                if h == 0 and j == 0 and qt % NT == 0:
                    c = qt // NT
                    pe.wait_ge(qk_in[p][c], 96 * (bg // 2) + 96)
                if n < R and n % R == NM % R:
                    pe.wait_ge(c_done, bg + 1)
                elif n < R:
                    before = max(m for m in range(NM) if m % R == n)
                    pe.wait_ge(mred_done, bg * MI + before + 1 - MI + R)
                else:
                    pe.wait_ge(mred_done, bg * MI + n + 1)
                out = mps[:, n % R, :]
                last = M(out[:, 0:w], qst[p][0:R3, h, qt * P:(qt + 1) * P], kst[p][0:R3, k0:k0 + w],
                         start=True, stop=True)
                if d is not None:
                    last = M(out[:, d:d + P], identb[:], cmask[:], start=False, stop=True, skip_group_check=True)
                last.then_inc(m_done, 1)

            def turn(bg, p):
                pe.wait_ge(mred_done, bg * MI + MI + R)
                pe.sem_inc(pe_pass, 1)
                TR(mps[0:GROUP * NKT, NM % R, 0:P], neg[:], ident[:]).then_inc(m_done, 1)

            pe.wait_ge(init_v, 6)
            pe.sem_inc(pv_done, 8)
            pe.sem_inc(ones_done, 4)
            for n in range(NM):
                piece(0, 0, n)
            turn(0, 0)

            def scores(bg, p, k, h):
                j, kt, r = steps[k]
                q0 = min(max(r, 0) * P, CH - 2 * P)
                u = GROUP * k + h
                before = u - R if u >= R else max(m for m in range(NU) if m % R == u % R) - NU
                pe.wait_ge(exp_done, bg * NU + before + 1 + R)
                M(sps[:, u % R, q0:CH], kst[p][0:R3 + 1, kt * P:(kt + 1) * P],
                  qst[p][0:R3 + 1, h, j * CH + q0:(j + 1) * CH], start=True, stop=True).then_inc(s_done, 1)

            def output(bg, p, k):
                j, kt, r = steps[k]
                q0 = max(r, 0) * P
                pe.wait_ge(exp_done, bg * NU + GROUP * (k + 1) + R)
                if r >= 0:
                    pe.wait_ge(sel_done, bg * 2 * len(diag) + 2 * diag.index(k) + 2)
                if kt == 0:
                    pe.wait_ge(den_done, bg * JC + j + 1)
                for h in range(GROUP):
                    last = M(ops[HD * h:HD * (h + 1), q0:CH], vst[p][:, kt, :],
                             prb[:, (2 * k + h // 2) % RP, h % 2, q0:CH], start=(kt == 0), stop=(r == 3),
                             skip_group_check=True)
                if r >= 0:
                    for h in range(GROUP):
                        last = M(dps[HD * h:HD * (h + 1), q0:CH], ones[:],
                                 prb[:, (2 * k + h // 2) % RP, h % 2, q0:CH], start=(kt == 0),
                                 stop=(r == 3), skip_group_check=True)
                last.then_inc(pv_done, 1)

            def pair_sum(bg, gi):
                j, kt, _ = steps[full[gi]]
                if kt == 0:
                    pe.wait_ge(den_done, bg * JC + j + 1)
                for pr in range(2):
                    pe.wait_ge(add_done, 2 * (bg * NGR + gi) + pr + 1)
                    for hh in range(2):
                        h = 2 * pr + hh
                        last = M(dps[HD * h:HD * (h + 1), :], ones[:], psum2[gi % 2][pr][:, hh, :],
                                 start=(kt == 0), stop=False, skip_group_check=True)
                    last.then_inc(ones_done, 1)

            def group(bg, p, nxt, prev=True):
                for k in range(NK):
                    todo = list(quota(k)) if nxt else []
                    for h in range(GROUP):
                        scores(bg, p, k, h)
                        for n in todo[h:h + 1]:
                            piece(bg + 1, 1 - p, n)
                    for gi, f in enumerate(full):
                        if k == f + LAG + 3:
                            pair_sum(bg, gi)
                    if k >= LAG:
                        output(bg, p, k - LAG)
                    elif prev:
                        output(bg - 1, 1 - p, NK + k - LAG)
                    for n in todo[GROUP:]:
                        piece(bg + 1, 1 - p, n)
                    if nxt and k == MFIN:
                        turn(bg + 1, 1 - p)
                if not nxt:
                    for k in range(NK - LAG, NK):
                        output(bg, p, k)

            def ready(bg, p):
                pe.wait_ge(v_in[p], 16 * (bg // 2) + 16)
                pe.wait_ge(c_in, 16 * bg + 32)

            ready(0, 0)
            group(0, 0, True, prev=False)
            with pe.Fori(0, BG // 2 - 1) as i:
                for bg, p in ((2 * i + 1, 1), (2 * i + 2, 0)):
                    ready(bg, p)
                    group(bg, p, True)
            ready(BG - 1, 1)
            group(BG - 1, 1, False)


def stage_c(nc, t):
    ctx = ExitStack()
    with ctx:
        def sb(name, shape, dt=F32):
            return ctx.enter_context(nc.sbuf_tensor(name, shape, dt))

        def sem(name):
            return ctx.enter_context(nc.semaphore(name))

        def two(name, shape, dt=F32):
            return [sb(f"{name}{p}", shape, dt) for p in range(2)]

        wo = sb("wo", [P, KC, D])
        wo_hi = sb("wo_hi", [P, KC, D], F32R)
        wo_lo = sb("wo_lo", [P, KC, D], F32R)
        a_in = two("a_in", [P, KC, CH])
        a_hi = two("a_hi", [P, KC, CH], F32R)
        a_lo = two("a_lo", [P, KC, CH], F32R)
        y = two("y_c", [P, NT, D])
        ops = ctx.enter_context(nc.psum_tensor("cps", [P, 8, D], F32))
        w_in = sem("wo_in")
        w_hi = sem("wo_hi_done")
        w_lo = sem("wo_lo_done")
        a_ld = [sem("a_ld0"), sem("a_ld1")]
        y_ld = [sem("y_ld0"), sem("y_ld1")]
        hi_done = sem("a_hi_done")
        lo_done = sem("a_lo_done")
        o_done = sem("o_done")
        y_done = sem("yc_done")
        y_st = [sem("y_st0"), sem("y_st1")]
        sp_pass = sem("sp_pass_c")
        block = ctx.enter_context(nc.Block())

        def rows(ap, c):
            v = ap.rearrange("(c t p) d -> c p t d", p=P, t=NT)
            return v[c] if isinstance(c, int) else v[ds(c, 1)].rearrange("o p t d -> (o p) t d")

        def load(sp, c, p):
            a = t["att"]
            if isinstance(c, int):
                a = a[c // JC, :, :, (c % JC) * CH:(c % JC + 1) * CH].rearrange("g p s -> p g s")
            else:
                a = a[ds(c // JC, 1), :, :, ds((c % JC) * CH, CH)].rearrange("o g p s -> (o p) g s")
            sp.dma_start(a_in[p][:], a).then_inc(a_ld[p], 16)
            sp.dma_start(y[p][:], rows(t["base"][0:T, :], c)).then_inc(y_ld[p], 16)

        @block.sync
        def _(sp):
            sp.dma_start(wo[:], t["w_o"].rearrange("(k p) n -> p k n", p=P)).then_inc(w_in, 16)
            load(sp, 0, 0)
            load(sp, 1, 1)
            with sp.Fori(0, NC // 2 - 1) as i:
                for p in range(2):
                    sp.wait_ge(y_st[p], 16 * i + 16)
                    sp.sem_inc(sp_pass, 1)
                    load(sp, 2 * i + p + 2, p)

        @block.scalar
        def _(act):
            act.wait_ge(w_in, 16)
            nc.scalar.activation(wo_hi[:], wo[:], ACT.Copy).then_inc(w_hi, 1)
            with act.Fori(0, NC // 2) as i:
                for p in range(2):
                    c = 2 * i + p
                    act.wait_ge(a_ld[p], 16 * i + 16)
                    act.wait_ge(o_done, 2 * NT * i)
                    nc.scalar.activation(a_hi[p][:], a_in[p][:], ACT.Copy).then_inc(hi_done, 1)
                    act.wait_ge(y_done, c * NT + NT)
                    act.dma_start(rows(t["out"], c), y[p][:]).then_inc(y_st[p], 16)
            act.wait_ge(y_st[0], 16 * (NC // 2))
            act.wait_ge(y_st[1], 16 * (NC // 2))

        @block.vector
        def _(dve):
            V = nc.vector
            dve.wait_ge(w_hi, 1)
            V.tensor_tensor(wo_lo[:], wo[:], wo_hi[:].bitcast(F32), ALU.subtract).then_inc(w_lo, 1)
            with dve.Fori(0, NC // 2) as i:
                for p in range(2):
                    c = 2 * i + p
                    dve.wait_ge(hi_done, c + 1)
                    V.tensor_tensor(a_lo[p][:], a_in[p][:], a_hi[p][:].bitcast(F32), ALU.subtract).then_inc(lo_done, 1)
                    dve.wait_ge(y_ld[p], 16 * i + 16)
                    for n in range(NT):
                        dve.wait_ge(o_done, c * NT + n + 1)
                        V.tensor_tensor(y[p][:, n, :], ops[:, NT * p + n, :], y[p][:, n, :], ALU.add).then_inc(y_done, 1)

        @block.tensor
        def _(pe):
            pe.wait_ge(w_lo, 1)
            with pe.Fori(0, NC // 2) as i:
                for p in range(2):
                    c = 2 * i + p
                    pe.wait_ge(lo_done, c + 1)
                    for n in range(NT):
                        m = 0
                        for k in range(KC):
                            for a, w in ((a_hi, wo_hi), (a_lo, wo_hi), (a_hi, wo_lo)):
                                last = nc.tensor.matmul(ops[:, NT * p + n, :], a[p][:, k, n * P:(n + 1) * P],
                                                        w[:, k, :], start=(m == 0), stop=(m == 3 * KC - 1))
                                m += 1
                        last.then_inc(o_done, 1)


def host_constants(np):
    tri = np.tril(np.ones((NG, NG), np.float32), -1).reshape(-1)
    row = np.concatenate([np.arange(E), np.arange(E) * CAP, tri]).astype(np.float32)
    cst = np.concatenate([np.tile(row, (P, 1)), (np.arange(P)[:, None] + P * np.arange(NT)[None, :])], 1)
    cmask = np.triu(np.full((P, P), NEG, np.float32), 1)
    upper = np.triu(np.ones((P, P)), 1)
    return {"ident": np.eye(P, dtype=np.float32), "upper": upper.astype(np.float32), "cmask": cmask,
            "cst": np.ascontiguousarray(cst, dtype=np.float32)}


def host_layout(np, a):
    gu = a["L0_ffn_ws_gate_up"]
    cols = []
    for m in range(FM):
        w = min(P, ISH - m * P)
        cols += [gu[:, m * P:m * P + w], gu[:, ISH + m * P:ISH + m * P + w]]
    w_a = np.concatenate([a["L0_attn_Wq"], a["L0_attn_Wk"], a["L0_attn_Wv"], a["L0_ffn_gate_w"].T] + cols, 1)
    w_d = np.concatenate([a["L0_ffn_ws_down"], np.zeros((FM * P - ISH, D), np.float32)], 0)
    return {"x": np.ascontiguousarray(a["L0_attn_x"]).reshape(T, D), "w_a": np.ascontiguousarray(w_a),
            "w_d": np.ascontiguousarray(w_d), "w_o": np.ascontiguousarray(a["L0_attn_Wo"]),
            "e_gu": np.ascontiguousarray(a["L0_ffn_w_gate_up"]), "e_d": np.ascontiguousarray(a["L0_ffn_w_down"])}


def scratch(nc, out, dbg=()):
    def dram(name, shape, dt):
        return nc.dram_tensor(name, shape, dt, **({"kind": "ExternalOutput"} if name in dbg else {})).ap()
    return {"base": dram("base", [T + CAP, D], F32), "xn": dram("xn_s", [T + CAP, D], F32), "v": dram("v_s", [T, P], F32),
            "q_hi": dram("q_hi_s", [B, NKV, P, S], F32), "q_lo": dram("q_lo_s", [B, NKV, P, S], F32),
            "k_hi": dram("k_hi_s", [B, 1, P, S], F32), "k_lo": dram("k_lo_s", [B, 1, P, S], F32),
            "tab": dram("tab_s", [E * CAP, 2], U32), "att": dram("att_s", [B, NKV, P, S], F32)}


def kernel(**inputs):
    import numpy as _np
    import concourse.bacc as _bacc
    from concourse.bass_utils import run_bass_kernel_spmd as _run

    nc = _bacc.Bacc("TRN2", target_bir_lowering=False, num_devices=1)
    arrays, t = {}, {}
    for name, a in {**host_layout(_np, inputs), **host_constants(_np)}.items():
        arrays[f"in_{name}"] = a
        t[name] = nc.dram_tensor(f"in_{name}", a.shape, mybir.dt.from_np(a.dtype), kind="ExternalInput").ap()
    t["out"] = nc.dram_tensor("out", [T, D], F32, kind="ExternalOutput").ap()
    t.update(scratch(nc, None))
    stage_a(nc, t)
    stage_m(nc, t)
    stage_b(nc, t)
    stage_c(nc, t)
    r = _run(nc, [arrays], core_ids=[0])
    return r.results[0]["out"].reshape(B, S, D)
```

```python
from contextlib import ExitStack

import concourse.bass as bass
from concourse import mybir

ALU = mybir.AluOpType
ACT = mybir.ActivationFunctionType
AX = mybir.AxisListType
F32 = mybir.dt.float32
F32R = mybir.dt.float32r
BF16 = mybir.dt.bfloat16
U32 = mybir.dt.uint32
ds = bass.ds

P = 128
B, S, D = 4, 2048, 512
T = B * S
NH, NKV, HD = 16, 4, 32
GROUP = NH // NKV
KC = D // P
CH = 512
NT = CH // P
NC = T // CH
JC = S // CH
SCALE = HD ** -0.5
EPS = 1e-5

E, TOPK, NG, TG, CAP, I = 32, 6, 8, 3, 96, 352
GE = E // NG
ROUTE_SCALE = 16.0
ISH = 2 * I
FM = (ISH + P - 1) // P
FT = ISH - (FM - 1) * P
NOSLOT = 100000.0
IC = (I + P - 1) // P
IT = I - (IC - 1) * P
NKT = S // P
BG = B * NKV
NEG = -1.0e30

C_Q, C_K, C_V, C_G = 0, D, D + P, D + 2 * P
C_GU = C_G + E
WCOL = C_GU + 2 * ISH


def stage_a(nc, t, dbg=None):
    ctx = ExitStack()
    with ctx:
        def sb(name, shape, dt=F32):
            return ctx.enter_context(nc.sbuf_tensor(name, shape, dt))

        def ps(name, shape):
            return ctx.enter_context(nc.psum_tensor(name, shape, F32))

        def sem(name):
            return ctx.enter_context(nc.semaphore(name))

        w_hi = sb("w_hi", [P, KC, WCOL], F32R)
        w_lo = sb("w_lo", [P, KC, WCOL], F32R)
        d_hi = sb("d_hi", [P, FM, D], F32R)
        d_lo = sb("d_lo", [P, FM, D], F32R)
        ident = sb("ident", [P, P])
        uppf = sb("uppf", [P, P])
        before = sb("before", [P, P], BF16)
        ones = sb("ones", [P, P], BF16)
        cst = sb("cst", [P, 2 * E + NG * NG + NT])
        x_sb = sb("x_sb", [P, NT, D])
        xn = sb("xn", [P, NT, D])
        x_hi = sb("x_hi", [P, KC, CH], F32R)
        x_lo = sb("x_lo", [P, KC, CH], F32R)
        qk_hi = sb("qk_hi", [P, NKV + 1, CH], F32R)
        qk_lo = sb("qk_lo", [P, NKV + 1, CH], F32R)
        v_f = sb("v_f", [P, CH])
        v_t = sb("v_t", [P, NT, P])
        l_f = sb("l_f", [E, CH])
        sil = sb("sil", [P, CH])
        h_sb = sb("h_sb", [P, CH])
        up_t = sb("up_t", [FT, CH])
        h_hi = sb("h_hi", [P, FM, CH], F32R)
        h_lo = sb("h_lo", [P, FM, CH], F32R)
        y_sb = sb("y_sb", [P, NT, D])
        stats = sb("stats", [P, NT, 6])
        mv = sb("mv", [P, NT, 2])
        rstd = sb("rstd", [P, NT])
        var = sb("var", [P, NT])
        dev = sb("dev", [P, NT])
        nwt = sb("nwt", [P, NT])
        lg = sb("lg", [P, NT, E])
        gm = sb("gm", [P, NT, NG])
        gt = sb("gt", [P, NT, NG, NG])
        eq = sb("eq", [P, NT, NG, NG])
        rank = sb("rank", [P, NT, NG])
        keep = sb("keep", [P, NT, NG])
        sc = sb("sc", [P, NT, E])
        rmax = sb("rmax", [P, NT])
        shf = sb("shf", [P, NT, E])
        pe_ = sb("pexp", [P, NT, E])
        rs = sb("rs", [P, NT])
        rr = sb("rr", [P, NT])
        prob = sb("prob", [P, NT, E])
        v8 = sb("v8", [P, NT, 8])
        i8 = sb("i8", [P, NT, 8], U32)
        i8f = sb("i8f", [P, NT, 8])
        oh = sb("oh", [P, NT, TOPK, E])
        mask = sb("mask", [P, NT, E], BF16)
        cnt = sb("cnt", [P, E])
        pos = sb("pos", [P, NT, E])
        ovf = sb("ovf", [P, NT, E])
        slt = sb("slt", [P, NT, E])
        ohs = sb("ohs", [P, NT, TOPK, E])
        slk = sb("slk", [P, NT, TOPK])
        slot = sb("slot", [P, NT, TOPK], U32)
        tokf = sb("tokf", [P, NT])
        pay = sb("pay", [P, NT, TOPK, 2], U32)
        empty = sb("empty", [CAP, E, 2], U32)

        ACCB = 3
        acc = ps("acc", [P, ACCB, CH])
        xtp = ps("xtp", [P, 2, CH])
        yp = ps("yp", [P, 2, D])
        smp = ps("smp", [P, CH])

        cst_in = sem("cst_in")
        w_in = [sem(f"w_in{n}") for n in range(2 * NT)]
        w_hi_done = sem("w_hi_done")
        w_lo_done = sem("w_lo_done")
        init_v = sem("init_v")
        x_in = sem("x_in")
        xr_in = sem("xr_in")
        xn_out = sem("xn_out")
        qkv_out = sem("qkv_out")
        y_out = sem("y_out")
        tab_init = sem("tab_init")
        tab_out = sem("tab_out")
        acc_done = sem("acc_done")
        xt_done = sem("xt_done")
        vt_psum = sem("vt_psum")
        lt_psum = sem("lt_psum")
        pos_psum = sem("pos_psum")
        y_done = sem("y_done")
        qhi_done = sem("qhi_done")
        qlo_done = sem("qlo_done")
        v_done = sem("v_done")
        l_done = sem("l_done")
        vt_done = sem("vt_done")
        lt_read = sem("lt_read")
        pos_read = sem("pos_read")
        shf_done = sem("shf_done")
        pexp_done = sem("pexp_done")
        mask_done = sem("mask_done")
        slots_done = sem("slots_done")
        ln_done = sem("ln_done")
        x_free = sem("x_free")
        sil_done = sem("sil_done")
        glu_done = sem("glu_done")
        hhi_done = sem("hhi_done")
        hlo_done = sem("hlo_done")
        xhi_done = sem("xhi_done")
        xlo_done = sem("xlo_done")
        ysb_done = sem("ysb_done")
        upt_done = sem("upt_done")
        var_done = sem("var_done")
        dev_done = sem("dev_done")
        rstd_done = sem("rstd_done")
        dve_pass, pe_pass, sp_pass, pool_pass = (sem(f"{e}_pass_a") for e in ("dve", "pe", "sp", "pool"))
        chain = sem("chain")

        NACC = NKV + 3 + 2 * FM - 1
        FIRST_F = NKV + 3

        pieces = []
        for k in range(KC):
            step = -(-WCOL // -(-WCOL // CH))
            for a in range(0, WCOL, step):
                n = min(step, WCOL - a)
                pieces.append((t["w_a"][k * P:(k + 1) * P, a:a + n], w_hi[:, k, a:a + n], w_lo[:, k, a:a + n], n))
        for m in range(FM):
            pieces.append((t["w_d"][m * P:(m + 1) * P, :], d_hi[:, m, :], d_lo[:, m, :], D))
        NPC = len(pieces)
        stg = [y_sb[:, i, :] for i in range(NT)] + [v_f[:], sil[:], h_sb[:], v_t[:].rearrange("p t d -> p (t d)")]
        NST = len(stg)

        def staged(n):
            return stg[n % NST][:, 0:pieces[n][3]]

        iota_e = cst[:, 0:E]
        slot_e = cst[:, E:2 * E]
        tri = cst[:, 2 * E:2 * E + NG * NG].rearrange("p (a b) -> p a b", b=NG)
        tok0 = cst[:, 2 * E + NG * NG:]

        x_d = t["x"].rearrange("(c t p) d -> c p t d", p=P, t=NT)
        xn_d = t["xn"][0:T, :].rearrange("(c t p) d -> c p t d", p=P, t=NT)
        base_d = t["base"][0:T, :].rearrange("(c t p) d -> c p t d", p=P, t=NT)
        v_d = t["v"].rearrange("(c t p) d -> c p t d", p=P, t=NT)

        def chunk(ap, c):
            return ap[c] if isinstance(c, int) else ap[ds(c, 1)].rearrange("o p t d -> (o p) t d")

        def columns(ap4, c):
            if isinstance(c, int):
                return ap4[c // JC, :, :, (c % JC) * CH:(c % JC + 1) * CH].rearrange("g p s -> p g s")
            return ap4[ds(c // JC, 1), :, :, ds((c % JC) * CH, CH)].rearrange("o g p s -> (o p) g s")

        block = ctx.enter_context(nc.Block())

        @block.sync
        def _(sp):
            sp.dma_start(ident[:], t["ident"]).then_inc(cst_in, 16)
            sp.dma_start(uppf[:], t["upper"]).then_inc(cst_in, 16)
            sp.dma_start(cst[:], t["cst"]).then_inc(cst_in, 16)
            sp.dma_start(x_sb[:], chunk(x_d, 0)).then_inc(x_in, 16)
            sp.wait_ge(init_v, 9)
            sp.dma_start(t["xn"][T:T + CAP, :], xn[0:CAP, 0, :]).then_inc(tab_init, 16)
            sp.dma_start(t["base"][T:T + CAP, :], xn[0:CAP, 0, :]).then_inc(tab_init, 16)
            for n, (src, hi, lo, cols) in enumerate(pieces):
                if n >= NST:
                    sp.wait_ge(w_lo_done, n - NST + 1)
                sp.dma_start(staged(n), src).then_inc(w_in[n % NST], 16)
            sp.dma_start(t["tab"].rearrange("(e s) w -> s e w", s=CAP), empty[:]).then_inc(tab_init, 16)
            sp.wait_ge(ln_done, NT)
            sp.dma_start(chunk(xn_d, 0), xn[:]).then_inc(xn_out, 16)
            sp.dma_start(x_sb[:], chunk(x_d, 1)).then_inc(x_in, 16)

            def body(c, nxt, nxt2):
                sp.wait_ge(ysb_done, c * NT + 2)
                sp.sem_inc(sp_pass, 1)
                sp.dma_start(y_sb[:], chunk(x_d, c)).then_inc(xr_in, 16)
                sp.wait_ge(qlo_done, c * (NKV + 1) + NKV + 1)
                sp.sem_inc(sp_pass, 1)
                sp.wait_ge(qhi_done, c * (NKV + 1) + NKV + 1)
                sp.sem_inc(sp_pass, 1)
                sp.dma_start(columns(t["q_hi"], c), qk_hi[:, 0:NKV, :].bitcast(F32)).then_inc(qkv_out, 16)
                sp.dma_start(columns(t["q_lo"], c), qk_lo[:, 0:NKV, :].bitcast(F32)).then_inc(qkv_out, 16)
                sp.dma_start(columns(t["k_hi"], c), qk_hi[:, NKV:NKV + 1, :].bitcast(F32)).then_inc(qkv_out, 16)
                sp.dma_start(columns(t["k_lo"], c), qk_lo[:, NKV:NKV + 1, :].bitcast(F32)).then_inc(qkv_out, 16)
                sp.wait_ge(vt_done, c + 1)
                sp.sem_inc(sp_pass, 1)
                sp.dma_start(chunk(v_d, c), v_t[:]).then_inc(qkv_out, 16)
                if nxt:
                    sp.wait_ge(ln_done, c * NT + 2 * NT)
                    sp.sem_inc(sp_pass, 1)
                    sp.dma_start(chunk(xn_d, c + 1), xn[:]).then_inc(xn_out, 16)
                if nxt2:
                    sp.dma_start(x_sb[:], chunk(x_d, c + 2)).then_inc(x_in, 16)
                sp.wait_ge(ysb_done, c * NT + NT + 2)
                sp.sem_inc(sp_pass, 1)
                sp.dma_start(chunk(base_d, c), y_sb[:]).then_inc(y_out, 16)
                sp.wait_ge(y_out, c * 16 + 16)
                sp.sem_inc(sp_pass, 1)

            sp.wait_ge(w_lo_done, NPC)
            with sp.Fori(0, NC - 2) as c:
                body(c, True, True)
            body(NC - 2, True, False)
            body(NC - 1, False, False)
            sp.wait_ge(tab_init, 48)
            sp.wait_ge(xn_out, 16 * NC)
            sp.wait_ge(qkv_out, 80 * NC)
            sp.wait_ge(y_out, 16 * NC)

        @block.gpsimd
        def _(pool):
            pool.wait_ge(tab_init, 48)

            with pool.Fori(0, NC) as c:
                pool.wait_ge(slots_done, c + 1)
                pool.sem_inc(pool_pass, 1)
                for i in range(NT):
                    for k in range(TOPK):
                        nc.gpsimd.indirect_dma_start(
                            t["tab"], bass.IndirectOffsetOnAxis(ap=slot[:, i, k:k + 1], axis=0),
                            pay[:, i, k, :], None, bounds_check=E * CAP - 1, oob_is_err=False,
                        ).then_inc(tab_out, 16)
                pool.wait_ge(tab_out, c * (16 * NT * TOPK) + 16 * NT * TOPK)
                pool.sem_inc(pool_pass, 1)

            pool.wait_ge(tab_out, NC * (16 * NT * TOPK))

        @block.scalar
        def _(act):
            def deviation(c):
                act.wait_ge(var_done, 2 * c + 2)
                nc.scalar.activation(dev[:], var[:], ACT.Sqrt).then_inc(dev_done, 1)

            deviation(0)

            for n in range(NPC):
                act.wait_ge(w_in[n % NST], 16 * (n // NST + 1))
                nc.scalar.activation(pieces[n][1], staged(n), ACT.Copy).then_inc(w_hi_done, 1)

            def xhi(c):
                for k in range(KC):
                    act.wait_ge(xt_done, c * KC + k + 1)
                    nc.scalar.activation(x_hi[:, k, :], xtp[:, k % 2, :], ACT.Copy).then_inc(xhi_done, 1)

            def body(c, nxt):
                def high(i):
                    act.wait_ge(acc_done, c * NACC + i + 3)
                    nc.scalar.activation(qk_hi[:, i, :], acc[:, (i + 2) % ACCB, :], ACT.Copy).then_inc(qhi_done, 1)

                act.wait_ge(acc_done, c * NACC + 1)
                nc.scalar.activation(l_f[:], acc[0:E, 0, :], ACT.Copy).then_inc(l_done, 1)
                act.wait_ge(acc_done, c * NACC + 2)
                nc.scalar.activation(v_f[:], acc[:, 1, :], ACT.Copy).then_inc(v_done, 1)
                act.wait_ge(qkv_out, c * 80)
                high(0)
                high(1)
                act.wait_ge(vt_psum, c + 1)
                nc.scalar.activation(v_t[:].rearrange("p t d -> p (t d)"), smp[:], ACT.Copy).then_inc(vt_done, 1)
                high(2)
                act.wait_ge(shf_done, c + 1)
                nc.scalar.activation(pe_[:], shf[:], ACT.Exp).then_inc(pexp_done, 1)
                high(3)
                high(4)
                if nxt:
                    deviation(c + 1)
                for m in range(FM):
                    last = m == FM - 1
                    rows = FT if last else P
                    i = FIRST_F + 2 * m
                    act.wait_ge(acc_done, c * NACC + i + 1)
                    act.wait_ge(glu_done, c * FM + m + FM)
                    nc.scalar.activation(sil[0:rows, :], acc[0:rows, i % ACCB, :], ACT.Silu).then_inc(sil_done, 1)
                    act.wait_ge(glu_done, c * FM + m + 1 + FM)
                    nc.scalar.activation(h_hi[0:rows, m, :], h_sb[0:rows, :], ACT.Copy).then_inc(hhi_done, 1)
                if nxt:
                    act.wait_ge(acc_done, c * NACC + NACC)
                    xhi(c + 1)

            act.wait_ge(init_v, 1)
            xhi(0)
            with act.Fori(0, NC - 1) as c:
                body(c, True)
            body(NC - 1, False)

        @block.vector
        def _(dve):
            N_CHAIN = 20
            count = [0]

            def link(ins, c):
                count[0] += 1
                ins.then_inc(chain, 1)
                dve.wait_ge(chain, c * N_CHAIN + count[0])

            V = nc.vector
            V.memset(h_hi[:, FM - 1, :].bitcast(F32), 0.0).then_inc(init_v, 1)
            V.memset(h_lo[:, FM - 1, :].bitcast(F32), 0.0).then_inc(init_v, 1)
            V.memset(ones[:], 1.0).then_inc(init_v, 1)
            V.memset(cnt[:], 0.0).then_inc(init_v, 1)
            V.memset(empty[:], 0).then_inc(init_v, 1)
            V.memset(xn[:, 0, :], 0.0).then_inc(init_v, 1)
            dve.sem_inc(glu_done, FM)
            dve.sem_inc(ysb_done, 2)
            dve.wait_ge(cst_in, 48)
            V.tensor_copy(before[:], uppf[:]).then_inc(init_v, 1)
            V.tensor_copy(tokf[:], tok0).then_inc(init_v, 1)
            dve.wait_ge(init_v, 6)
            V.tensor_scalar(empty[:, :, 0], tok0[0:CAP, 0:1].to_broadcast([CAP, E]), float(T), None,
                            ALU.add).then_inc(init_v, 1)
            dve.wait_ge(init_v, 9)

            def ln_stats(c):
                dve.wait_ge(x_in, c * 16 + 16)
                for i in range(NT):
                    V.bn_stats(out=stats[:, i, :], in_=x_sb[:, i, :]).then_inc(x_free, 1)

            def ln_variance(c):
                dve.wait_ge(x_free, c * NT + NT)
                dve.sem_inc(dve_pass, 1)
                for i in range(NT):
                    last = V.bn_aggr(out=mv[:, i, :], in_=stats[:, i, :])
                last.then_inc(var_done, 1)
                dve.wait_ge(var_done, 2 * c + 1)
                V.tensor_scalar(var[:], mv[:, :, 1], EPS, None, ALU.add).then_inc(var_done, 1)

            def ln_inverse(c):
                dve.wait_ge(dev_done, c + 1)
                V.reciprocal(rstd[:], dev[:]).then_inc(rstd_done, 1)
                dve.wait_ge(rstd_done, c * 5 + 1)
                V.tensor_tensor(nwt[:], var[:], rstd[:], ALU.mult).then_inc(rstd_done, 1)
                dve.wait_ge(rstd_done, c * 5 + 2)
                V.tensor_tensor(nwt[:], nwt[:], rstd[:], ALU.mult).then_inc(rstd_done, 1)
                dve.wait_ge(rstd_done, c * 5 + 3)
                V.tensor_scalar(nwt[:], nwt[:], -0.5, 1.5, ALU.mult, ALU.add).then_inc(rstd_done, 1)
                dve.wait_ge(rstd_done, c * 5 + 4)
                V.tensor_tensor(rstd[:], rstd[:], nwt[:], ALU.mult).then_inc(rstd_done, 1)

            def ln_scale(c):
                dve.wait_ge(rstd_done, c * 5 + 5)
                dve.wait_ge(tab_init, 32)
                dve.wait_ge(xn_out, c * 16)
                dve.wait_ge(xt_done, c * KC)
                for i in range(NT):
                    V.tensor_scalar(xn[:, i, :], x_sb[:, i, :], mv[:, i, 0:1], rstd[:, i:i + 1],
                                    ALU.subtract, ALU.mult).then_inc(ln_done, 1)

            def xlo(c, ks=range(KC)):
                for k in ks:
                    dve.wait_ge(xhi_done, c * KC + k + 1)
                    V.tensor_tensor(x_lo[:, k, :], xtp[:, k % 2, :], x_hi[:, k, :].bitcast(F32),
                                    ALU.subtract).then_inc(xlo_done, 1)

            ln_stats(0)
            ln_variance(0)
            ln_inverse(0)
            ln_scale(0)
            for n in range(NPC):
                dve.wait_ge(w_hi_done, n + 1)
                V.tensor_tensor(pieces[n][2], staged(n), pieces[n][1].bitcast(F32),
                                ALU.subtract).then_inc(w_lo_done, 1)
            xlo(0)

            def body(c, nxt):
                count[0] = 0

                def low(i):
                    dve.wait_ge(qhi_done, c * (NKV + 1) + i + 1)
                    V.tensor_tensor(qk_lo[:, i, :], acc[:, (i + 2) % ACCB, :], qk_hi[:, i, :].bitcast(F32),
                                    ALU.subtract).then_inc(qlo_done, 1)

                dve.wait_ge(lt_psum, c + 1)
                V.tensor_copy(lg[:].rearrange("p t e -> p (t e)"), smp[:, 0:NT * E]).then_inc(lt_read, 1)
                dve.wait_ge(lt_read, c + 1)
                link(V.tensor_reduce(gm[:].rearrange("p t g -> p (t g)"),
                                     lg[:].rearrange("p t (g e) -> p (t g) e", g=NG), AX.X, ALU.max), c)
                other = gm[:].unsqueeze(2).to_broadcast([P, NT, NG, NG])
                own = gm[:].unsqueeze(3).to_broadcast([P, NT, NG, NG])
                V.tensor_tensor(gt[:], other, own, ALU.is_gt)
                link(V.tensor_tensor(eq[:], other, own, ALU.is_equal), c)
                link(V.tensor_tensor(eq[:], eq[:], tri.unsqueeze(1).to_broadcast([P, NT, NG, NG]), ALU.mult), c)
                link(V.tensor_tensor(gt[:], gt[:], eq[:], ALU.add), c)
                link(V.tensor_reduce(rank[:].rearrange("p t g -> p (t g)"),
                                     gt[:].rearrange("p t a b -> p (t a) b"), AX.X, ALU.add), c)
                low(0)
                link(V.tensor_scalar(keep[:], rank[:], float(TG), None, ALU.is_lt), c)
                link(V.tensor_tensor(sc[:].rearrange("p t (g e) -> p t g e", g=NG),
                                     lg[:].rearrange("p t (g e) -> p t g e", g=NG),
                                     keep[:].unsqueeze(3).to_broadcast([P, NT, NG, GE]), ALU.mult), c)
                link(V.tensor_reduce(rmax[:], sc[:], AX.X, ALU.max), c)
                V.tensor_tensor(shf[:], sc[:], rmax[:].unsqueeze(2).to_broadcast([P, NT, E]),
                                ALU.subtract).then_inc(shf_done, 1)
                low(1)
                if nxt:
                    ln_stats(c + 1)
                    ln_variance(c + 1)
                low(2)
                dve.wait_ge(pexp_done, c + 1)
                link(V.tensor_reduce(rs[:], pe_[:], AX.X, ALU.add), c)
                link(V.reciprocal(rr[:], rs[:]), c)
                link(V.tensor_tensor(prob[:], pe_[:], rr[:].unsqueeze(2).to_broadcast([P, NT, E]), ALU.mult), c)
                dve.sem_inc(dve_pass, 1)
                for i in range(NT):
                    last = V.max(v8[:, i, :], prob[:, i, :])
                link(last, c)
                dve.sem_inc(dve_pass, 1)
                for i in range(NT):
                    last = V.max_index(i8[:, i, :], v8[:, i, :], prob[:, i, :])
                link(last, c)
                low(3)
                link(V.tensor_copy(i8f[:], i8[:]), c)
                link(V.tensor_tensor(oh[:], iota_e.unsqueeze(1).unsqueeze(1).to_broadcast([P, NT, TOPK, E]),
                                     i8f[:, :, 0:TOPK].unsqueeze(3).to_broadcast([P, NT, TOPK, E]),
                                     ALU.is_equal), c)
                with nc.allow_low_precision(reason="sums of zeros and at most one 1 are exact"):
                    V.tensor_reduce(mask[:], oh[:].rearrange("p t k e -> p t e k"), AX.X,
                                    ALU.add).then_inc(mask_done, 1)

                def glu(m):
                    last = m == FM - 1
                    rows = FT if last else P
                    i = FIRST_F + 2 * m
                    if last:
                        dve.wait_ge(acc_done, c * NACC + i + 1)
                        V.tensor_copy(up_t[:], acc[FT:2 * FT, i % ACCB, :]).then_inc(upt_done, 1)
                        dve.wait_ge(upt_done, c + 1)
                        up = up_t[:]
                    else:
                        dve.wait_ge(acc_done, c * NACC + i + 2)
                        up = acc[:, (i + 1) % ACCB, :]
                    dve.wait_ge(sil_done, c * FM + m + 1)
                    dve.wait_ge(hlo_done, c * FM + m)
                    V.tensor_tensor(h_sb[0:rows, :], sil[0:rows, :], up, ALU.mult).then_inc(glu_done, 1)
                    dve.wait_ge(hhi_done, c * FM + m + 1)
                    V.tensor_tensor(h_lo[0:rows, m, :], h_sb[0:rows, :], h_hi[0:rows, m, :].bitcast(F32),
                                    ALU.subtract).then_inc(hlo_done, 1)

                low(4)
                glu(0)
                glu(1)
                glu(2)
                if nxt:
                    ln_inverse(c + 1)
                    ln_scale(c + 1)
                dve.wait_ge(pos_psum, c + 1)
                V.tensor_tensor(pos[:], smp[:, 0:NT * E].rearrange("p (t e) -> p t e", e=E),
                                cnt[:].unsqueeze(1).to_broadcast([P, NT, E]), ALU.add).then_inc(pos_read, 1)
                dve.wait_ge(pos_read, 2 * c + 1)
                V.tensor_tensor(cnt[:], cnt[:], smp[:, NT * E:(NT + 1) * E], ALU.add).then_inc(pos_read, 1)
                V.tensor_scalar(ovf[:], pos[:], float(CAP), NOSLOT, ALU.is_ge, ALU.mult)
                link(V.tensor_tensor(slt[:], pos[:], slot_e.unsqueeze(1).to_broadcast([P, NT, E]), ALU.add), c)
                link(V.tensor_tensor(slt[:], slt[:], ovf[:], ALU.add), c)
                glu(3)
                link(V.tensor_tensor(ohs[:], oh[:], slt[:].unsqueeze(2).to_broadcast([P, NT, TOPK, E]),
                                     ALU.mult), c)
                link(V.tensor_reduce(slk[:], ohs[:], AX.X, ALU.add), c)
                dve.wait_ge(tab_out, c * (16 * NT * TOPK))
                V.tensor_copy(slot[:], slk[:])
                V.tensor_copy(pay[:, :, :, 0], tokf[:].unsqueeze(2).to_broadcast([P, NT, TOPK]))
                link(V.tensor_scalar(pay[:, :, :, 1].bitcast(F32), v8[:, :, 0:TOPK], ROUTE_SCALE, None,
                                     ALU.mult), c)
                V.tensor_scalar(tokf[:], tokf[:], float(CH), None, ALU.add).then_inc(slots_done, 1)
                glu(4)
                glu(5)
                if nxt:
                    xlo(c + 1, (0, 1))
                dve.wait_ge(xr_in, c * 16 + 16)
                for i in range(NT):
                    if nxt and i == 2:
                        xlo(c + 1, (2, 3))
                    dve.wait_ge(y_done, c * NT + i + 1)
                    V.tensor_tensor(y_sb[:, i, :], yp[:, i % 2, :], y_sb[:, i, :], ALU.add).then_inc(ysb_done, 1)
                if nxt:
                    assert count[0] == N_CHAIN, count

            with dve.Fori(0, NC - 1) as c:
                body(c, True)
            body(NC - 1, False)

        @block.tensor
        def _(pe):
            M = nc.tensor.matmul

            def transposes(c, ks=range(KC)):
                pe.wait_ge(ln_done, c * NT + NT)
                for k in ks:
                    if not isinstance(c, int) or c * KC + k >= 2:
                        pe.wait_ge(xlo_done, c * KC + k - 1)
                    for i in range(NT):
                        last = nc.tensor.transpose(xtp[:, k % 2, i * P:(i + 1) * P],
                                                   xn[:, i, k * P:(k + 1) * P], ident[:])
                    last.then_inc(xt_done, 1)

            def product(c, i, col, width):
                n = 0
                for k in range(KC):
                    for w, x in ((w_hi, x_hi), (w_hi, x_lo), (w_lo, x_hi)):
                        last = M(acc[0:width, i % ACCB, :], w[:, k, col:col + width], x[:, k, :],
                                 start=(n == 0), stop=(n == 3 * KC - 1))
                        n += 1
                last.then_inc(acc_done, 1)

            def released(c, i):
                j = i - ACCB
                if j < 0:
                    pe.wait_ge(glu_done, c * FM + (j + NACC - FIRST_F) // 2 + 1)
                elif j == 0:
                    pe.wait_ge(l_done, c + 1)
                elif j == 1:
                    pe.wait_ge(v_done, c + 1)
                elif j <= NKV + 2:
                    pe.wait_ge(qlo_done, c * (NKV + 1) + j - 1)
                else:
                    pe.wait_ge(glu_done, c * FM + (j - FIRST_F) // 2 + 1 + FM)

            def body(c, nxt):
                pe.wait_ge(xlo_done, c * KC + KC)
                for i, (col, width) in enumerate([(C_G, E), (C_V, P)] + [(C_Q + g * P, P) for g in range(NKV)] +
                                                 [(C_K, P)]):
                    released(c, i)
                    product(c, i, col, width)
                    if i == 1:
                        pe.wait_ge(l_done, c + 1)
                        pe.wait_ge(pos_read, 2 * c)
                        pe.sem_inc(pe_pass, 1)
                        for i in range(NT):
                            last = nc.tensor.transpose(smp[:, i * E:(i + 1) * E], l_f[:, i * P:(i + 1) * P],
                                                       ident[0:E, 0:E])
                        last.then_inc(lt_psum, 1)
                    elif i == 3:
                        pe.wait_ge(v_done, c + 1)
                        pe.wait_ge(lt_read, c + 1)
                        for i in range(NT):
                            last = nc.tensor.transpose(smp[:, i * P:(i + 1) * P], v_f[:, i * P:(i + 1) * P], ident[:])
                        last.then_inc(vt_psum, 1)
                for n in range(2 * FM - 1):
                    if n == 6:
                        pe.wait_ge(mask_done, c + 1)
                        pe.wait_ge(vt_done, c + 1)
                        for i in range(NT):
                            for j in range(i + 1):
                                M(smp[:, i * E:(i + 1) * E], before[:] if j == i else ones[:], mask[:, j, :],
                                  start=(j == 0), stop=(j == i))
                        for j in range(NT):
                            last = M(smp[:, NT * E:(NT + 1) * E], ones[:], mask[:, j, :],
                                     start=(j == 0), stop=(j == NT - 1))
                        last.then_inc(pos_psum, 1)
                    released(c, FIRST_F + n)
                    product(c, FIRST_F + n, C_GU + n * P, P)
                if nxt:
                    transposes(c + 1, (0, 1))
                pe.wait_ge(hlo_done, c * FM + FM - 1)
                for i in range(NT):
                    if nxt and i == 2:
                        transposes(c + 1, (2, 3))
                    pe.wait_ge(ysb_done, c * NT + i + 1)
                    n = 0
                    for m in range(FM):
                        if i == 0 and m == FM - 1:
                            pe.wait_ge(hlo_done, c * FM + FM)
                        for h, w in ((h_hi, d_hi), (h_lo, d_hi), (h_hi, d_lo)):
                            last = M(yp[:, i % 2, :], h[:, m, i * P:(i + 1) * P], w[:, m, :],
                                     start=(n == 0), stop=(n == 3 * FM - 1))
                            n += 1
                    last.then_inc(y_done, 1)

            pe.wait_ge(cst_in, 48)
            transposes(0)
            pe.wait_ge(w_lo_done, NPC)
            pe.wait_ge(init_v, 9)
            with pe.Fori(0, NC - 1) as c:
                body(c, True)
            body(NC - 1, False)


def stage_m(nc, t):
    ctx = ExitStack()
    with ctx:
        def sb(name, shape, dt=F32):
            return ctx.enter_context(nc.sbuf_tensor(name, shape, dt))

        def ps(name, shape):
            return ctx.enter_context(nc.psum_tensor(name, shape, F32))

        def sem(name):
            return ctx.enter_context(nc.semaphore(name))

        def two(name, shape, dt=F32):
            return [sb(f"{name}{p}", shape, dt) for p in range(2)]

        def four(name, shape, dt=F32):
            return [sb(f"{name}{q}", shape, dt) for q in range(4)]

        NQ = 4
        wgu = four("wgu", [P, KC, 2 * I])
        wdn = four("wdn", [P, IC, D])
        ids = four("ids", [CAP, 2], U32)
        xb = four("xb", [CAP, D])
        xbt = two("xbt", [P, KC, CAP])
        sil = two("silu", [CAP, I])
        hid = two("hid", [CAP, I])
        hidt = two("hidt", [P, IC, CAP])
        ysb = four("ysb", [CAP, D])
        ident = sb("ident_m", [P, P])
        gps = [ps(f"gps{p}", [P, 512]) for p in range(2)]
        ups = [ps(f"ups{p}", [P, 512]) for p in range(2)]
        yps = [ps(f"yps{p}", [P, 512]) for p in range(2)]
        xtps = ps("xtps", [P, 512])
        htps = ps("htps", [P, 512])

        id_in = sem("id_in")
        w_in = [sem(f"wgu_in{q}") for q in range(NQ)]
        tok_in = [sem(f"tok_in{q}") for q in range(NQ)]
        x_in = [sem(f"xb_in{q}") for q in range(NQ)]
        y_out = sem("yadd_out")
        xt_done = sem("xbt_psum")
        xt_read = sem("xbt_done")
        gu_done = sem("gu_done")
        sil_done = sem("esil_done")
        hid_done = sem("hid_done")
        ht_done = sem("ht_psum")
        ht_read = sem("ht_done")
        dn_done = sem("dn_done")
        y_done = sem("ey_done")
        sp_pass, pool_pass = sem("sp_pass_m"), sem("pool_pass_m")

        block = ctx.enter_context(nc.Block())

        def turns(engine, body):
            body(0)
            with engine.Fori(0, E // NQ - 2) as i:
                body(i + 1)
            body(E // NQ - 1)

        def first(i):
            return isinstance(i, int) and i == 0

        def final(i):
            return isinstance(i, int) and i > 0

        def expert(ap, e):
            return ap[e] if isinstance(e, int) else ap[ds(e, 1)].rearrange("o a b -> (o a) b")

        def load_table(sp, e, q):
            sp.dma_start(ids[q][:], expert(t["tab"].rearrange("(e s) w -> e s w", s=CAP), e)).then_inc(tok_in[q], 16)

        def load_weights(sp, e, q):
            sp.dma_start(wgu[q][:], expert(t["e_gu"], e).rearrange("(k p) n -> p k n", p=P)).then_inc(w_in[q], 16)
            w = expert(t["e_d"], e)
            sp.dma_start(wdn[q][:, 0:IC - 1, :], w[0:(IC - 1) * P, :].rearrange("(k p) n -> p k n", p=P)).then_inc(w_in[q], 16)
            sp.dma_start(wdn[q][0:IT, IC - 1, :], w[(IC - 1) * P:I, :]).then_inc(w_in[q], 16)

        @block.sync
        def _(sp):
            sp.dma_start(ident[:], t["ident"]).then_inc(id_in, 16)
            for q in range(NQ):
                load_table(sp, q, q)
            for q in range(NQ):
                load_weights(sp, q, q)
            with sp.Fori(0, E // NQ - 1) as i:
                for q in range(NQ):
                    n = NQ * i + q
                    sp.wait_ge(dn_done, n + 1)
                    sp.sem_inc(sp_pass, 1)
                    load_weights(sp, n + NQ, q)
                    sp.wait_ge(y_out, 16 * n + 16)
                    sp.sem_inc(sp_pass, 1)
                    load_table(sp, n + NQ, q)

        @block.gpsimd
        def _(pool):
            def gather(i, q):
                pool.wait_ge(tok_in[q], 16 * i + 16)
                pool.sem_inc(pool_pass, 1)
                if not first(i):
                    pool.wait_ge(xt_done, NQ * i + q - 3)
                    pool.sem_inc(pool_pass, 1)
                nc.gpsimd.indirect_dma_start(xb[q][:], None, t["xn"],
                                             bass.IndirectOffsetOnAxis(ap=ids[q][:, 0:1], axis=0),
                                             bounds_check=T + CAP - 1, oob_is_err=True).then_inc(x_in[q], 16)

            def scatter(n, q):
                pool.wait_ge(y_done, n + 1)
                pool.sem_inc(pool_pass, 1)
                if not first(n):
                    pool.wait_ge(y_out, 16 * n)
                    pool.sem_inc(pool_pass, 1)
                nc.gpsimd.indirect_dma_start(t["base"], bass.IndirectOffsetOnAxis(ap=ids[q][:, 0:1], axis=0),
                                             ysb[q][:], None, bounds_check=T + CAP - 1, oob_is_err=True,
                                             compute_op=ALU.add).then_inc(y_out, 16)

            def body(i):
                for q in range(NQ):
                    if q < NQ - 2:
                        gather(i, q + 2)
                    elif not final(i):
                        gather(i + 1, q + 2 - NQ)
                    if q or not first(i):
                        scatter(NQ * i + q - 1, (q - 1) % NQ)

            gather(0, 0)
            gather(0, 1)
            turns(pool, body)
            scatter(E - 1, NQ - 1)
            pool.wait_ge(y_out, 16 * E)

        @block.scalar
        def _(act):
            def rows(n, q):
                act.wait_ge(xt_done, n + 1)
                nc.scalar.activation(xbt[q % 2][:].rearrange("p k s -> p (k s)"), xtps[:, 0:KC * CAP],
                                     ACT.Copy).then_inc(xt_read, 1)

            def hidden(n, q):
                act.wait_ge(ht_done, n + 1)
                nc.scalar.activation(hidt[q % 2][:, 0:IC - 1, :].rearrange("p k s -> p (k s)"),
                                     htps[:, 0:(IC - 1) * CAP], ACT.Copy)
                nc.scalar.activation(hidt[q % 2][0:IT, IC - 1, :], htps[0:IT, (IC - 1) * CAP:IC * CAP],
                                     ACT.Copy).then_inc(ht_read, 1)

            def body(i):
                for q in range(NQ):
                    n = NQ * i + q
                    if q or not first(i):
                        hidden(n - 1, q - 1)
                    act.wait_ge(gu_done, n + 1)
                    nc.scalar.activation(sil[q % 2][:], gps[q % 2][0:CAP, 0:I], ACT.Silu).then_inc(sil_done, 1)
                    if q < NQ - 1 or not final(i):
                        rows(n + 1, q + 1)

            rows(0, 0)
            turns(act, body)
            hidden(E - 1, NQ - 1)

        @block.vector
        def _(dve):
            def weighted(n, q):
                dve.wait_ge(dn_done, n + 1)
                nc.vector.tensor_scalar(ysb[q][:], yps[q % 2][0:CAP, :], ids[q][:, 1:2].bitcast(F32), None,
                                        ALU.mult).then_inc(y_done, 1)

            def body(i):
                for q in range(NQ):
                    n = NQ * i + q
                    dve.wait_ge(sil_done, n + 1)
                    nc.vector.tensor_tensor(hid[q % 2][:], sil[q % 2][:], ups[q % 2][0:CAP, 0:I],
                                            ALU.mult).then_inc(hid_done, 1)
                    if q or not first(i):
                        weighted(n - 1, (q - 1) % NQ)

            turns(dve, body)
            weighted(E - 1, NQ - 1)

        @block.tensor
        def _(pe):
            M, TR = nc.tensor.matmul, nc.tensor.transpose

            def rows(i, q):
                pe.wait_ge(x_in[q], 16 * i + 16)
                for k in range(KC):
                    last = TR(xtps[:, k * CAP:(k + 1) * CAP], xb[q][:, k * P:(k + 1) * P], ident[0:CAP, 0:CAP])
                last.then_inc(xt_done, 1)

            def gate_up(i, q):
                pe.wait_ge(w_in[q], 48 * i + 48)
                pe.wait_ge(xt_read, NQ * i + q + 1)
                for a, bank in ((0, gps[q % 2]), (I, ups[q % 2])):
                    for k in range(KC):
                        last = M(bank[0:CAP, 0:I], xbt[q % 2][:, k, :], wgu[q][:, k, a:a + I],
                                 start=(k == 0), stop=(k == KC - 1))
                last.then_inc(gu_done, 1)

            def turn_hidden(n, q):
                pe.wait_ge(hid_done, n + 1)
                for k in range(IC):
                    w = P if k < IC - 1 else IT
                    last = TR(htps[0:w, k * CAP:(k + 1) * CAP], hid[q % 2][:, k * P:k * P + w], ident[0:CAP, 0:CAP])
                last.then_inc(ht_done, 1)

            def down(n, q):
                pe.wait_ge(ht_read, n + 1)
                for k in range(IC):
                    w = P if k < IC - 1 else IT
                    last = M(yps[q % 2][0:CAP, :], hidt[q % 2][0:w, k, :], wdn[q][0:w, k, :],
                             start=(k == 0), stop=(k == IC - 1))
                last.then_inc(dn_done, 1)

            def body(i):
                for q in range(NQ):
                    n = NQ * i + q
                    before = q or not first(i)
                    if before:
                        turn_hidden(n - 1, (q - 1) % NQ)
                    gate_up(i, q)
                    if q < NQ - 1:
                        rows(i, q + 1)
                    elif not final(i):
                        rows(i + 1, 0)
                    if before:
                        down(n - 1, (q - 1) % NQ)

            pe.wait_ge(id_in, 16)
            rows(0, 0)
            turns(pe, body)
            turn_hidden(E - 1, NQ - 1)
            down(E - 1, NQ - 1)


def stage_b(nc, t):
    ctx = ExitStack()
    with ctx:
        def sb(name, shape, dt=F32):
            return ctx.enter_context(nc.sbuf_tensor(name, shape, dt))

        def ps(name, shape):
            return ctx.enter_context(nc.psum_tensor(name, shape, F32))

        def sem(name):
            return ctx.enter_context(nc.semaphore(name))

        def two(name, shape, dt=F32):
            return [sb(f"{name}{p}", shape, dt) for p in range(2)]

        LAG = 2
        RP = 16
        R3 = 3 * HD
        qst = two("qst", [P, GROUP, S], F32R)
        kst = two("kst", [P, S], F32R)
        vst = two("vst", [P, NKT, HD])
        prb = sb("prb", [P, RP, 2, CH])
        psum2 = [two(f"psum2{g}", [P, 2, CH]) for g in range(2)]
        mx = sb("mx", [P, GROUP * NKT, JC])
        neg = sb("neg", [P, GROUP * NKT])
        negt = sb("negt", [GROUP * NKT, P], F32R)
        num = two("num", [P, CH])
        den = two("den", [P, CH])
        rden = two("rden", [P, CH])
        att = two("att", [P, CH])
        ident = sb("ident_b", [P, P])
        lowf = sb("lowf", [P, P])
        identb = sb("identb", [P, P], BF16)
        cmask = sb("cmask", [P, P], BF16)
        ones = sb("ones_b", [P, HD])
        R = 3
        sps = ps("sps", [P, R, CH])
        mps = ps("mps", [P, R, CH])
        ops = ps("ops", [P, CH])
        dps = ps("dps", [P, CH])

        cst_in = sem("cst_b")
        init_v = sem("init_b")
        qk_in = [[sem(f"qk_in{p}{c}") for c in range(JC)] for p in range(2)]
        v_in = [sem("v_in0"), sem("v_in1")]
        c_in = sem("c_in")
        att_out = sem("att_out")
        s_done = sem("s_done")
        exp_done = sem("exp_done")
        sel_done = sem("sel_done")
        pv_done = sem("pv_done")
        add_done = sem("add_done")
        ones_done = sem("ones_done")
        m_done = sem("m_done")
        mred_done = sem("mred_done")
        c_done = sem("c_done")
        num_done = sem("num_done")
        den_done = sem("den_done")
        rden_done = sem("rden_done")
        att_done = sem("att_done")
        pe_pass, sp_pass, pool_pass = (sem(f"{e}_pass_b") for e in ("pe", "sp", "pool"))

        steps = [(j, kt, kt - JC * j) for j in range(JC) for kt in range(JC * (j + 1))]
        NK = len(steps)
        NU = GROUP * NK
        steps = [(j, kt, r if r >= 0 else -1) for j, kt, r in steps]
        full = [n for n, (j, kt, r) in enumerate(steps) if r < 0 and kt % 2 == 0]
        NGR = len(full)
        diag = [n for n, (j, kt, r) in enumerate(steps) if r >= 0]
        lasts = [n for n, (j, kt, r) in enumerate(steps) if r == 3]

        pieces = []
        for qt in range(NKT):
            for h in range(GROUP):
                n = (qt + 1) * P
                for j in range((n + CH - 1) // CH):
                    k0, w = j * CH, min(CH, n - j * CH)
                    if w == P and j:
                        k0, w = k0 - P, 2 * P
                    d = n - P - k0
                    pieces.append((h, qt, j, k0, max(w, 2 * P), w, d if n - k0 == w else None))
        NM = len(pieces)
        MI = NM + 1
        M1 = 37

        work = [1.0 * (CH - max(r, 0) * P) + (1.1 if steps[k - LAG][2] < 0 else 1.6) *
                (CH - max(steps[k - LAG][2], 0) * P) + CH for k, (j, kt, r) in enumerate(steps)][:M1]
        for k in range(M1):
            if any(k - LAG - 1 - part in lasts for part in range(NT)) or LAG <= k < LAG + NT:
                work[k] -= 400
        cost = [64 + piece[5] for piece in pieces]

        def upto(k):
            share = sum(work[:k]) / sum(work) * sum(cost)
            return sum(1 for n in range(NM) if sum(cost[:n + 1]) <= share + 1)

        first = [upto(k) for k in range(M1)] + [NM] * (NK - M1 + 1)

        def quota(k):
            return range(first[k], first[k + 1])

        MFIN = M1

        block = ctx.enter_context(nc.Block())

        @block.sync
        def _(sp):
            def load_qk(i, p, c):
                b = i // 2
                g = 2 * (i % 2) + p
                cols = slice(c * CH, (c + 1) * CH)
                if isinstance(i, int):
                    qh, ql = t["q_hi"][b, g], t["q_lo"][b, g]
                    kh, kl = (t[n][b, 0, g * HD:(g + 1) * HD, :] for n in ("k_hi", "k_lo"))
                else:
                    qh, ql = (t[n][ds(b, 1), ds(g, 1)].rearrange("o u p s -> (o u p) s") for n in ("q_hi", "q_lo"))
                    kh, kl = (t[n][ds(b, 1), :, ds(g * HD, HD), :].rearrange("o u p s -> (o u p) s") for n in ("k_hi", "k_lo"))
                for r, src in enumerate((qh, qh, ql)):
                    sp.dma_start(qst[p][r * HD:(r + 1) * HD, :, cols].bitcast(F32),
                                 src[:, cols].rearrange("(h d) s -> d h s", d=HD)).then_inc(qk_in[p][c], 16)
                for r, src in enumerate((kh, kl, kh)):
                    sp.dma_start(kst[p][r * HD:(r + 1) * HD, cols].bitcast(F32), src[:, cols]).then_inc(qk_in[p][c], 16)

            def load_v(i, p):
                b = i // 2
                g = 2 * (i % 2) + p
                v = t["v"].rearrange("(b k p) (g d) -> b g p k d", p=P, k=NKT, d=HD)
                v = v[b, g] if isinstance(i, int) else v[ds(b, 1), ds(g, 1)].rearrange("o u p k d -> (o u p) k d")
                sp.dma_start(vst[p][:], v).then_inc(v_in[p], 16)

            def store(i, p, j):
                b = i // 2
                g = 2 * (i % 2) + p
                a = t["att"]
                a = a[b, g] if isinstance(i, int) else a[ds(b, 1), ds(g, 1)].rearrange("o u p s -> (o u p) s")
                bg = 2 * i + p
                sp.wait_ge(att_done, bg * JC + j + 3)
                sp.sem_inc(sp_pass, 1)
                sp.dma_start(a[:, j * CH:(j + 1) * CH], att[j % 2][:]).then_inc(att_out, 16)
                sp.wait_ge(att_out, 16 * (bg * JC + j + 2))
                sp.sem_inc(sp_pass, 1)

            sp.sem_inc(att_out, 16)
            sp.dma_start(ident[:], t["ident"]).then_inc(cst_in, 16)
            sp.dma_start(lowf[:], t["cmask"]).then_inc(cst_in, 16)
            for p in range(2):
                for c in range(JC):
                    load_qk(0, p, c)
                load_v(0, p)
            with sp.Fori(0, BG // 2 - 1) as i:
                for p in range(2):
                    for j in range(JC - 1):
                        store(i, p, j)
                    for c in range(JC):
                        sp.wait_ge(s_done, (2 * i + p) * NU + GROUP * (lasts[-2] + 1 + NT * (c + 1)))
                        sp.sem_inc(sp_pass, 1)
                        load_qk(i + 1, p, c)
                    sp.wait_ge(pv_done, (2 * i + p) * NK + NK + 8)
                    sp.sem_inc(sp_pass, 1)
                    load_v(i + 1, p)
                    store(i, p, JC - 1)
            for p in range(2):
                for j in range(JC):
                    store(BG // 2 - 1, p, j)

        @block.gpsimd
        def _(pool):
            def normalize(bg, j):
                pool.wait_ge(rden_done, NT * (bg * JC + j + 1))
                pool.sem_inc(pool_pass, 1)
                pool.wait_ge(att_out, 16 * (bg * JC + j))
                pool.sem_inc(pool_pass, 1)
                nc.gpsimd.tensor_tensor(att[j % 2][:], num[j % 2][:], rden[j % 2][:], ALU.mult).then_inc(att_done, 1)

            def group(bg, prev):
                for k in range(NK):
                    if k - LAG - NT - 1 in lasts:
                        normalize(bg, lasts.index(k - LAG - NT - 1))
                    if prev and k == LAG + NT:
                        normalize(bg - 1, JC - 1)
                    if steps[k][2] >= 0:
                        q0 = steps[k][2] * P
                        for pr in range(2):
                            pool.wait_ge(exp_done, bg * NU + GROUP * k + 2 * pr + 2 + R)
                            pool.sem_inc(pool_pass, 1)
                            blk = prb[:, (2 * k + pr) % RP, :, q0:q0 + P]
                            nc.gpsimd.affine_select(out=blk, in_=blk, compare_op=ALU.is_ge, fill=0.0, base=0,
                                                    pattern=[[0, 2], [1, P]], channel_multiplier=-1).then_inc(sel_done, 1)
                    for gi, f in enumerate(full):
                        G = bg * NGR + gi
                        if k in (f + 2, f + 3):
                            pr = k - f - 2
                            pool.wait_ge(exp_done, bg * NU + GROUP * (f + 1) + 2 * pr + 2 + R)
                            pool.sem_inc(pool_pass, 1)
                            pool.wait_ge(ones_done, 2 * G + pr + 1)
                            pool.sem_inc(pool_pass, 1)
                            nc.gpsimd.tensor_tensor(psum2[gi % 2][pr][:], prb[:, (2 * f + pr) % RP],
                                                    prb[:, (2 * (f + 1) + pr) % RP], ALU.add).then_inc(add_done, 1)

            pool.sem_inc(att_done, 2)
            group(0, False)
            with pool.Fori(0, BG // 2 - 1) as i:
                group(2 * i + 1, True)
                group(2 * i + 2, True)
            group(BG - 1, True)
            normalize(BG - 1, JC - 1)

        @block.scalar
        def _(act):
            act.sem_inc(exp_done, R)
            act.sem_inc(num_done, 1)
            act.sem_inc(den_done, 1)
            act.sem_inc(c_done, 1)
            act.sem_inc(c_in, 16)

            def maxima(bg, p):
                act.wait_ge(m_done, bg * MI + MI)
                act.wait_ge(c_in, 16 * bg + 16)
                nc.scalar.activation(negt[:], mps[0:GROUP * NKT, NM % R, 0:P], ACT.Copy).then_inc(c_done, 1)
                act.wait_ge(c_done, bg + 2)
                act.dma_start(qst[p][R3:R3 + 1, :, :].bitcast(F32), negt[:].bitcast(F32)).then_inc(c_in, 16)

            maxima(0, 0)

            def take_outputs(bg, j):
                act.wait_ge(pv_done, bg * NK + lasts[j] + 1 + 8)
                act.wait_ge(att_done, bg * JC + j + 1)
                nc.scalar.activation(num[j % 2][:], ops[:], ACT.Copy).then_inc(num_done, 1)

            def take_denominators(bg, j):
                nc.scalar.activation(den[j % 2][:], dps[:], ACT.Copy).then_inc(den_done, 1)

            def group(bg, p, nxt, prev=True):
                for k, (j, kt, r) in enumerate(steps):
                    q0 = max(r, 0) * P
                    if nxt and k == MFIN + 2:
                        maxima(bg + 1, 1 - p)
                    ended = []
                    if k - LAG - 1 in lasts:
                        ended = [(bg, lasts.index(k - LAG - 1))]
                    if prev and k == LAG:
                        ended = [(bg - 1, JC - 1)]
                    for chunk in ended:
                        take_outputs(*chunk)
                    act.wait_ge(pv_done, bg * NK + k + 1)
                    kk = k - RP // 2
                    gi = [n for n, f in enumerate(full) if f <= kk % NK < f + 2]
                    if gi and (kk >= 0 or prev):
                        act.wait_ge(add_done, 2 * (bg * NGR + gi[0] - (NGR if kk < 0 else 0)) + 2)
                    for h in range(GROUP):
                        act.wait_ge(s_done, bg * NU + GROUP * k + h + 1)
                        nc.scalar.activation(prb[:, (2 * k + h // 2) % RP, h % 2, q0:CH],
                                             sps[:, (GROUP * k + h) % R, q0:CH], ACT.Exp, scale=SCALE).then_inc(exp_done, 1)
                        for chunk in ended:
                            if h == 1:
                                take_denominators(*chunk)
                if not nxt:
                    take_outputs(bg, JC - 1)
                    take_denominators(bg, JC - 1)

            group(0, 0, True, prev=False)
            with act.Fori(0, BG // 2 - 1) as i:
                group(2 * i + 1, 1, True)
                group(2 * i + 2, 0, True)
            group(BG - 1, 1, False)

        @block.vector
        def _(dve):
            V = nc.vector
            V.memset(mx[:], -3.0e38).then_inc(init_v, 1)
            V.memset(ones[:], 1.0).then_inc(init_v, 1)
            for p in range(2):
                V.memset(kst[p][R3:R3 + 1, :].bitcast(F32), 1.0).then_inc(init_v, 1)
            dve.wait_ge(cst_in, 32)
            V.tensor_copy(identb[:], ident[:]).then_inc(init_v, 1)
            V.tensor_copy(cmask[:], lowf[:]).then_inc(init_v, 1)
            dve.wait_ge(init_v, 6)
            dve.sem_inc(mred_done, R)

            def reduce(bg, p, n):
                h, qt, j, k0, w, wr, d = pieces[n]
                dve.wait_ge(m_done, bg * MI + n + 1)
                V.tensor_reduce(mx[:, h * NKT + qt, j:j + 1], mps[:, n % R, 0:wr], AX.X,
                                ALU.max).then_inc(mred_done, 1)

            def negate(bg):
                dve.wait_ge(mred_done, bg * MI + NM + R)
                V.tensor_reduce(neg[:], mx[:], AX.X, ALU.max, negate=True).then_inc(mred_done, 1)

            for n in range(NM):
                reduce(0, 0, n)
            negate(0)

            def invert(bg, j, part):
                if part == 0:
                    dve.wait_ge(den_done, bg * JC + j + 2)
                cols = slice(part * P, (part + 1) * P)
                V.reciprocal(rden[j % 2][:, cols], den[j % 2][:, cols]).then_inc(rden_done, 1)

            def group(bg, p, nxt, prev=True):
                for k in range(NK):
                    if nxt:
                        for n in quota(k):
                            reduce(bg + 1, 1 - p, n)
                        if k == MFIN:
                            negate(bg + 1)
                    for part in range(NT):
                        if k - LAG - 1 - part in lasts:
                            invert(bg, lasts.index(k - LAG - 1 - part), part)
                        if prev and k == LAG + part:
                            invert(bg - 1, JC - 1, part)
                if not nxt:
                    for part in range(NT):
                        invert(bg, JC - 1, part)

            group(0, 0, True, prev=False)
            with dve.Fori(0, BG // 2 - 1) as i:
                group(2 * i + 1, 1, True)
                group(2 * i + 2, 0, True)
            group(BG - 1, 1, False)

        @block.tensor
        def _(pe):
            M, TR = nc.tensor.matmul, nc.tensor.transpose

            def piece(bg, p, n):
                h, qt, j, k0, w, wr, d = pieces[n]
                if h == 0 and j == 0 and qt % NT == 0:
                    c = qt // NT
                    pe.wait_ge(qk_in[p][c], 96 * (bg // 2) + 96)
                if n < R and n % R == NM % R:
                    pe.wait_ge(c_done, bg + 1)
                elif n < R:
                    before = max(m for m in range(NM) if m % R == n)
                    pe.wait_ge(mred_done, bg * MI + before + 1 - MI + R)
                else:
                    pe.wait_ge(mred_done, bg * MI + n + 1)
                out = mps[:, n % R, :]
                last = M(out[:, 0:w], qst[p][0:R3, h, qt * P:(qt + 1) * P], kst[p][0:R3, k0:k0 + w],
                         start=True, stop=True)
                if d is not None:
                    last = M(out[:, d:d + P], identb[:], cmask[:], start=False, stop=True, skip_group_check=True)
                last.then_inc(m_done, 1)

            def turn(bg, p):
                pe.wait_ge(mred_done, bg * MI + MI + R)
                pe.sem_inc(pe_pass, 1)
                TR(mps[0:GROUP * NKT, NM % R, 0:P], neg[:], ident[:]).then_inc(m_done, 1)

            pe.wait_ge(init_v, 6)
            pe.sem_inc(pv_done, 8)
            pe.sem_inc(ones_done, 4)
            for n in range(NM):
                piece(0, 0, n)
            turn(0, 0)

            def scores(bg, p, k, h):
                j, kt, r = steps[k]
                q0 = min(max(r, 0) * P, CH - 2 * P)
                u = GROUP * k + h
                before = u - R if u >= R else max(m for m in range(NU) if m % R == u % R) - NU
                pe.wait_ge(exp_done, bg * NU + before + 1 + R)
                M(sps[:, u % R, q0:CH], kst[p][0:R3 + 1, kt * P:(kt + 1) * P],
                  qst[p][0:R3 + 1, h, j * CH + q0:(j + 1) * CH], start=True, stop=True).then_inc(s_done, 1)

            def output(bg, p, k):
                j, kt, r = steps[k]
                q0 = max(r, 0) * P
                pe.wait_ge(exp_done, bg * NU + GROUP * (k + 1) + R)
                if r >= 0:
                    pe.wait_ge(sel_done, bg * 2 * len(diag) + 2 * diag.index(k) + 2)
                if kt == 0:
                    pe.wait_ge(num_done, bg * JC + j + 1)
                    if r >= 0:
                        pe.wait_ge(den_done, bg * JC + j + 1)
                for h in range(GROUP):
                    last = M(ops[HD * h:HD * (h + 1), q0:CH], vst[p][:, kt, :],
                             prb[:, (2 * k + h // 2) % RP, h % 2, q0:CH], start=(kt == 0), stop=(r == 3),
                             skip_group_check=True)
                if r >= 0:
                    for h in range(GROUP):
                        last = M(dps[HD * h:HD * (h + 1), q0:CH], ones[:],
                                 prb[:, (2 * k + h // 2) % RP, h % 2, q0:CH], start=(kt == 0),
                                 stop=(r == 3), skip_group_check=True)
                last.then_inc(pv_done, 1)

            def pair_sum(bg, gi):
                j, kt, _ = steps[full[gi]]
                if kt == 0:
                    pe.wait_ge(den_done, bg * JC + j + 1)
                for pr in range(2):
                    pe.wait_ge(add_done, 2 * (bg * NGR + gi) + pr + 1)
                    for hh in range(2):
                        h = 2 * pr + hh
                        last = M(dps[HD * h:HD * (h + 1), :], ones[:], psum2[gi % 2][pr][:, hh, :],
                                 start=(kt == 0), stop=False, skip_group_check=True)
                    last.then_inc(ones_done, 1)

            def group(bg, p, nxt, prev=True):
                for k in range(NK):
                    todo = list(quota(k)) if nxt else []
                    for h in range(GROUP):
                        scores(bg, p, k, h)
                        for n in todo[h:h + 1]:
                            piece(bg + 1, 1 - p, n)
                    for gi, f in enumerate(full):
                        if k == f + LAG + 3:
                            pair_sum(bg, gi)
                    if k >= LAG:
                        output(bg, p, k - LAG)
                    elif prev:
                        output(bg - 1, 1 - p, NK + k - LAG)
                    for n in todo[GROUP:]:
                        piece(bg + 1, 1 - p, n)
                    if nxt and k == MFIN:
                        turn(bg + 1, 1 - p)
                if not nxt:
                    for k in range(NK - LAG, NK):
                        output(bg, p, k)

            def ready(bg, p):
                pe.wait_ge(v_in[p], 16 * (bg // 2) + 16)
                pe.wait_ge(c_in, 16 * bg + 32)

            ready(0, 0)
            group(0, 0, True, prev=False)
            with pe.Fori(0, BG // 2 - 1) as i:
                for bg, p in ((2 * i + 1, 1), (2 * i + 2, 0)):
                    ready(bg, p)
                    group(bg, p, True)
            ready(BG - 1, 1)
            group(BG - 1, 1, False)


def stage_c(nc, t):
    ctx = ExitStack()
    with ctx:
        def sb(name, shape, dt=F32):
            return ctx.enter_context(nc.sbuf_tensor(name, shape, dt))

        def sem(name):
            return ctx.enter_context(nc.semaphore(name))

        def two(name, shape, dt=F32):
            return [sb(f"{name}{p}", shape, dt) for p in range(2)]

        wo = sb("wo", [P, KC, D])
        wo_hi = sb("wo_hi", [P, KC, D], F32R)
        wo_lo = sb("wo_lo", [P, KC, D], F32R)
        a_in = two("a_in", [P, KC, CH])
        a_hi = two("a_hi", [P, KC, CH], F32R)
        a_lo = two("a_lo", [P, KC, CH], F32R)
        NQ = 4
        y = [sb(f"y_c{q}", [P, NT, D]) for q in range(NQ)]
        ops = ctx.enter_context(nc.psum_tensor("cps", [P, 8, D], F32))
        w_in = sem("wo_in")
        w_hi = sem("wo_hi_done")
        w_lo = sem("wo_lo_done")
        a_ld = [sem("a_ld0"), sem("a_ld1")]
        y_ld = [sem(f"y_ld{q}") for q in range(NQ)]
        hi_done = sem("a_hi_done")
        lo_done = sem("a_lo_done")
        o_done = sem("o_done")
        y_done = sem("yc_done")
        y_st = [sem(f"y_st{q}") for q in range(NQ)]
        sp_pass = sem("sp_pass_c")
        block = ctx.enter_context(nc.Block())

        def rows(ap, c):
            v = ap.rearrange("(c t p) d -> c p t d", p=P, t=NT)
            return v[c] if isinstance(c, int) else v[ds(c, 1)].rearrange("o p t d -> (o p) t d")

        def load_att(sp, c, p):
            a = t["att"]
            if isinstance(c, int):
                a = a[c // JC, :, :, (c % JC) * CH:(c % JC + 1) * CH].rearrange("g p s -> p g s")
            else:
                a = a[ds(c // JC, 1), :, :, ds((c % JC) * CH, CH)].rearrange("o g p s -> (o p) g s")
            sp.dma_start(a_in[p][:], a).then_inc(a_ld[p], 16)

        def load_base(sp, c, q):
            sp.dma_start(y[q][:], rows(t["base"][0:T, :], c)).then_inc(y_ld[q], 16)

        @block.sync
        def _(sp):
            def body(i, nxt):
                for q in range(NQ):
                    c = NQ * i + q
                    if nxt or q < NQ - 2:
                        sp.wait_ge(lo_done, c + 1)
                        sp.sem_inc(sp_pass, 1)
                        load_att(sp, c + 2, q % 2)
                    if nxt or q < NQ - 3:
                        sp.wait_ge(y_st[(q + 3) % NQ], 16 * i + 16)
                        sp.sem_inc(sp_pass, 1)
                        load_base(sp, c + 3, (q + 3) % NQ)

            sp.sem_inc(y_st[NQ - 1], 16)
            load_att(sp, 0, 0)
            sp.dma_start(wo[:], t["w_o"].rearrange("(k p) n -> p k n", p=P)).then_inc(w_in, 16)
            load_att(sp, 1, 1)
            for q in range(NQ - 1):
                load_base(sp, q, q)
            with sp.Fori(0, NC // NQ - 1) as i:
                body(i, True)
            body(NC // NQ - 1, False)

        @block.scalar
        def _(act):
            def high(i, q):
                p = q % 2
                act.wait_ge(a_ld[p], 32 * i + 16 * (q // 2) + 16)
                act.wait_ge(o_done, NT * (NQ * i + q + 1))
                nc.scalar.activation(a_hi[p][:], a_in[p][:], ACT.Copy).then_inc(hi_done, 1)

            def store(c, q):
                act.wait_ge(y_done, NT * (c + 1))
                act.dma_start(rows(t["out"], c), y[q][:]).then_inc(y_st[q], 16)

            def body(i, after=True):
                for q in range(NQ):
                    high(i, q)
                    if q or after:
                        store(NQ * i + q - 1, (q - 1) % NQ)

            act.wait_ge(w_in, 16)
            nc.scalar.activation(wo_hi[:], wo[:], ACT.Copy).then_inc(w_hi, 1)
            body(0, False)
            with act.Fori(0, NC // NQ - 1) as i:
                body(i + 1)
            store(NC - 1, NQ - 1)
            for q in range(NQ):
                act.wait_ge(y_st[q], 16 * (NC // NQ) + (16 if q == NQ - 1 else 0))

        @block.vector
        def _(dve):
            V = nc.vector
            dve.wait_ge(w_hi, 1)
            V.tensor_tensor(wo_lo[:], wo[:], wo_hi[:].bitcast(F32), ALU.subtract).then_inc(w_lo, 1)

            def low(c, p):
                dve.wait_ge(hi_done, c + 1)
                V.tensor_tensor(a_lo[p][:], a_in[p][:], a_hi[p][:].bitcast(F32), ALU.subtract).then_inc(lo_done, 1)

            def body(i, nxt):
                for q in range(NQ):
                    c = NQ * i + q
                    if q < NQ - 1 or nxt:
                        low(c + 1, (q + 1) % 2)
                    dve.wait_ge(y_ld[q], 16 * i + 16)
                    for n in range(NT):
                        dve.wait_ge(o_done, NT * (c + 2) + n + 1)
                        V.tensor_tensor(y[q][:, n, :], ops[:, NT * (q % 2) + n, :], y[q][:, n, :],
                                        ALU.add).then_inc(y_done, 1)

            low(0, 0)
            with dve.Fori(0, NC // NQ - 1) as i:
                body(i, True)
            body(NC // NQ - 1, False)

        @block.tensor
        def _(pe):
            pe.sem_inc(o_done, 2 * NT)
            pe.wait_ge(w_lo, 1)
            with pe.Fori(0, NC // 2) as i:
                for p in range(2):
                    c = 2 * i + p
                    pe.wait_ge(lo_done, c + 1)
                    for n in range(NT):
                        m = 0
                        for k in range(KC):
                            for a, w in ((a_hi, wo_hi), (a_lo, wo_hi), (a_hi, wo_lo)):
                                last = nc.tensor.matmul(ops[:, NT * p + n, :], a[p][:, k, n * P:(n + 1) * P],
                                                        w[:, k, :], start=(m == 0), stop=(m == 3 * KC - 1))
                                m += 1
                        last.then_inc(o_done, 1)


def host_constants(np):
    tri = np.tril(np.ones((NG, NG), np.float32), -1).reshape(-1)
    row = np.concatenate([np.arange(E), np.arange(E) * CAP, tri]).astype(np.float32)
    cst = np.concatenate([np.tile(row, (P, 1)), (np.arange(P)[:, None] + P * np.arange(NT)[None, :])], 1)
    cmask = np.triu(np.full((P, P), NEG, np.float32), 1)
    upper = np.triu(np.ones((P, P)), 1)
    return {"ident": np.eye(P, dtype=np.float32), "upper": upper.astype(np.float32), "cmask": cmask,
            "cst": np.ascontiguousarray(cst, dtype=np.float32)}


def host_layout(np, a):
    gu = a["L0_ffn_ws_gate_up"]
    cols = []
    for m in range(FM):
        w = min(P, ISH - m * P)
        cols += [gu[:, m * P:m * P + w], gu[:, ISH + m * P:ISH + m * P + w]]
    w_a = np.concatenate([a["L0_attn_Wq"], a["L0_attn_Wk"], a["L0_attn_Wv"], a["L0_ffn_gate_w"].T] + cols, 1)
    w_d = np.concatenate([a["L0_ffn_ws_down"], np.zeros((FM * P - ISH, D), np.float32)], 0)
    return {"x": np.ascontiguousarray(a["L0_attn_x"]).reshape(T, D), "w_a": np.ascontiguousarray(w_a),
            "w_d": np.ascontiguousarray(w_d), "w_o": np.ascontiguousarray(a["L0_attn_Wo"]),
            "e_gu": np.ascontiguousarray(a["L0_ffn_w_gate_up"]), "e_d": np.ascontiguousarray(a["L0_ffn_w_down"])}


def scratch(nc, out, dbg=()):
    def dram(name, shape, dt):
        return nc.dram_tensor(name, shape, dt, **({"kind": "ExternalOutput"} if name in dbg else {})).ap()
    return {"base": dram("base", [T + CAP, D], F32), "xn": dram("xn_s", [T + CAP, D], F32), "v": dram("v_s", [T, P], F32),
            "q_hi": dram("q_hi_s", [B, NKV, P, S], F32), "q_lo": dram("q_lo_s", [B, NKV, P, S], F32),
            "k_hi": dram("k_hi_s", [B, 1, P, S], F32), "k_lo": dram("k_lo_s", [B, 1, P, S], F32),
            "tab": dram("tab_s", [E * CAP, 2], U32), "att": dram("att_s", [B, NKV, P, S], F32)}


def kernel(**inputs):
    import numpy as _np
    import concourse.bacc as _bacc
    from concourse.bass_utils import run_bass_kernel_spmd as _run

    nc = _bacc.Bacc("TRN2", target_bir_lowering=False, num_devices=1)
    arrays, t = {}, {}
    for name, a in {**host_layout(_np, inputs), **host_constants(_np)}.items():
        arrays[f"in_{name}"] = a
        t[name] = nc.dram_tensor(f"in_{name}", a.shape, mybir.dt.from_np(a.dtype), kind="ExternalInput").ap()
    t["out"] = nc.dram_tensor("out", [T, D], F32, kind="ExternalOutput").ap()
    t.update(scratch(nc, None))
    stage_a(nc, t)
    stage_m(nc, t)
    stage_b(nc, t)
    stage_c(nc, t)
    r = _run(nc, [arrays], core_ids=[0])
    return r.results[0]["out"].reshape(B, S, D)
```
